# Optimizing a Trainium2 kernel written in Bass

```python
import numpy as np
import jax
import jax.numpy as jnp

def _softmax(x, axis=-1):
    return jax.nn.softmax(x, axis=axis)

def _gelu(x):
    return jax.nn.gelu(x, approximate=True)

def _silu(x):
    return jax.nn.silu(x)

def _sigmoid(x):
    return jax.nn.sigmoid(x)

def _layernorm(x, axis=-1, eps=1e-05):
    m = jnp.mean(x, axis=axis, keepdims=True)
    v = jnp.var(x, axis=axis, keepdims=True)
    return (x - m) / jnp.sqrt(v + eps)

def _scatter_add(tgt, idx, src, axis=0):
    return tgt.at[idx].add(src)

def _segment_sum(src, seg, n):
    return jax.ops.segment_sum(src, seg, n)
kernel_name = 'mk_gnn_ffn_d1_gnn_r8_0ffe34'

def setup_inputs(seed: int=0):
    np.random.seed(seed)
    _w = jnp.asarray

    def _rec_inputs():
        import jax
        import jax.numpy as jnp
        _gk = jax.random.key(seed)
        x = -0.0003713 + 1 * jax.random.normal(jax.random.fold_in(_gk, 1), (6250, 256), jnp.float32)
        src = jax.random.randint(jax.random.fold_in(_gk, 2), (100000,), 0, 6250, jnp.int32)
        dst = jnp.minimum((6250 * jax.random.uniform(jax.random.fold_in(_gk, 3), (100000,)) ** 2.0).astype(jnp.int32), 49999)
        _o = jnp.argsort(dst, stable=True)
        src = src[_o]
        dst = dst[_o]
        return (x, src, dst)
    x, src, dst = _rec_inputs()

    def _L0_gnn_setup():
        import jax, jax.numpy as jnp
        import numpy as np
        N = 6250
        E = 100000
        IN = 256
        H = 8
        C = 32
        NEG_SLOPE = 0.2
        LN_EPS = 1e-05

        def _gat_block(x, edge_index, W, att_src, att_dst, bias, ln_scale, ln_bias):
            src, dst = (edge_index[0], edge_index[1])
            h = (x @ W).reshape(N, H, C)
            a_src = jnp.einsum('nhc,hc->nh', h, att_src)
            a_dst = jnp.einsum('nhc,hc->nh', h, att_dst)
            alpha = jax.nn.leaky_relu(a_src[src] + a_dst[dst], NEG_SLOPE)
            amax = jax.ops.segment_max(alpha, dst, num_segments=N)
            amax = jnp.where(jnp.isfinite(amax), amax, 0.0)
            ex = jnp.exp(alpha - amax[dst])
            denom = jax.ops.segment_sum(ex, dst, num_segments=N)
            attn = ex / (denom[dst] + 1e-16)
            msg = h[src] * attn[:, :, None]
            out = jax.ops.segment_sum(msg, dst, num_segments=N)
            out = out.reshape(N, H * C) + bias
            out = out + x
            out = jax.nn.elu(out)
            mu = jnp.mean(out, axis=-1, keepdims=True)
            var = jnp.var(out, axis=-1, keepdims=True)
            return (out - mu) * jax.lax.rsqrt(var + LN_EPS) * ln_scale + ln_bias
        key = jax.random.key(seed)
        ks = jax.random.split(key, 8)
        x = jax.random.normal(ks[0], (N, IN), dtype=jnp.float32)
        edge_index = jax.random.randint(ks[1], (2, E), 0, N, dtype=jnp.int64)
        W = jax.random.normal(ks[2], (IN, H * C), dtype=jnp.float32) / np.sqrt(IN)
        att_src = jax.random.normal(ks[3], (H, C), dtype=jnp.float32) / np.sqrt(C)
        att_dst = jax.random.normal(ks[4], (H, C), dtype=jnp.float32) / np.sqrt(C)
        bias = jnp.zeros((H * C,), dtype=jnp.float32)
        ln_scale = jnp.ones((H * C,), dtype=jnp.float32)
        ln_bias = jnp.zeros((H * C,), dtype=jnp.float32)
        return {'x': x, 'edge_index': edge_index, 'W': W, 'att_src': att_src, 'att_dst': att_dst, 'bias': bias, 'ln_scale': ln_scale, 'ln_bias': ln_bias}
    _L0_gnn_all = _L0_gnn_setup()
    _L0_gnn_in = {k: v for k, v in _L0_gnn_all.items() if k in ('W', 'att_src', 'att_dst', 'bias', 'ln_scale', 'ln_bias')}
    del _L0_gnn_all

    def _L0_ffn_setup():
        import jax, jax.numpy as jnp
        import numpy as np
        B, N, D = (16, 512, 256)
        NUM_EXPERTS, TOP_K, HEADS = (4, 2, 4)
        N_EDGES = 131072
        LN_EPS = 1e-05

        def _layernorm(x, g, b):
            mu = x.mean(-1, keepdims=True)
            var = ((x - mu) ** 2).mean(-1, keepdims=True)
            return (x - mu) * jax.lax.rsqrt(var + LN_EPS) * g + b

        def _forward(x, edge_index, W_gat, att_src, att_dst, b_gat, ln_gamma, ln_beta, W1, b1, W2, b2):
            Bc, Nc, Dc = x.shape
            M = Bc * Nc
            x_flat = x.reshape(M, Dc)
            h = (x_flat @ W_gat).reshape(M, HEADS, NUM_EXPERTS)
            loops = jnp.arange(M, dtype=edge_index.dtype)
            src = jnp.concatenate([edge_index[0], loops])
            dst = jnp.concatenate([edge_index[1], loops])
            a_src = (h * att_src).sum(-1)
            a_dst = (h * att_dst).sum(-1)
            e = jax.nn.leaky_relu(a_src[src] + a_dst[dst], negative_slope=0.2)
            e_max = jax.ops.segment_max(e, dst, num_segments=M)
            ee = jnp.exp(e - e_max[dst])
            denom = jax.ops.segment_sum(ee, dst, num_segments=M)
            alpha = ee / (denom[dst] + 1e-16)
            msg = h[src] * alpha[:, :, None]
            agg = jax.ops.segment_sum(msg, dst, num_segments=M).reshape(M, HEADS * NUM_EXPERTS) + b_gat
            scores = _layernorm(agg, ln_gamma, ln_beta).reshape(M, HEADS, NUM_EXPERTS).mean(1)
            scores = scores.reshape(Bc, Nc, NUM_EXPERTS)
            topk_s, topk_i = jax.lax.top_k(scores, TOP_K)
            w = jax.nn.softmax(topk_s, axis=-1)
            out = jnp.zeros_like(x)
            for ei in range(NUM_EXPERTS):
                g = jnp.where(topk_i == ei, w, 0.0).sum(-1)
                hh = jax.nn.gelu(x @ W1[ei] + b1[ei], approximate=False)
                out = out + g[..., None] * (hh @ W2[ei] + b2[ei])
            return out
        key = jax.random.key(seed)
        ks = jax.random.split(key, 8)
        s = 0.05
        return {'x': jax.random.normal(ks[0], (B, N, D), jnp.float32), 'W_gat': jax.random.normal(ks[1], (D, HEADS * NUM_EXPERTS), jnp.float32) * s, 'att_src': jax.random.normal(ks[2], (HEADS, NUM_EXPERTS), jnp.float32) * s, 'att_dst': jax.random.normal(ks[3], (HEADS, NUM_EXPERTS), jnp.float32) * s, 'b_gat': jnp.zeros((HEADS * NUM_EXPERTS,), jnp.float32), 'ln_gamma': jnp.ones((HEADS * NUM_EXPERTS,), jnp.float32), 'ln_beta': jnp.zeros((HEADS * NUM_EXPERTS,), jnp.float32), 'W1': jax.random.normal(ks[4], (NUM_EXPERTS, D, 2 * D), jnp.float32) * s, 'b1': jnp.zeros((NUM_EXPERTS, 2 * D), jnp.float32), 'W2': jax.random.normal(ks[5], (NUM_EXPERTS, 2 * D, D), jnp.float32) * s, 'b2': jnp.zeros((NUM_EXPERTS, D), jnp.float32), 'edge_index': jax.random.randint(ks[6], (2, N_EDGES), 0, B * N, jnp.int32)}
    _L0_ffn_all = _L0_ffn_setup()
    _L0_ffn_in = {k: v for k, v in _L0_ffn_all.items() if k in ('W_gat', 'att_src', 'att_dst', 'b_gat', 'ln_gamma', 'ln_beta', 'W1', 'b1', 'W2', 'b2', 'edge_index')}
    del _L0_ffn_all
    return {'x': x, 'src': src, 'dst': dst, 'L0_gnn_W': _L0_gnn_in['W'], 'L0_gnn_att_src': _L0_gnn_in['att_src'], 'L0_gnn_att_dst': _L0_gnn_in['att_dst'], 'L0_gnn_bias': _L0_gnn_in['bias'], 'L0_gnn_ln_scale': _L0_gnn_in['ln_scale'], 'L0_gnn_ln_bias': _L0_gnn_in['ln_bias'], 'L0_ffn_W_gat': _L0_ffn_in['W_gat'], 'L0_ffn_att_src': _L0_ffn_in['att_src'], 'L0_ffn_att_dst': _L0_ffn_in['att_dst'], 'L0_ffn_b_gat': _L0_ffn_in['b_gat'], 'L0_ffn_ln_gamma': _L0_ffn_in['ln_gamma'], 'L0_ffn_ln_beta': _L0_ffn_in['ln_beta'], 'L0_ffn_W1': _L0_ffn_in['W1'], 'L0_ffn_b1': _L0_ffn_in['b1'], 'L0_ffn_W2': _L0_ffn_in['W2'], 'L0_ffn_b2': _L0_ffn_in['b2'], 'L0_ffn_edge_index': _L0_ffn_in['edge_index']}

def reference(x, src, dst, L0_gnn_W, L0_gnn_att_src, L0_gnn_att_dst, L0_gnn_bias, L0_gnn_ln_scale, L0_gnn_ln_bias, L0_ffn_W_gat, L0_ffn_att_src, L0_ffn_att_dst, L0_ffn_b_gat, L0_ffn_ln_gamma, L0_ffn_ln_beta, L0_ffn_W1, L0_ffn_b1, L0_ffn_W2, L0_ffn_b2, L0_ffn_edge_index):
    import jax
    import jax.numpy as jnp

    def _L0_gnn_ref(x, edge_index, W, att_src, att_dst, bias, ln_scale, ln_bias):
        import jax, jax.numpy as jnp
        import numpy as np
        N = 6250
        E = 100000
        IN = 256
        H = 8
        C = 32
        NEG_SLOPE = 0.2
        LN_EPS = 1e-05

        def _gat_block(x, edge_index, W, att_src, att_dst, bias, ln_scale, ln_bias):
            src, dst = (edge_index[0], edge_index[1])
            h = (x @ W).reshape(N, H, C)
            a_src = jnp.einsum('nhc,hc->nh', h, att_src)
            a_dst = jnp.einsum('nhc,hc->nh', h, att_dst)
            alpha = jax.nn.leaky_relu(a_src[src] + a_dst[dst], NEG_SLOPE)
            amax = jax.ops.segment_max(alpha, dst, num_segments=N)
            amax = jnp.where(jnp.isfinite(amax), amax, 0.0)
            ex = jnp.exp(alpha - amax[dst])
            denom = jax.ops.segment_sum(ex, dst, num_segments=N)
            attn = ex / (denom[dst] + 1e-16)
            msg = h[src] * attn[:, :, None]
            out = jax.ops.segment_sum(msg, dst, num_segments=N)
            out = out.reshape(N, H * C) + bias
            out = out + x
            out = jax.nn.elu(out)
            mu = jnp.mean(out, axis=-1, keepdims=True)
            var = jnp.var(out, axis=-1, keepdims=True)
            return (out - mu) * jax.lax.rsqrt(var + LN_EPS) * ln_scale + ln_bias
        return _gat_block(x, edge_index, W, att_src, att_dst, bias, ln_scale, ln_bias)

    def _L0_ffn_ref(x, W_gat, att_src, att_dst, b_gat, ln_gamma, ln_beta, W1, b1, W2, b2, edge_index):
        import jax, jax.numpy as jnp
        import numpy as np
        B, N, D = (16, 512, 256)
        NUM_EXPERTS, TOP_K, HEADS = (4, 2, 4)
        N_EDGES = 131072
        LN_EPS = 1e-05

        def _layernorm(x, g, b):
            mu = x.mean(-1, keepdims=True)
            var = ((x - mu) ** 2).mean(-1, keepdims=True)
            return (x - mu) * jax.lax.rsqrt(var + LN_EPS) * g + b

        def _forward(x, edge_index, W_gat, att_src, att_dst, b_gat, ln_gamma, ln_beta, W1, b1, W2, b2):
            Bc, Nc, Dc = x.shape
            M = Bc * Nc
            x_flat = x.reshape(M, Dc)
            h = (x_flat @ W_gat).reshape(M, HEADS, NUM_EXPERTS)
            loops = jnp.arange(M, dtype=edge_index.dtype)
            src = jnp.concatenate([edge_index[0], loops])
            dst = jnp.concatenate([edge_index[1], loops])
            a_src = (h * att_src).sum(-1)
            a_dst = (h * att_dst).sum(-1)
            e = jax.nn.leaky_relu(a_src[src] + a_dst[dst], negative_slope=0.2)
            e_max = jax.ops.segment_max(e, dst, num_segments=M)
            ee = jnp.exp(e - e_max[dst])
            denom = jax.ops.segment_sum(ee, dst, num_segments=M)
            alpha = ee / (denom[dst] + 1e-16)
            msg = h[src] * alpha[:, :, None]
            agg = jax.ops.segment_sum(msg, dst, num_segments=M).reshape(M, HEADS * NUM_EXPERTS) + b_gat
            scores = _layernorm(agg, ln_gamma, ln_beta).reshape(M, HEADS, NUM_EXPERTS).mean(1)
            scores = scores.reshape(Bc, Nc, NUM_EXPERTS)
            topk_s, topk_i = jax.lax.top_k(scores, TOP_K)
            w = jax.nn.softmax(topk_s, axis=-1)
            out = jnp.zeros_like(x)
            for ei in range(NUM_EXPERTS):
                g = jnp.where(topk_i == ei, w, 0.0).sum(-1)
                hh = jax.nn.gelu(x @ W1[ei] + b1[ei], approximate=False)
                out = out + g[..., None] * (hh @ W2[ei] + b2[ei])
            return out
        return _forward(x, edge_index, W_gat, att_src, att_dst, b_gat, ln_gamma, ln_beta, W1, b1, W2, b2)
    edge_index = jnp.stack([src, dst])
    x = x + _L0_gnn_ref(_layernorm(x, axis=-1), edge_index, L0_gnn_W, L0_gnn_att_src, L0_gnn_att_dst, L0_gnn_bias, L0_gnn_ln_scale, L0_gnn_ln_bias)
    x = x + _L0_ffn_ref(_layernorm(x, axis=-1)[None], L0_ffn_W_gat, L0_ffn_att_src, L0_ffn_att_dst, L0_ffn_b_gat, L0_ffn_ln_gamma, L0_ffn_ln_beta, L0_ffn_W1, L0_ffn_b1, L0_ffn_W2, L0_ffn_b2, L0_ffn_edge_index)[0]
    return x

_drawn_inputs = setup_inputs


def setup_inputs(seed=0):
    import zlib

    import numpy as np

    out = dict(_drawn_inputs(seed))
    spreads = {'L0_gnn_bias': (0.0, 0.1),
     'L0_gnn_ln_scale': (1.0, 0.2),
     'L0_gnn_ln_bias': (0.0, 0.1),
     'L0_ffn_b_gat': (0.0, 0.1),
     'L0_ffn_ln_gamma': (1.0, 0.2),
     'L0_ffn_ln_beta': (0.0, 0.1),
     'L0_ffn_b1': (0.0, 0.296),
     'L0_ffn_b2': (0.0, 0.1)}
    factors = {'L0_ffn_att_dst': 3.076}
    for name, (base, spread) in spreads.items():
        noise = np.random.default_rng([zlib.crc32(name.encode()), seed]).standard_normal(out[name].shape)
        drawn = base * np.exp(spread * noise) if base else spread * noise
        out[name] = jnp.asarray(drawn.astype(out[name].dtype))
    for name, factor in factors.items():
        out[name] = (out[name] * factor).astype(out[name].dtype)
    return out
```

```python
import concourse.bass as bass
from concourse import mybir
from contextlib import ExitStack

N = 6250
T = 49
NP = T * 128
D = 256
SENT = N
SENT_DL = 255
CH = 4


class Queue:

    def __init__(self, name, sem):
        self.name, self.sem, self.count, self.items, self.seen = name, sem, 0, [], {}

    def wait(self, *tokens):
        for tok in tokens:
            if tok is None:
                continue
            sem, value = tok
            if self.seen.get(id(sem), 0) >= value:
                continue
            self.seen[id(sem)] = value
            self.items.append(lambda eng, sem=sem, value=value: eng.wait_ge(sem, value))

    def do(self, fn, *waits):
        self.wait(*waits)
        self.count += 1
        self.items.append(lambda eng, fn=fn: fn(eng).then_inc(self.sem, 1))
        return (self.sem, self.count)

    def raw(self, fn, *waits):
        self.wait(*waits)
        self.items.append(lambda eng, fn=fn: fn(eng))

    def dma(self, fn, line, *waits):
        self.wait(*waits)
        line.count += 16
        self.items.append(lambda eng, fn=fn, sem=line.sem: fn(eng).then_inc(sem, 16))
        return (line.sem, line.count)

    def emit(self, eng):
        for item in self.items:
            item(eng)


class Line:
    def __init__(self, sem):
        self.sem, self.count = sem, 0

    def now(self):
        return (self.sem, self.count)


def build(nc, x_d, src_d, dst_d, W_d, as_d, ad_d, bias_d, lns_d, lnb_d, Wg_d, gas_d, gad_d, bg_d, gam_d, bet_d,
          W1_d, b1_d, W2_d, b2_d, ei_d, out_d):
    f32, i32, u32 = mybir.dt.float32, mybir.dt.int32, mybir.dt.uint32
    ALU = mybir.AluOpType
    ACT = mybir.ActivationFunctionType
    X = mybir.AxisListType.X

    ctx = ExitStack()
    with ctx:
        def sb(name, shape, dt=f32):
            return ctx.enter_context(nc.sbuf_tensor(name, shape, dt))

        def pb(name, shape, dt=f32):
            return ctx.enter_context(nc.psum_tensor(name, shape, dt))

        def sem(name):
            return ctx.enter_context(nc.semaphore(name))

        def line(name):
            return Line(sem(name))

        V, A, P, G, S = (Queue(n, sem("q_" + n)) for n in ("dve", "act", "pe", "pool", "sp"))
        v, a, g, pe = nc.vector, nc.scalar, nc.gpsimd, nc.tensor

        class Graph:
            pass

        g1, g2 = Graph(), Graph()
        g1.n, g1.E, g1.J, g1.H, g1.C = 1, 100000, 782, 8, 32
        g2.n, g2.E, g2.J, g2.H, g2.C = 2, 131072, 1024, 4, 4
        for q in (g1, g2):
            q.F = q.H * q.C
            q.R = q.F + q.H
            q.NCH = -(-(-(-q.E // 128) + T) // CH) * CH
            q.K = -(-q.NCH // 128)
            q.table = nc.dram_tensor(f"table{q.n}", (NP, q.R), f32).ap()
            q.slots_d = nc.dram_tensor(f"slots{q.n}", (128 * q.NCH, 1), i32).ap()
            q.tm_d = nc.dram_tensor(f"tm{q.n}", (2 * q.K * 128,), i32).ap()
            q.idx = sb(f"idx{q.n}", [128, q.NCH], u32)
            q.dl = sb(f"dl{q.n}", [128, q.NCH])
            q.tab = sb(f"tab{q.n}", [128, (T + 1) * 2 * q.H])
            q.tm = sb(f"tmr{q.n}", [1, 2 * q.K * 128], i32)

        big = sb("big", [128, (T + 1) * g1.R])
        x_sb = sb("x_sb", [128, T, D])
        acc1 = big[:, :].rearrange("p (t r) -> p t r", r=g1.R)
        acc2f = sb("acc2", [128, (T + 1) * g2.R])
        acc2 = acc2f[:, :].rearrange("p (t r) -> p t r", r=g2.R)
        xT = acc1

        def tmp(i, dt, n=1024):
            ap = big[:, i * 1024:i * 1024 + n]
            return ap.bitcast(dt) if dt != f32 else ap

        iota = sb("iota", [128, 128])
        ident = sb("ident", [128, 128])
        tri = sb("tri", [128, 128])
        ones = sb("ones", [128, 128])
        pidx = sb("pidx", [128, 9])
        rmask = sb("rmask", [128, 1])
        epsc = sb("epsc", [128, 1])

        l_x, l_e, l_w, l_ld = (line(n) for n in ("l_x", "l_e", "l_w", "l_ld"))
        NSL = 4
        l_g = [line(f"l_g{i}") for i in range(NSL)]
        l_h = [line(f"l_h{i}") for i in range(2)]
        l_o = line("l_o")

        esrc = {1: src_d, 2: ei_d[0, :]}
        edst = {1: dst_d, 2: ei_d[1, :]}

        def load_edges(q, waits):
            J, full = q.J, q.E // q.J
            left = q.E - full * J
            for t_i, ap in ((0, esrc[q.n]), (1, edst[q.n])):
                buf = tmp(t_i, i32)
                S.dma(lambda e, buf=buf, ap=ap: e.dma_start(buf[0:full, 0:J], ap[0:full * J].rearrange("(p j) -> p j", j=J)),
                      l_e, *waits)
                if left:
                    S.dma(lambda e, buf=buf, ap=ap: e.dma_start(buf[full:full + 1, 0:left],
                                                                ap[full * J:q.E].rearrange("(p j) -> p j", p=1)), l_e)
            return l_e.now()

        t_m0 = V.do(lambda e: v.memset(tmp(0, i32), 0))
        t_m1 = V.do(lambda e: v.memset(tmp(1, i32), 128 * 63))
        edges1 = load_edges(g1, [t_m0, t_m1])
        t_x0 = V.do(lambda e: v.memset(x_sb[:, T - 1, :], 0.0))
        xv = x_d[0:48 * 128, :].rearrange("(t p) d -> p t d", p=128)
        for k in range(4):
            S.dma(lambda e, k=k: e.dma_start(x_sb[:, 12 * k:12 * k + 12, :], xv[:, 12 * k:12 * k + 12, :]), l_x)
        x_in = S.dma(lambda e: e.dma_start(x_sb[0:N - 48 * 128, 48, :], x_d[48 * 128:N, :]), l_x, t_x0)

        Wx1 = sb("Wx1", [128, 2, D + 16])
        Wx2 = sb("Wx2", [128, 2, 24])
        biasB, lnsB, lnbB = sb("biasB", [128, D]), sb("lnsB", [128, D]), sb("lnbB", [128, D])
        attB = sb("attB", [128, 2, D])
        gatB = sb("gatB", [128, 2, 16])
        gB = sb("gB", [128, 3, 16])
        b2B = sb("b2B", [128, 4, D])
        b1c = sb("b1c", [128, 4, 4])
        Wt = sb("Wt", [128, 2, D])

        def load(dst, srcap, *waits):
            return S.dma(lambda e: e.dma_start(dst, srcap, allow_slow_non_contiguous=True), l_w, *waits)

        load(Wt[:, :, :], W_d.rearrange("(k p) n -> p k n", p=128))
        load(Wx1[:, :, 0:D], W_d.rearrange("(k p) n -> p k n", p=128))
        load(Wx2[:, :, 0:16], Wg_d.rearrange("(k p) n -> p k n", p=128))
        load(attB[:, 0, :], as_d.rearrange("h c -> (h c)").partition_broadcast(128))
        load(attB[:, 1, :], ad_d.rearrange("h c -> (h c)").partition_broadcast(128))
        load(gatB[:, 0, :], gas_d.rearrange("h c -> (h c)").partition_broadcast(128))
        load(gatB[:, 1, :], gad_d.rearrange("h c -> (h c)").partition_broadcast(128))
        load(biasB[:, :], bias_d.partition_broadcast(128))
        load(lnsB[:, :], lns_d.partition_broadcast(128))
        load(lnbB[:, :], lnb_d.partition_broadcast(128))
        load(gB[:, 0, :], bg_d.partition_broadcast(128))
        load(gB[:, 1, :], gam_d.partition_broadcast(128))
        load(gB[:, 2, :], bet_d.partition_broadcast(128))
        load(b2B[:, :, :].rearrange("p e d -> p (e d)"), b2_d.rearrange("e d -> (e d)").partition_broadcast(128))
        weights_in = load(b1c[:, :, :], b1_d.rearrange("e (f p) -> p e f", p=128))

        t = G.do(lambda e: g.iota(iota[:, :], [[1, 128]], base=0, channel_multiplier=0,
                                  allow_small_or_imprecise_dtypes=True))
        t = G.do(lambda e: g.iota(pidx[:, :], [[128, 9]], base=0, channel_multiplier=1,
                                  allow_small_or_imprecise_dtypes=True))
        t = G.do(lambda e: g.memset(ones[:, :], 1.0))
        t = G.do(lambda e: g.memset(epsc[:, :], 1e-5))
        t = G.do(lambda e: g.affine_select(out=ident[:, :], in_=ones[:, :], compare_op=ALU.is_equal, fill=0.0, base=0,
                                           pattern=[[1, 128]], channel_multiplier=-1), t)
        t = G.do(lambda e: g.affine_select(out=tri[:, :], in_=ones[:, :], compare_op=ALU.is_gt, fill=0.0, base=0,
                                           pattern=[[1, 128]], channel_multiplier=-1))
        consts = G.do(lambda e: g.affine_select(out=rmask[:, :], in_=ones[:, 0:1], compare_op=ALU.is_gt, fill=0.0,
                                                base=N - 48 * 128, pattern=[[0, 1]], channel_multiplier=-1))

        pbank = [pb(f"pb{i}", [128, 512]) for i in range(8)]
        free = [None] * 8

        cnt = sb("cnt", [128, T])
        tot = sb("tot", [128, T])
        nch = sb("nch", [128, T])
        nchi = sb("nchi", [128, T], i32)
        cum = sb("cum", [128, T])
        off = sb("off", [128, T])
        tcn = sb("tcn", [128, 9])
        tci = sb("tci", [128, 2, 9], i32)
        junk = sb("junk", [128, T])

        def sort(q, edges):
            J, NCH = q.J, q.NCH
            srcI, dstI = tmp(0, i32, J), tmp(1, i32, J)
            bI, bF = tmp(2, i32, J), tmp(3, f32, J)
            pos, sc = tmp(4, f32, J), tmp(5, f32, J)
            mask, pk = tmp(6, i32, J), tmp(7, i32, J)
            fill = tmp(8, i32, 2048)[:, 0:NCH]
            l_fill, l_tm, l_tml, l_sc, l_raw = (line(f"{nm}{q.n}") for nm in ("l_fill", "l_tm", "l_tml", "l_sc", "l_raw"))
            t = V.do(lambda e: v.memset(fill, SENT + 8192 * SENT_DL))
            S.dma(lambda e: e.dma_start(q.slots_d.rearrange("(p c) o -> p (c o)", p=128), fill), l_fill, t)
            filled = l_fill.now()
            t = V.do(lambda e: v.tensor_scalar(bI, dstI, 7, None, ALU.logical_shift_right), edges)
            t = V.do(lambda e: v.tensor_copy(bF, bI), t)
            t = V.do(lambda e: v.tensor_scalar(bI, dstI, 127, None, ALU.bitwise_and), t)
            t2 = V.do(lambda e: v.tensor_scalar(srcI, srcI, float(N - 1), None, ALU.min))
            t = V.do(lambda e: v.scalar_tensor_tensor(pk, bI, 8192.0, srcI, ALU.mult, ALU.add), t, t2)
            V.do(lambda e: v.memset(pos, float(2 ** 26)))
            for b in range(T):
                t = V.do(lambda e, b=b: v.tensor_scalar(sc, bF, float(b), 0.0, ALU.is_equal, ALU.add,
                                                        accum_out=cnt[:, b:b + 1]), t)
            p = P.do(lambda e: pe.matmul(pbank[0][:, 0:T], ones[:, :], cnt[:, :], start=True, stop=True), t, consts, free[0])
            p = P.do(lambda e: pe.matmul(pbank[1][:, 0:T], tri[:, :], cnt[:, :], start=True, stop=True), free[1])
            t = V.do(lambda e: v.tensor_scalar(nchi[:, :], pbank[0][:, 0:T], 127.0, None, ALU.add), p)
            t = V.do(lambda e: v.tensor_scalar(nchi[:, :], nchi[:, :], 7, None, ALU.logical_shift_right), t)
            t = V.do(lambda e: v.tensor_copy(nch[:, :], nchi[:, :]), t)
            t = V.do(lambda e: v.tensor_tensor_scan(cum[:, :], ones[:, 0:T], nch[:, :], 0.0, ALU.mult, ALU.add), t, consts)
            t = V.do(lambda e: v.tensor_tensor(off[:, :], cum[:, :], nch[:, :], ALU.subtract), t)
            t = V.do(lambda e: v.tensor_scalar(off[:, :], off[:, :], 128.0, -1.0, ALU.mult, ALU.add), t)
            t = V.do(lambda e: v.tensor_tensor(off[:, :], off[:, :], pbank[1][:, 0:T], ALU.add), t)
            free[0] = free[1] = t
            onesJ = ones[:, 0:1].broadcast_to([128, J])
            for b in range(T):
                t = V.do(lambda e, b=b: v.tensor_scalar(mask, bF, float(b), None, ALU.is_equal), t)
                t = V.do(lambda e, b=b: v.tensor_tensor_scan(sc, onesJ, mask, off[:, b:b + 1], ALU.mult, ALU.add), t)
                t = V.do(lambda e, b=b: v.copy_predicated(pos, mask, sc), t)
            posI = bI
            t = V.do(lambda e: v.tensor_copy(posI, pos), t)
            t2 = V.do(lambda e: v.tensor_scalar(mask, posI, 127, None, ALU.bitwise_and), t)
            t3 = V.do(lambda e: v.tensor_scalar(srcI, posI, 7, None, ALU.logical_shift_right))
            addr = V.do(lambda e: v.scalar_tensor_tensor(dstI, mask, float(NCH), srcI, ALU.mult, ALU.add), t2, t3)
            addrU = dstI.bitcast(u32)
            for k in range(q.K):
                t = V.do(lambda e, k=k: v.tensor_scalar(junk[:, :], cum[:, :], pidx[:, k:k + 1], 0.0, ALU.is_le, ALU.add,
                                                        accum_out=tcn[:, k:k + 1]), t)
            t = V.do(lambda e: v.tensor_scalar(tci[:, 0, 0:q.K], tcn[:, 0:q.K], float(q.R), None, ALU.mult), t)
            t = V.do(lambda e: v.tensor_scalar(tci[:, 1, 0:q.K], tcn[:, 0:q.K], float(2 * q.H), None, ALU.mult))
            for w in range(2):
                for k in range(q.K):
                    S.dma(lambda e, w=w, k=k: e.dma_start(q.tm_d[(w * q.K + k) * 128:(w * q.K + k + 1) * 128].rearrange("(p o) -> p o", o=1),
                                                          tci[:, w, k:k + 1]), l_tm, t)
            S.dma(lambda e: e.dma_start(q.tm[:, :], q.tm_d.rearrange("(a n) -> a n", a=1)), l_tml, l_tm.now())
            q.tm_in = l_tml.now()
            G.wait(filled)
            for j in range(J):
                G.dma(lambda e, j=j: e.indirect_dma_start(
                    out=q.slots_d, out_offset=bass.IndirectOffsetOnAxis(ap=addrU[:, j:j + 1], axis=0),
                    in_=pk[:, j:j + 1], in_offset=None, bounds_check=128 * NCH - 1, oob_is_err=False),
                    l_sc, addr)
            raw = tmp(10, i32, 2048)[:, 0:NCH]
            S.dma(lambda e: e.dma_start(raw, q.slots_d.rearrange("(p c) o -> p (c o)", p=128)), l_raw, l_sc.now(), filled)
            q.raw_in = l_raw.now()
            q.scattered = l_sc.now()
            q.raw = raw

        def unpack(q):
            t = V.do(lambda e: v.tensor_scalar(q.idx[:, :], q.raw.bitcast(u32), 8191, None, ALU.bitwise_and), q.raw_in)
            t2 = V.do(lambda e: v.tensor_scalar(q.raw, q.raw, 13, None, ALU.logical_shift_right), t)
            t2 = V.do(lambda e: v.tensor_copy(q.dl[:, :], q.raw), t2)
            return t2

        fold = sb("fold", [128, 2, D])
        t = None
        for w in range(2):
            t = V.do(lambda e, w=w: v.tensor_tensor(fold[:, :, :], Wt[:, :, :], attB[:, w, :].unsqueeze(1).broadcast_to([128, 2, D]),
                                                    ALU.mult), weights_in, t)
            t = V.do(lambda e, w=w: v.tensor_reduce(Wx1[:, :, D + 8 * w:D + 8 * w + 8],
                                                    fold[:, :, :].rearrange("p k (h c) -> p k h c", c=32), X, ALU.add), t)
        for w in range(2):
            t = V.do(lambda e, w=w: v.tensor_tensor(fold[:, :, 0:16], Wx2[:, :, 0:16],
                                                    gatB[:, w, :].unsqueeze(1).broadcast_to([128, 2, 16]), ALU.mult), t)
            t = V.do(lambda e, w=w: v.tensor_reduce(Wx2[:, :, 16 + 4 * w:20 + 4 * w],
                                                    fold[:, :, 0:16].rearrange("p k (h c) -> p k h c", c=4), X, ALU.add), t)
        folded = t

        sort(g1, edges1)

        bst = sb("bst", [128, T, 6])
        mv1 = sb("mv1", [128, T, 2])
        rs1 = sb("rs1", [128, T])
        mv2 = sb("mv2", [128, T, 2])
        rs2 = sb("rs2", [128, T])
        xn = sb("xn", [128, 2, D])
        xTb = sb("xTb", [128, 2, 2, 128])
        hrow = sb("hrow", [128, 2, g1.R])
        asall = sb("asall", [128, T, 8])
        gmx = sb("gmx", [128, 2, 8])

        def stats(get, mv, rs, start):
            t = None
            for i in range(T):
                t = V.do(lambda e, i=i: v.bn_stats(bst[:, i, :], get(i)), *start(i))
                t = V.do(lambda e, i=i: v.bn_aggr(mv[:, i, :], bst[:, i, :]), t)
            r = A.do(lambda e: a.activation(rs[:, :], mv[:, :, 1], ACT.Sqrt, bias=epsc[:, :]), t, consts)
            return V.do(lambda e: v.reciprocal(rs[:, :], rs[:, :]), r)

        st1 = stats(lambda i: x_sb[:, i, :], mv1, rs1, lambda i: [x_in])

        def features(q, Wx, normed, keep_T, ready):
            M = q.F + 2 * q.H
            tT, tabw, cp, hcp = [None] * T, [None] * T, [None] * T, [None] * T
            mmt = [None] * T
            last = None
            for i in range(T):
                s = i % 2
                vt = normed(i, s, (tT[i - 2],) if i >= 2 else (), ready)
                for k in range(2):
                    pt = P.do(lambda e, k=k, s=s: pe.transpose(pbank[s][:, k * 128:k * 128 + 128], xn[:, s, k * 128:k * 128 + 128],
                                                               ident[:, :]), vt, cp[i - 2] if i >= 2 else free[s])
                tT[i] = pt
                dst = xT[:, i, 0:256].rearrange("p (k n) -> p k n", k=2) if keep_T else xTb[:, s, :, :]
                cp[i] = A.do(lambda e, s=s, dst=dst: a.copy(dst, pbank[s][:, 0:256].rearrange("p (k n) -> p k n", k=2)), pt,
                             mmt[i - 2] if i >= 2 and not keep_T else None)
                for k in range(2):
                    mm = P.do(lambda e, k=k, s=s, dst=dst: pe.matmul(pbank[2 + s][:, 0:M], dst[:, k, :], Wx[:, k, :], start=k == 0,
                                                                    stop=k == 1), cp[i], folded, tabw[i - 2] if i >= 2 else free[2 + s])
                mmt[i] = mm
                hc = A.do(lambda e, s=s: a.copy(hrow[:, s, 0:q.R], pbank[2 + s][:, 0:q.R]), mm, hcp[i - 2] if i >= 2 else None)
                V.do(lambda e, i=i, s=s: v.tensor_copy(asall[:, i, 0:q.H], pbank[2 + s][:, q.F:q.R]), mm, hc)
                tabw[i] = last = V.do(lambda e, i=i, s=s: v.tensor_copy(q.tab[:, 2 * q.H * i:2 * q.H * i + q.H],
                                                                        pbank[2 + s][:, q.R:q.R + q.H]))
                hcp[i] = S.dma(lambda e, i=i, s=s: e.dma_start(q.table[128 * i:128 * i + 128, :], hrow[:, s, 0:q.R]), l_h[s], hc)
            free[0], free[1] = cp[T - 1], cp[T - 1]
            free[2] = free[3] = last
            q.table_in = [hcp[T - 1], hcp[T - 2]]
            t = V.do(lambda e: v.tensor_reduce(gmx[:, 0, 0:q.H], asall[:, :, 0:q.H].rearrange("p t h -> p h t"), X, ALU.max), last)
            t = G.do(lambda e: g.partition_all_reduce(gmx[:, 1, 0:q.H], gmx[:, 0, 0:q.H], 128, bass_max), t)
            tabv = q.tab[:, 0:T * 2 * q.H].rearrange("p (t w) -> p t w", t=T)
            t = V.do(lambda e: v.tensor_tensor(tabv[:, :, q.H:2 * q.H], tabv[:, :, 0:q.H],
                                               gmx[:, 1, 0:q.H].unsqueeze(1).broadcast_to([128, T, q.H]), ALU.add), t)
            t = V.do(lambda e: v.scalar_tensor_tensor(tabv[:, :, q.H:2 * q.H], tabv[:, :, q.H:2 * q.H], 0.2,
                                                      tabv[:, :, q.H:2 * q.H], ALU.mult, ALU.max), t)
            q.tab_in = V.do(lambda e: v.memset(q.tab[:, T * 2 * q.H:(T + 1) * 2 * q.H], 0.0), t)

        bass_max = bass.bass_isa.ReduceOp.max

        def normed1(i, s, waits, ready):
            return V.do(lambda e: v.tensor_scalar(xn[:, s, :], x_sb[:, i, :], mv1[:, i, 0:1], rs1[:, i:i + 1], ALU.subtract,
                                                  ALU.mult), ready, *waits)

        features(g1, Wx1, normed1, False, st1)
        up1 = unpack(g1)

        edges2 = load_edges(g2, [g1.scattered, up1])
        sort(g2, edges2)
        up2 = unpack(g2)

        Gb = sb("Gb", [128, NSL, CH, g1.R])
        Sb = sb("Sb", [128, NSL, CH, 128])
        STb = sb("STb", [128, NSL, CH, 128])
        zb = sb("zb", [128, NSL, CH, 8])
        zc = sb("zc", [128, NSL, CH, 8])

        def edge_pass(q, acc, accf, start, unpacked):
            H, C, R, F, NG = q.H, q.C, q.R, q.F, q.NCH // CH
            Gt = [Gb[:, s, :, :].rearrange("p c r -> p (c r)")[:, 0:CH * R].rearrange("p (c r) -> p c r", r=R) for s in range(NSL)]
            zt = [zb[:, s, :, 0:H] for s in range(NSL)]
            ar = [zc[:, s, :, 0:H] for s in range(NSL)]
            gat, sd, trp, stc, adg, z3, wex, msg, agg, add = ({} for _ in range(10))
            adp = {}
            PEr, DVr = [None] * 4, [None] * 4

            def alloc(e, regs, nm):
                for k in range(4):
                    regs[k] = e.alloc_register(f"{nm}{q.n}_{k}")

            P.raw(lambda e: alloc(e, PEr, "per"))
            V.raw(lambda e: alloc(e, DVr, "dvr"))

            def g_gather(i):
                s = i % NSL
                for k in range(CH):
                    c = i * CH + k
                    gat[i] = G.dma(lambda e, k=k, s=s, c=c: e.indirect_dma_start(
                        out=Gt[s][:, k, :], out_offset=None, in_=q.table,
                        in_offset=bass.IndirectOffsetOnAxis(ap=q.idx[:, c:c + 1], axis=0)),
                        l_g[s], agg.get(i - NSL), msg.get(i - NSL), unpacked, *q.table_in)

            def v_onehot(i):
                s = i % NSL
                sd[i] = V.do(lambda e: v.tensor_tensor(Sb[:, s, :, :], iota[:, :].unsqueeze(1).broadcast_to([128, CH, 128]),
                                                       q.dl[:, i * CH:i * CH + CH].unsqueeze(2).broadcast_to([128, CH, 128]),
                                                       ALU.is_equal), agg.get(i - NSL), unpacked, start)

            def p_transpose(i):
                s, b = i % NSL, i % 2
                for k in range(CH):
                    trp[i] = P.do(lambda e, k=k: pe.transpose(pbank[b][:, k * 128:k * 128 + 128], Sb[:, s, k, :], ident[:, :]),
                                  sd[i], stc.get(i - 2, free[b]))

            def a_stcopy(i):
                s, b = i % NSL, i % 2
                stc[i] = A.do(lambda e: a.copy(STb[:, s, :, :].rearrange("p c n -> p (c n)"), pbank[b][:, :]), trp[i],
                              adg.get(i - NSL))

            def p_adst(i):
                s, b = i % NSL, 2 + i % 2
                P.raw(lambda e: e.load(PEr, q.tm[0:1, q.K * 128 + i * CH:q.K * 128 + i * CH + CH]), q.tm_in)
                for k in range(CH):
                    adg[i] = P.do(lambda e, k=k: pe.matmul(
                        pbank[b][:, k * 16:k * 16 + 2 * H], STb[:, s, k, :],
                        q.tab[:, bass.ds(e.snap(PEr[k], min_val=0, max_val=T * 2 * H), 2 * H)], start=True, stop=True),
                        stc[i], q.tab_in, z3.get(i - 2, free[b]))

            def v_score(i):
                s, b = i % NSL, 2 + i % 2
                pv = pbank[b][:, 0:64].rearrange("p (c w) -> p c w", w=16)
                t = V.do(lambda e: v.tensor_tensor(ar[s], Gt[s][:, :, F:R], pv[:, :, 0:H], ALU.add), adg[i], gat[i])
                t = V.do(lambda e: v.scalar_tensor_tensor(ar[s], ar[s], 0.2, ar[s], ALU.mult, ALU.max), t)
                z3[i] = V.do(lambda e: v.tensor_tensor(zt[s], ar[s], pv[:, :, H:2 * H], ALU.subtract), t, wex.get(i - NSL))

            def a_exp(i):
                s = i % NSL
                wex[i] = A.do(lambda e: a.activation(Gt[s][:, :, F:R], zt[s], ACT.Exp), z3[i])

            def v_message(i):
                s = i % NSL
                for k in range(CH if C > 4 else CH):
                    hv = Gt[s][:, k, 0:F].rearrange("p (h c) -> p h c", c=C)
                    msg[i] = V.do(lambda e, hv=hv, k=k: v.tensor_tensor(hv, hv, Gt[s][:, k, F:R].unsqueeze(2).broadcast_to([128, H, C]),
                                                                      ALU.mult), wex[i])

            def p_sum(i):
                s = i % NSL
                for k in range(CH):
                    agg[i] = P.do(lambda e, k=k: pe.matmul(pbank[4 + k][:, 0:R], Sb[:, s, k, :], Gt[s][:, k, :], start=True, stop=True),
                                  msg[i], add.get((i - 1, k), free[4 + k]))
                    adp[(i, k)] = agg[i]

            def v_add(i):
                V.raw(lambda e: e.load(DVr, q.tm[0:1, i * CH:i * CH + CH]), q.tm_in)
                for k in range(CH):
                    def f(e, k=k):
                        o = accf[:, bass.ds(e.snap(DVr[k], min_val=0, max_val=T * R), R)]
                        return v.tensor_tensor(o, o, pbank[4 + k][:, 0:R], ALU.add)
                    add[(i, k)] = V.do(f, adp[(i, k)], add.get((i, k - 1)) if k else add.get((i - 1, CH - 1)), start)

            for i in range(NG + 3):
                if i < NG:
                    g_gather(i)
                    v_onehot(i)
                    p_transpose(i)
                    a_stcopy(i)
                    p_adst(i)
                if 1 <= i < NG + 1:
                    v_score(i - 1)
                    a_exp(i - 1)
                if 2 <= i < NG + 2:
                    v_message(i - 2)
                if 3 <= i:
                    v_add(i - 3)
                if 2 <= i < NG + 2:
                    p_sum(i - 2)
            end = add[(NG - 1, CH - 1)]
            for b in range(2):
                free[b] = stc[NG - 1]
                free[2 + b] = z3[NG - 1]
            for b in range(4, 8):
                free[b] = end
            return end

        zero1 = V.do(lambda e: v.memset(big[:, :], 0.0), g2.scattered, up2)
        done1 = edge_pass(g1, acc1, big, zero1, up1)

        exb = fold
        rec = sb("rec", [128, T, 8])
        t = V.do(lambda e: v.tensor_scalar(rec[:, :, :], acc1[:, 0:T, 256:264], 1e-16, None, ALU.add), done1)
        t = V.do(lambda e: v.reciprocal(rec[:, :, :], rec[:, :, :]), t)
        ue, us = {}, {}
        vb = xn

        def fin_a(i):
            s = i % 2
            u = acc1[:, i, 0:256]
            uh = u.rearrange("p (h c) -> p h c", c=32)
            t0 = V.do(lambda e: v.tensor_scalar(vb[:, s, :], x_sb[:, i, :], mv1[:, i, 0:1], rs1[:, i:i + 1], ALU.subtract, ALU.mult), t)
            t1 = V.do(lambda e: v.tensor_tensor(uh, uh, rec[:, i, :].unsqueeze(2).broadcast_to([128, 8, 32]), ALU.mult), t)
            t1 = V.do(lambda e: v.tensor_tensor(u, u, biasB[:, :], ALU.add), t1)
            t1 = V.do(lambda e: v.tensor_tensor(u, u, vb[:, s, :], ALU.add), t1)
            ue[i] = A.do(lambda e: a.activation(exb[:, s, :], u, ACT.Exp), t1, us.get(i - 2))

        def fin_b(i):
            s = i % 2
            u = acc1[:, i, 0:256]
            t0 = V.do(lambda e: v.tensor_scalar(exb[:, s, :], exb[:, s, :], 1.0, -1.0, ALU.min, ALU.add), ue[i])
            us[i] = V.do(lambda e: v.scalar_tensor_tensor(u, u, 0.0, exb[:, s, :], ALU.max, ALU.add), t0)

        for i in range(T + 1):
            if i < T:
                fin_a(i)
            if i:
                fin_b(i - 1)
        st = stats(lambda i: acc1[:, i, 0:256], mv2, rs2, lambda i: [us[i]])
        tk = {}
        for i in range(T):
            u = acc1[:, i, 0:256]
            t = V.do(lambda e, i=i, u=u: v.tensor_scalar(u, u, mv2[:, i, 0:1], rs2[:, i:i + 1], ALU.subtract, ALU.mult), st)
            t = V.do(lambda e, u=u: v.tensor_tensor(u, u, lnsB[:, :], ALU.mult), t)
            t = V.do(lambda e, u=u: v.tensor_tensor(u, u, lnbB[:, :], ALU.add), t)
            tk[i] = V.do(lambda e, i=i, u=u: v.tensor_tensor(x_sb[:, i, :], x_sb[:, i, :], u, ALU.add), t)
        tk[T - 1] = V.do(lambda e: v.tensor_scalar(x_sb[:, T - 1, :], x_sb[:, T - 1, :], rmask[:, :], None, ALU.mult), tk[T - 1])
        st2 = stats(lambda i: x_sb[:, i, :], mv2, rs2, lambda i: [tk[i]])

        def normed2(i, s, waits, ready):
            return V.do(lambda e: v.tensor_scalar(xn[:, s, :], x_sb[:, i, :], mv2[:, i, 0:1], rs2[:, i:i + 1], ALU.subtract,
                                                  ALU.mult), ready, *waits)

        h2keep = {}

        def features2():
            features(g2, Wx2, normed2, True, st2)

        late = STb[:, :, :, :].rearrange("p s c n -> p (s c n)")
        hk = late[:, 0:784].rearrange("p (t c) -> p t c", t=T)
        features2()
        own = S.dma(lambda e: e.dma_start(acc2[:, 0:T, :], g2.table.rearrange("(t p) r -> p t r", p=128)), l_ld, *g2.table_in)
        tab2 = g2.tab[:, 0:T * 8].rearrange("p (t w) -> p t w", t=T)
        zo = sb("zo", [128, T, 4])
        t = V.do(lambda e: v.tensor_tensor(zo[:, :, :], acc2[:, 0:T, 16:20], tab2[:, :, 0:4], ALU.add), own, g2.tab_in)
        t = V.do(lambda e: v.scalar_tensor_tensor(zo[:, :, :], zo[:, :, :], 0.2, zo[:, :, :], ALU.mult, ALU.max), t)
        t = V.do(lambda e: v.tensor_tensor(zo[:, :, :], zo[:, :, :], tab2[:, :, 4:8], ALU.subtract), t)
        t = A.do(lambda e: a.activation(acc2[:, 0:T, 16:20], zo[:, :, :], ACT.Exp), t)
        for h in range(4):
            tt = V.do(lambda e, h=h: v.tensor_tensor(acc2[:, 0:T, 4 * h:4 * h + 4], acc2[:, 0:T, 4 * h:4 * h + 4],
                                                     acc2[:, 0:T, 16 + h:17 + h].broadcast_to([128, T, 4]), ALU.mult), t)
        t = V.do(lambda e: v.memset(acc2[:, T, :], 0.0), tt)
        done2 = edge_pass(g2, acc2, acc2f, t, up2)

        sq = late[:, 784:1568].rearrange("p (t c) -> p t c", t=T)
        sc4 = late[:, 1568:1764].rearrange("p (t c) -> p t c", t=T)
        r1 = late[:, 1764:1960].rearrange("p (t c) -> p t c", t=T)
        m1 = sb("m1", [128, T])
        ct = sb("ct", [128, T])
        gate = sb("gate", [128, T, 4])
        ag = acc2[:, 0:T, 0:16]
        t = V.do(lambda e: v.tensor_scalar(r1[:, :, :], acc2[:, 0:T, 16:20], 1e-16, None, ALU.add), done2)
        t = V.do(lambda e: v.reciprocal(r1[:, :, :], r1[:, :, :]), t)
        for h in range(4):
            tt = V.do(lambda e, h=h: v.tensor_tensor(hk[:, :, 4 * h:4 * h + 4], acc2[:, 0:T, 4 * h:4 * h + 4],
                                                     r1[:, :, h:h + 1].broadcast_to([128, T, 4]), ALU.mult), t)

        def bc16(ap):
            return ap.unsqueeze(1).broadcast_to([128, T, 16])

        def col16(ap):
            return ap.unsqueeze(2).broadcast_to([128, T, 16])

        t = V.do(lambda e: v.tensor_tensor(hk[:, :, :], hk[:, :, :], bc16(gB[:, 0, :]), ALU.add), tt)
        t = V.do(lambda e: v.tensor_reduce(m1[:, :], hk[:, :, :], X, ALU.add), t)
        t = V.do(lambda e: v.tensor_scalar(m1[:, :], m1[:, :], 1.0 / 16, None, ALU.mult), t)
        t = V.do(lambda e: v.tensor_tensor(hk[:, :, :], hk[:, :, :], col16(m1[:, :]), ALU.subtract), t)
        t = V.do(lambda e: v.tensor_tensor(sq[:, :, :], hk[:, :, :], hk[:, :, :], ALU.mult), t)
        t = V.do(lambda e: v.tensor_reduce(ct[:, :], sq[:, :, :], X, ALU.add), t)
        t = A.do(lambda e: a.activation(ct[:, :], ct[:, :], ACT.Sqrt, scale=1.0 / 16, bias=epsc[:, :]), t)
        t = V.do(lambda e: v.reciprocal(ct[:, :], ct[:, :]), t)
        t = V.do(lambda e: v.tensor_tensor(hk[:, :, :], hk[:, :, :], col16(ct[:, :]), ALU.mult), t)
        t = V.do(lambda e: v.tensor_tensor(hk[:, :, :], hk[:, :, :], bc16(gB[:, 1, :]), ALU.mult), t)
        t = V.do(lambda e: v.tensor_tensor(hk[:, :, :], hk[:, :, :], bc16(gB[:, 2, :]), ALU.add), t)
        t = V.do(lambda e: v.tensor_tensor(sc4[:, :, :], hk[:, :, 0:4], hk[:, :, 4:8], ALU.add), t)
        t = V.do(lambda e: v.tensor_tensor(sc4[:, :, :], sc4[:, :, :], hk[:, :, 8:12], ALU.add), t)
        t = V.do(lambda e: v.tensor_tensor(sc4[:, :, :], sc4[:, :, :], hk[:, :, 12:16], ALU.add), t)
        t = V.do(lambda e: v.tensor_scalar(sc4[:, :, :], sc4[:, :, :], 0.25, None, ALU.mult), t)
        t = V.do(lambda e: v.tensor_reduce(m1[:, :], sc4[:, :, :], X, ALU.max), t)
        rank = sq[:, :, 0:4]
        t = V.do(lambda e: v.memset(sq[:, :, 0:4], 0.0), t)
        for i in range(4):
            for j in range(4):
                if i == j:
                    continue
                op = ALU.is_ge if j < i else ALU.is_gt
                t = V.do(lambda e, i=i, j=j, op=op: v.tensor_tensor(ct[:, :], sc4[:, :, j], sc4[:, :, i], op), t)
                t = V.do(lambda e, i=i: v.tensor_tensor(sq[:, :, i], sq[:, :, i], ct[:, :], ALU.add), t)
        t = V.do(lambda e: v.tensor_scalar(rank, rank, 2.0, None, ALU.is_lt), t)
        t = V.do(lambda e: v.tensor_tensor(r1[:, :, :], sc4[:, :, :], m1[:, :].unsqueeze(2).broadcast_to([128, T, 4]),
                                           ALU.subtract), t)
        t = A.do(lambda e: a.activation(r1[:, :, :], r1[:, :, :], ACT.Exp), t)
        t = V.do(lambda e: v.tensor_tensor(r1[:, :, :], r1[:, :, :], rank, ALU.mult), t)
        t = V.do(lambda e: v.tensor_reduce(ct[:, :], r1[:, :, :], X, ALU.add), t)
        t = V.do(lambda e: v.reciprocal(ct[:, :], ct[:, :]), t)
        gated = V.do(lambda e: v.tensor_tensor(gate[:, :, :], r1[:, :, :], ct[:, :].unsqueeze(2).broadcast_to([128, T, 4]),
                                               ALU.mult), t)

        Wb1 = Sb[:, :, :, :].rearrange("p s c n -> p (s c n)")
        Wb2 = STb[:, :, :, :].rearrange("p s c n -> p (s c n)")
        W1s = Wb1.rearrange("p (w k f) -> p w k f", w=2, k=2)
        W2s = Wb2.rearrange("p (w f d) -> p w f d", w=2, f=4)
        hh = Gb[:, :, :, :].rearrange("p s c r -> p (s c r)")[:, 0:4096].rearrange("p (s f n) -> p s f n", s=2, f=4)
        l_w1 = [line(f"l_w1{i}") for i in range(2)]
        groups = [(4 * i, 4) for i in range(12)] + [(48, 1)]
        use1, use2 = {}, {}
        wl = {}

        def wload(ei):
            s = ei % 2
            S.dma(lambda e: e.dma_start(W1s[:, s, :, :], W1_d[ei].rearrange("(k p) f -> p k f", p=128)), l_w1[s], use1.get(ei - 2), gated)
            wl[ei] = S.dma(lambda e: e.dma_start(W2s[:, s, :, :], W2_d[ei].rearrange("(f p) d -> p f d", p=128)), l_w1[s],
                           use2.get(ei - 2))

        wload(0)
        wload(1)
        gel, mm2, ev = {}, {}, {}
        fr = {b: free[b] for b in range(8)}
        n1 = n2 = 0
        blk = [(ei, gi) for ei in range(4) for gi in range(13)]
        last_x = {}

        def up(bi):
            nonlocal n1
            ei, gi = blk[bi]
            t0, nt = groups[gi]
            s, w = bi % 2, ei % 2
            for f in range(4):
                b = n1 % 4
                n1 += 1
                for k in range(2):
                    p = P.do(lambda e, k=k, f=f, b=b: pe.matmul(
                        pbank[b][:, 0:nt * 128], W1s[:, w, k, f * 128:f * 128 + 128],
                        xT[:, t0:t0 + nt, k * 128:k * 128 + 128], start=k == 0, stop=k == 1), wl[ei], fr[b])
                gel[(bi, f)] = fr[b] = A.do(lambda e, f=f, b=b: a.activation(hh[:, s, f, 0:nt * 128], pbank[b][:, 0:nt * 128],
                                                                             ACT.Gelu, bias=b1c[:, ei, f:f + 1]),
                                            p, mm2.get(bi - 2))
            use1[ei] = p

        def down(bi):
            nonlocal n2
            ei, gi = blk[bi]
            t0, nt = groups[gi]
            s, w = bi % 2, ei % 2
            for j in range(nt):
                ti = t0 + j
                b = 4 + n2 % 4
                n2 += 1
                for f in range(4):
                    p = P.do(lambda e, f=f, b=b, j=j: pe.matmul(pbank[b][:, 0:D], hh[:, s, f, j * 128:j * 128 + 128],
                                                                W2s[:, w, f, :], start=f == 0, stop=f == 3),
                             gel[(bi, f)], fr[b])
                fr[b] = V.do(lambda e, b=b, ti=ti: v.scalar_tensor_tensor(x_sb[:, ti, :], pbank[b][:, 0:D], gate[:, ti, ei:ei + 1],
                                                                         x_sb[:, ti, :], ALU.mult, ALU.add), p, gated,
                             last_x.get(ti))
                last_x[ti] = V.do(lambda e, ti=ti: v.scalar_tensor_tensor(x_sb[:, ti, :], b2B[:, ei, :], gate[:, ti, ei:ei + 1],
                                                                         x_sb[:, ti, :], ALU.mult, ALU.add), fr[b])
            mm2[bi] = use2[ei] = p
            if ei == 3:
                if gi < 12:
                    S.dma(lambda e: e.dma_start(out_d[t0 * 128:(t0 + nt) * 128, :].rearrange("(t p) d -> p t d", p=128),
                                                x_sb[:, t0:t0 + nt, :]), l_o, *[last_x[t0 + j] for j in range(nt)])
                else:
                    S.dma(lambda e: e.dma_start(out_d[48 * 128:N, :], x_sb[0:N - 48 * 128, 48, :]), l_o, last_x[48])

        up(0)
        for bi in range(len(blk)):
            if bi + 1 < len(blk):
                up(bi + 1)
            down(bi)
            if blk[bi][1] == 12 and blk[bi][0] + 2 < 4:
                wload(blk[bi][0] + 2)
        S.wait(l_o.now())

        block = ctx.enter_context(nc.Block())

        @block.sync
        def _(e):
            S.emit(e)

        @block.scalar
        def _(e):
            A.emit(e)

        @block.vector
        def _(e):
            V.emit(e)

        @block.tensor
        def _(e):
            P.emit(e)

        @block.gpsimd
        def _(e):
            G.emit(e)


_INS = ['x', 'src', 'dst', 'L0_gnn_W', 'L0_gnn_att_src', 'L0_gnn_att_dst', 'L0_gnn_bias', 'L0_gnn_ln_scale',
        'L0_gnn_ln_bias', 'L0_ffn_W_gat', 'L0_ffn_att_src', 'L0_ffn_att_dst', 'L0_ffn_b_gat', 'L0_ffn_ln_gamma',
        'L0_ffn_ln_beta', 'L0_ffn_W1', 'L0_ffn_b1', 'L0_ffn_W2', 'L0_ffn_b2', 'L0_ffn_edge_index']


def kernel(**inputs):
    import numpy as _np
    import concourse.bacc as _bacc
    from concourse import mybir as _mybir
    from concourse.bass_utils import run_bass_kernel_spmd as _run

    nc = _bacc.Bacc("TRN2", target_bir_lowering=False, num_devices=1)
    arrays, args = {}, []
    for name in _INS:
        a = _np.ascontiguousarray(inputs[name])
        arrays[f"in_{name}_dram"] = a
        args.append(nc.dram_tensor(f"in_{name}_dram", a.shape, _mybir.dt.from_np(a.dtype), kind="ExternalInput").ap())
    args.append(nc.dram_tensor("out_0_dram", (N, D), _mybir.dt.float32, kind="ExternalOutput").ap())
    build(nc, *args)
    r = _run(nc, [arrays], core_ids=[0])
    return r.results[0]["out_0_dram"]
```

```python
import concourse.bass as bass
from concourse import mybir
from contextlib import ExitStack

N = 6250
T = 49
NP = T * 128
D = 256
BLK = 128
CH = 4
NSL = 4
SPREAD = 60.0


class Queue:

    def __init__(self, name, sem):
        self.name, self.sem, self.count, self.items, self.seen = name, sem, 0, [], {}

    def wait(self, *tokens):
        for tok in tokens:
            if tok is None:
                continue
            sem, value = tok
            if self.seen.get(id(sem), 0) >= value:
                continue
            self.seen[id(sem)] = value
            self.items.append(lambda eng, sem=sem, value=value: eng.wait_ge(sem, value))

    def do(self, fn, *waits):
        self.wait(*waits)
        self.count += 1
        self.items.append(lambda eng, fn=fn: fn(eng).then_inc(self.sem, 1))
        return (self.sem, self.count)

    def raw(self, fn, *waits):
        self.wait(*waits)
        self.items.append(lambda eng, fn=fn: fn(eng))

    def dma(self, fn, line, *waits):
        self.wait(*waits)
        line.count += 16
        self.items.append(lambda eng, fn=fn, sem=line.sem: fn(eng).then_inc(sem, 16))
        return (line.sem, line.count)

    def emit(self, eng):
        for item in self.items:
            item(eng)


class Line:
    def __init__(self, sem):
        self.sem, self.count = sem, 0

    def now(self):
        return (self.sem, self.count)


def build(nc, x_d, src_d, dst_d, W_d, as_d, ad_d, bias_d, lns_d, lnb_d, Wg_d, gas_d, gad_d, bg_d, gam_d, bet_d,
          W1_d, b1_d, W2_d, b2_d, ei_d, out_d):
    f32, i32, u32, i16, f16 = (mybir.dt.float32, mybir.dt.int32, mybir.dt.uint32, mybir.dt.int16, mybir.dt.float16)
    ALU = mybir.AluOpType
    ACT = mybir.ActivationFunctionType
    X = mybir.AxisListType.X

    ctx = ExitStack()
    with ctx:
        def sb(name, shape, dt=f32):
            return ctx.enter_context(nc.sbuf_tensor(name, shape, dt))

        def pb(name, shape, dt=f32):
            return ctx.enter_context(nc.psum_tensor(name, shape, dt))

        def sem(name):
            return ctx.enter_context(nc.semaphore(name))

        lines, conditional = [], []

        def line(name):
            lines.append(Line(sem(name)))
            return lines[-1]

        def queues(tag):
            return tuple(Queue(n, sem(f"q_{n}{tag}")) for n in ("dve", "act", "pe", "pool", "sp"))

        V, A, P, G, S = main = queues("")
        v, a, g, pe = nc.vector, nc.scalar, nc.gpsimd, nc.tensor
        ENG = {"dve": v, "act": a, "pe": pe, "pool": g, "sp": nc.sync}
        flags = sb("flags", [1, 16], i32)

        def when(index, ready, subs, ends):
            conditional.extend(ends)
            starts = [(q.sem, q.count) for q in main if q.count] + [ln.now() for ln in lines if ln.count and ln not in conditional]
            finals = [(q.sem, q.count) for q in subs if q.count] + [ln.now() for ln in ends if ln.count]
            for mq, sq in zip(main, subs):
                taken, sq.items = sq.items, []

                def item(eng, taken=taken, name=sq.name):
                    reg = eng.alloc_register(f"flag{index}_{name}")
                    eng.wait_ge(*ready)
                    eng.load([reg], flags[0:1, index:index + 1])
                    with eng.If_ne(reg, 0):
                        for st in starts:
                            eng.wait_ge(*st)
                        for it in taken:
                            it(eng)
                        for fi in finals:
                            eng.wait_ge(*fi)
                    eng.free_register(reg)
                mq.items.append(item)

        class Graph:
            pass

        g1, g2 = Graph(), Graph()
        g1.n, g1.E, g1.J, g1.H, g1.C = 1, 100000, 782, 8, 32
        g2.n, g2.E, g2.J, g2.H, g2.C = 2, 131072, 1024, 4, 4
        for q in (g1, g2):
            q.F = q.H * q.C
            q.R = q.F + q.H
            q.NCH = -(-(-(-q.E // BLK) + T) // CH) * CH
            q.K = -(-q.NCH // BLK)
            q.table = nc.dram_tensor(f"table{q.n}", (NP, q.R), f32).ap()
            q.asrc = nc.dram_tensor(f"asrc{q.n}", (NP, q.H), f32).ap()
            q.tm_d = nc.dram_tensor(f"tm{q.n}", (2 * q.K * 128,), i16).ap()
            q.dl = sb(f"dl{q.n}", [128, q.NCH])
            q.tab = sb(f"tab{q.n}", [128, (T + 1) * 2 * q.H])
            q.tm = sb(f"tmr{q.n}", [1, 2 * q.K * 128], i16)
            q.cum = sb(f"cum{q.n}", [128, T])
            q.flagrow = sb(f"fr{q.n}", [1, 8])
        idx1f = sb("idx1", [128, 1664])
        g1.idx = idx1f[:, 0:g1.NCH].bitcast(u32)
        g2.idx = sb("idx2", [128, g2.NCH], u32)
        slots1 = nc.dram_tensor("slots1", (g1.NCH * BLK, 2), i32).ap()
        slots2 = nc.dram_tensor("slots2", (g2.NCH * BLK, 1), i32).ap()
        rowS_d = nc.dram_tensor("rowS", (g1.J, BLK), i32).ap()
        rowD_d = nc.dram_tensor("rowD", (g1.J, BLK), i32).ap()
        Y_d = nc.dram_tensor("Y", (NP, 4, D), f32).ap()

        big = sb("big", [128, (T + 1) * g1.R])
        x_f = sb("x_sb", [128, T * D])
        x_sb = x_f[:, :].rearrange("p (t d) -> p t d", d=D)
        acc1 = big[:, :].rearrange("p (t r) -> p t r", r=g1.R)
        acc2f = sb("acc2", [128, (T + 1) * g2.R])
        acc2 = acc2f[:, :].rearrange("p (t r) -> p t r", r=g2.R)
        xT = acc1

        early = sb("early", [128, 4608])

        def part(lo, n, dt=f32):
            ap = early[:, lo:lo + n]
            return ap if dt == f32 else ap.bitcast(dt)

        Wt = part(0, 512).rearrange("p (k d) -> p k d", k=2)
        attB = part(512, 512).rearrange("p (k d) -> p k d", k=2)
        fold = part(1024, 512).rearrange("p (k d) -> p k d", k=2)
        xn = part(1536, 512).rearrange("p (k d) -> p k d", k=2)
        xTb = part(2048, 512).rearrange("p (s k n) -> p s k n", s=2, k=2)
        hrow = part(2560, 528).rearrange("p (s r) -> p s r", s=2)
        Wx1 = part(3088, 544).rearrange("p (k d) -> p k d", k=2)
        biasB, lnsB, lnbB = part(3632, 256), part(3888, 256), part(4144, 256)

        Wx2 = sb("Wx2", [128, 2, 24])
        gatB = sb("gatB", [128, 2, 16])
        gB = sb("gB", [128, 3, 16])
        b2B = sb("b2B", [128, 4, D])
        b1c = sb("b1c", [128, 4, 4])
        iota = sb("iota", [128, 128])
        ident = sb("ident", [128, 128])
        tri = sb("tri", [128, 128])
        ones = sb("ones", [128, 128])
        pidx = sb("pidx", [128, 9])
        rmask = sb("rmask", [128, 1])
        epsc = sb("epsc", [128, 1])
        iota16 = sb("iota16", [128, g2.NCH], f16)
        cnt, tot, pre, nch, dd, off, junk = (sb(n, [128, T]) for n in ("cnt", "tot", "pre", "nch", "dd", "off", "junk"))
        nchi = sb("nchi", [128, T], i32)
        tcn = sb("tcn", [128, 9])
        t128 = sb("t128", [128, 9])
        tci = sb("tci", [128, 2, 9], i16)
        pair = sb("pair", [128, 9])
        pairu = sb("pairu", [128, 9], u32)
        small = sb("small", [128, 32])
        small4 = sb("small4", [128, 4 * T])
        PRE2 = 24

        pbank = [pb(f"pb{i}", [128, 512]) for i in range(8)]
        free = [None] * 8

        l_x, l_w, l_e1, l_e2 = (line(n) for n in ("l_x", "l_w", "l_e1", "l_e2"))

        def tmp(i, dt, n=1024):
            ap = big[:, i * 1024:i * 1024 + n]
            return ap.bitcast(dt) if dt != f32 else ap

        def xtmp(i, dt, n=1024):
            ap = x_f[:, i * 1024:i * 1024 + n]
            return ap.bitcast(dt) if dt != f32 else ap

        src1, dst1, nxt1 = tmp(0, i32, 782), tmp(1, i32, 782), tmp(2, i32, 782)
        V.do(lambda e: v.memset(tmp(0, i32), 0))
        V.do(lambda e: v.memset(tmp(1, i32), 8191))
        t = V.do(lambda e: v.memset(tmp(2, i32), 8191))
        J1 = g1.J
        for buf, ap, o in ((src1, src_d, 0), (dst1, dst_d, 0), (nxt1, dst_d, 1)):
            S.dma(lambda e, buf=buf, ap=ap, o=o: e.dma_start(
                buf[0:127, :], ap[o:o + 127 * J1].rearrange("(p j) -> p j", j=J1)), l_e1, t)
            n = g1.E - 127 * J1 - o
            S.dma(lambda e, buf=buf, ap=ap, o=o, n=n: e.dma_start(
                buf[127:128, 0:n], ap[o + 127 * J1:g1.E].rearrange("(p j) -> p j", p=1)), l_e1)
        edges1 = l_e1.now()
        t = V.do(lambda e: v.memset(x_sb[:, T - 1, :], 0.0))
        xv = x_d[0:48 * 128, :].rearrange("(t p) d -> p t d", p=128)
        for k in range(4):
            S.dma(lambda e, k=k: e.dma_start(x_sb[:, 12 * k:12 * k + 12, :], xv[:, 12 * k:12 * k + 12, :]), l_x)
        x_in = S.dma(lambda e: e.dma_start(x_sb[0:N - 48 * 128, 48, :], x_d[48 * 128:N, :]), l_x, t)

        def load(dst, srcap, *waits):
            return S.dma(lambda e: e.dma_start(dst, srcap, allow_slow_non_contiguous=True), l_w, *waits)

        load(Wt, W_d.rearrange("(k p) n -> p k n", p=128))
        load(Wx1[:, :, 0:D], W_d.rearrange("(k p) n -> p k n", p=128))
        load(Wx2[:, :, 0:16], Wg_d.rearrange("(k p) n -> p k n", p=128))
        load(attB[:, 0, :], as_d.rearrange("h c -> (h c)").partition_broadcast(128))
        load(attB[:, 1, :], ad_d.rearrange("h c -> (h c)").partition_broadcast(128))
        load(gatB[:, 0, :], gas_d.rearrange("h c -> (h c)").partition_broadcast(128))
        load(gatB[:, 1, :], gad_d.rearrange("h c -> (h c)").partition_broadcast(128))
        load(biasB, bias_d.partition_broadcast(128))
        load(lnsB, lns_d.partition_broadcast(128))
        load(lnbB, lnb_d.partition_broadcast(128))
        load(gB[:, 0, :], bg_d.partition_broadcast(128))
        load(gB[:, 1, :], gam_d.partition_broadcast(128))
        load(gB[:, 2, :], bet_d.partition_broadcast(128))
        load(b2B[:, :, :].rearrange("p e d -> p (e d)"), b2_d.rearrange("e d -> (e d)").partition_broadcast(128))
        weights_in = load(b1c[:, :, :], b1_d.rearrange("e (f p) -> p e f", p=128))

        imp = dict(allow_small_or_imprecise_dtypes=True)
        t = G.do(lambda e: g.iota(iota[:, :], [[1, 128]], base=0, channel_multiplier=0, **imp))
        G.do(lambda e: g.iota(pidx[:, :], [[128, 9]], base=0, channel_multiplier=1, **imp))
        G.do(lambda e: g.iota(iota16[:, :], [[1, g2.NCH]], base=0, channel_multiplier=0, **imp))
        t = G.do(lambda e: g.memset(ones[:, :], 1.0))
        G.do(lambda e: g.memset(epsc[:, :], 1e-5))
        G.do(lambda e: g.affine_select(out=ident[:, :], in_=ones[:, :], compare_op=ALU.is_equal, fill=0.0, base=0,
                                       pattern=[[1, 128]], channel_multiplier=-1), t)
        G.do(lambda e: g.affine_select(out=tri[:, :], in_=ones[:, :], compare_op=ALU.is_gt, fill=0.0, base=0,
                                       pattern=[[1, 128]], channel_multiplier=-1))
        consts = G.do(lambda e: g.affine_select(out=rmask[:, :], in_=ones[:, 0:1], compare_op=ALU.is_gt, fill=0.0,
                                                base=N - 48 * 128, pattern=[[0, 1]], channel_multiplier=-1))

        def tiles_of(Vq, dstI, bI, bF, sc, ready, step=None):
            t = Vq.do(lambda e: v.tensor_scalar(bI, dstI, 7, None, ALU.logical_shift_right), ready)
            t = Vq.do(lambda e: v.tensor_copy(bF, bI), t)
            for b in range(T):
                t = Vq.do(lambda e, b=b: v.tensor_scalar(sc, bF, float(b), 0.0, ALU.is_equal, ALU.add,
                                                         accum_out=cnt[:, b:b + 1]), t)
                yield t

        def totals(Vq, Pq, ready, banks):
            t = Pq.do(lambda e: pe.matmul(pbank[banks[0]][:, 0:T], ones[:, :], cnt[:, :], start=True, stop=True), ready, consts,
                      free[banks[0]])
            t = Pq.do(lambda e: pe.matmul(pbank[banks[1]][:, 0:T], tri[:, :], cnt[:, :], start=True, stop=True), free[banks[1]])
            t = Vq.do(lambda e: v.tensor_copy(tot[:, :], pbank[banks[0]][:, 0:T]), t)
            return Vq.do(lambda e: v.tensor_copy(pre[:, :], pbank[banks[1]][:, 0:T]), t)

        def prefix(Vq, cum, n, ready):
            return Vq.do(lambda e: v.tensor_tensor_scan(cum, ones[:, 0:T], n, 0.0, ALU.mult, ALU.add), ready, consts)

        def shift7(Vq, out, in_, add, ready):
            t = Vq.do(lambda e: v.tensor_scalar(nchi[:, :], in_, float(add), None, ALU.add), ready)
            t = Vq.do(lambda e: v.tensor_scalar(nchi[:, :], nchi[:, :], 7, None, ALU.arith_shift_right), t)
            return Vq.do(lambda e: v.tensor_copy(out, nchi[:, :]), t)

        def padded_chunks(Vq, cum, ready):
            t = shift7(Vq, nch[:, :], tot[:, :], 127, ready)
            return prefix(Vq, cum, nch[:, :], t)

        def offsets(Vq, cum, ready):
            t = Vq.do(lambda e: v.tensor_tensor(off[:, :], cum, nch[:, :], ALU.subtract), ready)
            t = Vq.do(lambda e: v.tensor_scalar(off[:, :], off[:, :], 128.0, -1.0, ALU.mult, ALU.add), t)
            return Vq.do(lambda e: v.tensor_tensor(off[:, :], off[:, :], pre[:, :], ALU.add), t)

        def tile_map(q, Vq, Sq, tag, ready):
            lt, ll = line(f"l_tm{tag}"), line(f"l_tml{tag}")
            t = ready
            for k in range(q.K):
                t = Vq.do(lambda e, k=k: v.tensor_scalar(junk[:, :], q.cum[:, :], pidx[:, k:k + 1], 0.0, ALU.is_le, ALU.add,
                                                         accum_out=tcn[:, k:k + 1]), t)
            K = q.K
            Vq.do(lambda e: v.tensor_scalar(tci[:, 0, 0:K], tcn[:, 0:K], float(q.R), None, ALU.mult), t)
            t = Vq.do(lambda e: v.tensor_scalar(tci[:, 1, 0:K], tcn[:, 0:K], float(2 * q.H), None, ALU.mult))
            for w in range(2):
                for k in range(K):
                    Sq.dma(lambda e, w=w, k=k: e.dma_start(
                        q.tm_d[(w * K + k) * 128:(w * K + k + 1) * 128].rearrange("(p o) -> p o", o=1), tci[:, w, k:k + 1]), lt, t)
            Sq.dma(lambda e: e.dma_start(q.tm[:, :], q.tm_d.rearrange("(a n) -> a n", a=1)), ll, lt.now())
            return t, ll.now(), [lt, ll]

        def ranks(Vq, q, bF, mask, sc, pos, ready):
            J = q.J
            onesJ = ones[:, 0:1].broadcast_to([128, J])
            t = Vq.do(lambda e: v.memset(pos, float(2 ** 26)), ready)
            for b in range(T):
                t = Vq.do(lambda e, b=b: v.tensor_scalar(mask, bF, float(b), None, ALU.is_equal), t)
                yield t
                t = Vq.do(lambda e, b=b: v.tensor_tensor_scan(sc, onesJ, mask, off[:, b:b + 1], ALU.mult, ALU.add), t)
                yield t
                t = Vq.do(lambda e, b=b: v.copy_predicated(pos, mask, sc), t)
                yield t

        def run(gen):
            t = None
            for t in gen:
                pass
            return t

        bI1, bF1, sc1 = tmp(3, i32, J1), tmp(4, f32, J1), tmp(5, f32, J1)
        l_row = line("l_row")
        S.dma(lambda e: e.dma_start(rowS_d.rearrange("a b -> (a b)").rearrange("(p j) -> p j", p=128), src1), l_row, edges1)
        S.dma(lambda e: e.dma_start(rowD_d.rearrange("a b -> (a b)").rearrange("(p j) -> p j", p=128), dst1), l_row)
        rows_out = l_row.now()
        t = run(tiles_of(V, dst1, bI1, bF1, sc1, edges1))
        t = V.do(lambda e: v.scalar_tensor_tensor(sc1, dst1, 1.0, nxt1, ALU.mult, ALU.is_gt, accum_out=small[:, 0:1]), t)
        t = totals(V, P, t, (0, 1))
        t = V.do(lambda e: v.tensor_tensor_scan(off[:, :], ones[:, 0:T], tot[:, :], 0.0, ALU.mult, ALU.add), t)
        t = V.do(lambda e: v.tensor_tensor(dd[:, :], off[:, :], tot[:, :], ALU.subtract), t)
        t = shift7(V, dd[:, :], dd[:, :], 0, t)
        t = shift7(V, nch[:, :], off[:, :], -1, t)
        t = V.do(lambda e: v.tensor_tensor(nch[:, :], nch[:, :], dd[:, :], ALU.subtract), t)
        t = V.do(lambda e: v.tensor_scalar(nch[:, :], nch[:, :], 1.0, None, ALU.add), t)
        t = V.do(lambda e: v.tensor_scalar(off[:, :], tot[:, :], 0.0, None, ALU.is_gt), t)
        t = V.do(lambda e: v.tensor_tensor(nch[:, :], nch[:, :], off[:, :], ALU.mult), t)
        t = prefix(V, g1.cum[:, :], nch[:, :], t)
        t = V.do(lambda e: v.tensor_tensor(dd[:, :], dd[:, :], g1.cum[:, :], ALU.subtract), t)
        t = V.do(lambda e: v.tensor_tensor(dd[:, :], dd[:, :], nch[:, :], ALU.add), t)
        t = V.do(lambda e: v.tensor_tensor(off[:, 0:T - 1], dd[:, 1:T], dd[:, 0:T - 1], ALU.subtract), t)
        t = V.do(lambda e: v.memset(off[:, T - 1:T], 0.0), t)
        for k in range(g1.K):
            t = V.do(lambda e, k=k: v.scalar_tensor_tensor(junk[:, :], g1.cum[:, :], pidx[:, k:k + 1], off[:, :], ALU.is_le,
                                                           ALU.mult, accum_out=pair[:, k:k + 1]), t)
        t = V.do(lambda e: v.tensor_tensor(pair[:, 0:g1.K], pair[:, 0:g1.K], pidx[:, 0:g1.K], ALU.add), t)
        t = V.do(lambda e: v.tensor_scalar(pairu[:, 0:g1.K], pair[:, 0:g1.K], float(J1 - 1), 0.0, ALU.min, ALU.max), t)
        t, tm1_in, _ = tile_map(g1, V, S, "1", t)
        g1.tm_in = [tm1_in]
        R1S, R1D = tmp(6, i32, 896).rearrange("p (k n) -> p k n", n=128), tmp(7, i32, 896).rearrange("p (k n) -> p k n", n=128)
        l_blk = line("l_blk")
        for k in range(g1.K):
            for rb, rd in ((R1S, rowS_d), (R1D, rowD_d)):
                G.dma(lambda e, k=k, rb=rb, rd=rd: e.indirect_dma_start(
                    out=rb[:, k, :], out_offset=None, in_=rd,
                    in_offset=bass.IndirectOffsetOnAxis(ap=pairu[:, k:k + 1], axis=0)), l_blk, rows_out, t)
        blocks_in = l_blk.now()
        t = P.do(lambda e: pe.matmul(pbank[0][:, 64:65], ones[:, :], small[:, 0:1], start=True, stop=True), t)
        flag1 = V.do(lambda e: v.tensor_copy(flags[0:1, 0:1], pbank[0][0:1, 64:65]), t)
        free[0] = free[1] = flag1

        U = VU, AU, PU, GU, SU = queues("u")
        l_fu, l_su, l_ru = line("l_fu"), line("l_su"), line("l_ru")
        fillu = tmp(8, i32, 2 * 896).rearrange("p (n w) -> p n w", w=2)
        VU.do(lambda e: v.memset(fillu[:, :, 0], N))
        t = VU.do(lambda e: v.memset(fillu[:, :, 1], 8191))
        SU.dma(lambda e: e.dma_start(slots1.rearrange("(p c) w -> p (c w)", p=128), fillu[:, 0:832, :].rearrange("p n w -> p (n w)")), l_fu, t)
        t = padded_chunks(VU, g1.cum[:, :], None)
        t = offsets(VU, g1.cum[:, :], t)
        masku, posu = tmp(10, i32, J1), tmp(11, f32, J1)
        t = run(ranks(VU, g1, bF1, masku, sc1, posu, t))
        t = VU.do(lambda e: v.tensor_copy(bI1, posu), t)
        payu = tmp(8, i32, 2 * 832).rearrange("p (n w) -> p n w", w=2)
        t = VU.do(lambda e: v.tensor_copy(payu[:, 0:J1, 0], src1), l_fu.now(), t)
        t = VU.do(lambda e: v.tensor_copy(payu[:, 0:J1, 1], dst1), t)
        for j in range(J1):
            GU.dma(lambda e, j=j: e.indirect_dma_start(
                out=slots1, out_offset=bass.IndirectOffsetOnAxis(ap=bI1.bitcast(u32)[:, j:j + 1], axis=0),
                in_=payu[:, j, :], in_offset=None, bounds_check=BLK * g1.NCH - 1, oob_is_err=False), l_su, t, l_fu.now())
        t, _, endu = tile_map(g1, VU, SU, "u", t)
        rawu = tmp(8, i32, 7 * 256).rearrange("p (k n w) -> p k n w", k=7, w=2)
        full = g1.NCH // 128
        SU.dma(lambda e: e.dma_start(rawu[:, 0:full, :, :].rearrange("p k n w -> p k (n w)"),
                                     slots1[0:full * 128 * 128, :].rearrange("(k p n) w -> p k (n w)", p=128, n=128)), l_ru,
               l_su.now())
        SU.dma(lambda e: e.dma_start(rawu[0:g1.NCH - full * 128, full, :, :].rearrange("p n w -> p (n w)"),
                                     slots1[full * 128 * 128:g1.NCH * 128, :].rearrange("(p n) w -> p (n w)", n=128)), l_ru,
               l_su.now())
        t = VU.do(lambda e: v.tensor_copy(R1S, rawu[:, :, :, 0]), l_ru.now(), t)
        VU.do(lambda e: v.tensor_copy(R1D, rawu[:, :, :, 1]), t)

        t = None
        for w in range(2):
            t = V.do(lambda e, w=w: v.tensor_tensor(fold, Wt, attB[:, w, :].unsqueeze(1).broadcast_to([128, 2, D]),
                                                    ALU.mult), weights_in, t)
            t = V.do(lambda e, w=w: v.tensor_reduce(Wx1[:, :, D + 8 * w:D + 8 * w + 8],
                                                    fold.rearrange("p k (h c) -> p k h c", c=32), X, ALU.add), t)
        for w in range(2):
            t = V.do(lambda e, w=w: v.tensor_tensor(fold[:, :, 0:16], Wx2[:, :, 0:16],
                                                    gatB[:, w, :].unsqueeze(1).broadcast_to([128, 2, 16]), ALU.mult), t)
            t = V.do(lambda e, w=w: v.tensor_reduce(Wx2[:, :, 16 + 4 * w:20 + 4 * w],
                                                    fold[:, :, 0:16].rearrange("p k (h c) -> p k h c", c=4), X, ALU.add), t)
        folded = t

        bst = sb("bst", [128, T, 6])
        mv1 = sb("mv1", [128, T, 2])
        rs1 = sb("rs1", [128, T])
        mv2 = sb("mv2", [128, T, 2])
        rs2 = sb("rs2", [128, T])
        nb1 = sb("nb1", [128, T])
        nb2 = sb("nb2", [128, T])
        asall = sb("asall", [128, T, 8])
        l_h = [line(f"l_h{i}") for i in range(2)]

        def stat(get, mv, i, ready):
            t = V.do(lambda e: v.bn_stats(bst[:, i, :], get), ready)
            return V.do(lambda e: v.bn_aggr(mv[:, i, :], bst[:, i, :]), t)

        def rstd(mv, rs, nb, lo, hi, ready):
            r = A.do(lambda e: a.activation(rs[:, lo:hi], mv[:, lo:hi, 1], ACT.Sqrt, bias=epsc[:, :]), ready, consts)
            t = V.do(lambda e: v.reciprocal(rs[:, lo:hi], rs[:, lo:hi]), r)
            if nb is None:
                return t
            return V.do(lambda e: v.scalar_tensor_tensor(nb[:, lo:hi], mv[:, lo:hi, 0], -1.0, rs[:, lo:hi], ALU.mult, ALU.mult), t)

        fst = {"tT": {}, "tw": {}, "cp": {}, "hc": {}, "mm": {}}

        def features(q, Wx, keep_T, i, rs, nb, ready, n0):
            M = q.F + 2 * q.H
            s = i % 2
            tT, tw, cp, hcp, mm = (fst[k] for k in ("tT", "tw", "cp", "hc", "mm"))
            n = n0 + i
            va = A.do(lambda e: a.activation(xn[:, s, :], x_sb[:, i, :], ACT.Identity, scale=rs[:, i:i + 1], bias=nb[:, i:i + 1]),
                      ready, tT.get(n - 2))
            for k in range(2):
                tT[n] = P.do(lambda e, k=k: pe.transpose(pbank[s][:, k * 128:k * 128 + 128], xn[:, s, k * 128:k * 128 + 128],
                                                         ident[:, :]), va, cp.get(n - 2, free[s]))
            dst = xT[:, i, 0:256].rearrange("p (k n) -> p k n", k=2) if keep_T else xTb[:, s, :, :]
            cp[n] = V.do(lambda e: v.tensor_copy(dst, pbank[s][:, 0:256].rearrange("p (k n) -> p k n", k=2)), tT[n], mm.get(n - 2))
            for k in range(2):
                mm[n] = P.do(lambda e, k=k: pe.matmul(pbank[2 + s][:, 0:M], dst[:, k, :], Wx[:, k, :], start=k == 0,
                                                      stop=k == 1), cp[n], folded, tw.get(n - 2, free[2 + s]))
            hc = A.do(lambda e: a.copy(hrow[:, s, 0:q.R], pbank[2 + s][:, 0:q.R]), mm[n], hcp.get(n - 2))
            if keep_T:
                V.do(lambda e: v.tensor_copy(acc2[:, i, :], pbank[2 + s][:, 0:q.R]), hc)
            else:
                V.do(lambda e: v.tensor_copy(asall[:, i, 0:q.H], pbank[2 + s][:, q.F:q.R]), hc)
            tw[n] = V.do(lambda e: v.tensor_copy(q.tab[:, 2 * q.H * i:2 * q.H * i + q.H], pbank[2 + s][:, q.R:q.R + q.H]))
            hcp[n] = S.dma(lambda e: e.dma_start(q.table[128 * i:128 * i + 128, :], hrow[:, s, 0:q.R]), l_h[s], hc)
            q.table_in = [hcp[n], hcp.get(n - 1)]
            return tw[n]

        def peaks(q, last, index):
            H = q.H
            b = 4
            t = V.do(lambda e: v.tensor_reduce(small[:, 0:H], asall[:, :, 0:H].rearrange("p t h -> p h t"), X, ALU.max), last)
            t = V.do(lambda e: v.tensor_reduce(small[:, H:2 * H], asall[:, :, 0:H].rearrange("p t h -> p h t"), X, ALU.min), t)
            t = V.do(lambda e: v.tensor_scalar(small[:, H:2 * H], small[:, H:2 * H], -1.0, None, ALU.mult), t)
            t = P.do(lambda e: pe.transpose(pbank[b][0:2 * H, 0:128], small[:, 0:2 * H], ident[:, :]), t, free[b])
            t = V.do(lambda e: v.tensor_reduce(small[0:2 * H, 16:17], pbank[b][0:2 * H, 0:128], X, ALU.max), t)
            t = V.do(lambda e: v.tensor_scalar(small[0:2 * H, 0:2 * H], ident[0:2 * H, 0:2 * H], small[0:2 * H, 16:17], None,
                                               ALU.mult), t)
            t = P.do(lambda e: pe.matmul(pbank[b][:, 128:128 + 2 * H], ones[0:2 * H, :], small[0:2 * H, 0:2 * H], start=True,
                                         stop=True), t)
            peak = t = V.do(lambda e: v.tensor_copy(q.peak[:, :], pbank[b][:, 128:128 + 2 * H]), t)
            t = V.do(lambda e: v.tensor_tensor(q.flagrow[:, 0:H], q.peak[0:1, 0:H], q.peak[0:1, H:2 * H], ALU.add), t)
            t = V.do(lambda e: v.tensor_reduce(small[0:1, 20:21], q.flagrow[:, 0:H], X, ALU.max), t)
            t = V.do(lambda e: v.tensor_scalar(flags[0:1, index:index + 1], small[0:1, 20:21], SPREAD, None, ALU.is_gt), t)
            free[b] = t
            return peak, t

        def shift_table(q, ready, own):
            H = q.H
            tabv = q.tab[:, 0:T * 2 * H].rearrange("p (t w) -> p t w", t=T)
            peak, flag = peaks(q, ready, q.n)
            t = V.do(lambda e: v.tensor_copy(tabv[:, :, H:2 * H], q.peak[:, 0:H].unsqueeze(1).broadcast_to([128, T, H])), flag)
            t = V.do(lambda e: v.memset(q.tab[:, T * 2 * H:(T + 1) * 2 * H], 0.0), t)
            q.pending = (flag, own)
            return t

        def finish_shift(q):
            H = q.H
            tabv = q.tab[:, 0:T * 2 * H].rearrange("p (t w) -> p t w", t=T)
            t = V.do(lambda e: v.tensor_tensor(tabv[:, :, H:2 * H], tabv[:, :, H:2 * H], tabv[:, :, 0:H], ALU.add),
                     (V.sem, V.count))
            return V.do(lambda e: v.scalar_tensor_tensor(tabv[:, :, H:2 * H], tabv[:, :, H:2 * H], 0.2,
                                                         tabv[:, :, H:2 * H], ALU.mult, ALU.max), t)

        xs = {n: sem("x_" + n) for n in ("v", "p", "z", "m", "go_p", "end_p")}

        def true_peaks(q, ready):
            H, R = q.H, q.R
            flag, own = q.pending
            xd, xr = Sb[:, 0, 1, 0:1], Sb[:, 0, 1, 8:8 + H]
            rows = (big if q.n == 1 else early)[:, 0:q.NCH * H].rearrange("p (c h) -> p c h", h=H)
            Z = Sb[:, 1, 0, :]
            ZH = STb[:, :, :, :].rearrange("p s c n -> p (s c n)")[:, 0:H * 128].rearrange("p (h n) -> p h n", n=128)
            red = small[:, 0:H]
            tabv = q.tab[:, 0:T * 2 * H].rearrange("p (t w) -> p t w", t=T)
            W = queues(f"w{q.n}")
            l_ta, l_tg = line(f"l_ta{q.n}"), line(f"l_tg{q.n}")
            W[4].dma(lambda e: e.dma_start(q.asrc.rearrange("(t p) h -> p t h", p=128), asall[:, :, 0:H]), l_ta)
            for c in range(q.NCH):
                W[3].dma(lambda e, c=c: e.indirect_dma_start(
                    out=rows[:, c, :], out_offset=None, in_=q.asrc,
                    in_offset=bass.IndirectOffsetOnAxis(ap=q.idx[:, c:c + 1], axis=0)), l_tg, l_ta.now())
            when(q.n, ready, W, [l_ta, l_tg])

            def enter(eng):
                reg = eng.alloc_register(f"xf{q.n}")
                eng.load([reg], flags[0:1, q.n:q.n + 1])
                return reg

            def on_v(eng):
                reg = enter(eng)
                rt = eng.alloc_register(f"xt{q.n}")
                with eng.If_ne(reg, 0):
                    if own:
                        v.tensor_copy(tabv[:, :, H:2 * H], asall[:, :, 0:H]).then_inc(xs["m"], 1)
                    else:
                        v.memset(q.tab[:, :].rearrange("p (t w) -> p t w", w=2 * H)[:, :, H:2 * H], -1e30).then_inc(xs["m"], 1)
                    eng.wait_ge(xs["m"], 1)
                    eng.sem_clear(xs["m"])
                    with eng.Fori(0, q.NCH) as i:
                        iv = eng.snap(i, min_val=0, max_val=q.NCH - 1)
                        v.tensor_copy(xr, rows[:, bass.ds(iv, 1), :].rearrange("p c h -> p (c h)")).then_inc(xs["v"], 1)
                        v.tensor_copy(xd, q.dl[:, bass.ds(iv, 1)]).then_inc(xs["v"], 1)
                        eng.wait_ge(xs["v"], 2)
                        v.tensor_scalar(Z, iota[:, :], xd, None, ALU.is_equal).then_inc(xs["v"], 1)
                        eng.wait_ge(xs["v"], 3)
                        v.tensor_scalar(Z, Z, -1.0, 1e30, ALU.add, ALU.mult).then_inc(xs["v"], 1)
                        eng.wait_ge(xs["v"], 4)
                        v.tensor_tensor(ZH, Z.unsqueeze(1).broadcast_to([128, H, 128]),
                                        xr.unsqueeze(2).broadcast_to([128, H, 128]), ALU.add).then_inc(xs["v"], 1)
                        eng.wait_ge(xs["p"], H)
                        for w in range(H // 4):
                            v.tensor_reduce(red[:, 4 * w:4 * w + 4], pbank[w][:, :].rearrange("p (h n) -> p h n", n=128), X,
                                            ALU.max).then_inc(xs["z"], 1)
                        eng.wait_ge(xs["z"], H // 4)
                        eng.load([rt], q.tm[0:1, bass.ds(iv + q.K * 128, 1)])
                        o = q.tab[:, bass.ds(eng.snap(rt, min_val=0, max_val=T * 2 * H) + H, H)]
                        v.tensor_tensor(o, o, red, ALU.max).then_inc(xs["m"], 1)
                        eng.wait_ge(xs["m"], 1)
                        eng.wait_ge(xs["end_p"], 1)
                        for n in ("v", "p", "z", "m", "end_p"):
                            eng.sem_clear(xs[n])
                        eng.sem_inc(xs["go_p"], 1)
                eng.free_register(rt)
                eng.free_register(reg)

            def on_p(eng):
                reg = enter(eng)
                with eng.If_ne(reg, 0):
                    with eng.Fori(0, q.NCH) as i:
                        eng.wait_ge(xs["v"], 5)
                        for h in range(H):
                            pe.transpose(pbank[h // 4][:, 128 * (h % 4):128 * (h % 4) + 128], ZH[:, h, :],
                                         ident[:, :]).then_inc(xs["p"], 1)
                        eng.wait_ge(xs["p"], H)
                        eng.sem_inc(xs["end_p"], 1)
                        eng.wait_ge(xs["go_p"], 1)
                        eng.sem_clear(xs["go_p"])
                eng.free_register(reg)

            V.items.append(on_v)
            P.items.append(on_p)

        for q in (g1, g2):
            q.peak = sb(f"peak{q.n}", [128, 2 * q.H])

        Gb = sb("Gb", [128, NSL, CH, g1.R])
        Sb = sb("Sb", [128, NSL, CH, 128])
        STb = sb("STb", [128, 2, CH, 128])
        zb = sb("zb", [128, NSL, CH, 8])
        zc = sb("zc", [128, NSL, CH, 8])

        t = x_in
        for i in range(T):
            t = stat(x_sb[:, i, :], mv1, i, x_in)
        st1 = rstd(mv1, rs1, nb1, 0, T, t)
        for i in range(T):
            last = features(g1, Wx1, False, i, rs1, nb1, st1, 0)
        when(0, flag1, U, [l_fu, l_su, l_ru] + endu)
        tab1 = shift_table(g1, last, False)

        K1 = g1.K
        t = V.do(lambda e: v.tensor_scalar(t128[:, 0:K1], tcn[:, 0:K1], -128.0, None, ALU.mult), blocks_in)
        dF, sF, ok = tmp(3, f32, 896), tmp(4, f32, 896), tmp(5, f32, 896)
        dF3, sF3, ok3 = (z.rearrange("p (k n) -> p k n", n=128) for z in (dF, sF, ok))
        for k in range(K1):
            t = V.do(lambda e, k=k: v.tensor_scalar(dF3[:, k, :], R1D[:, k, :], t128[:, k:k + 1], None, ALU.add), t)
        t = V.do(lambda e: v.tensor_scalar(ok, dF, 0.0, None, ALU.is_ge), t)
        t = V.do(lambda e: v.scalar_tensor_tensor(ok, dF, 128.0, ok, ALU.is_lt, ALU.mult), t)
        t = V.do(lambda e: v.tensor_scalar(sF, tmp(6, i32, 896), float(N - 1), None, ALU.min), t)
        t = V.do(lambda e: v.scalar_tensor_tensor(sF, sF, float(-N), ok, ALU.add, ALU.mult), t)
        t = V.do(lambda e: v.tensor_scalar(sF, sF, float(N), None, ALU.add), t)
        for b, w, z in ((5, 0, sF3), (6, 1, dF3)):
            for k0 in (0, 4):
                kn = min(4, K1 - k0)
                for k in range(kn):
                    pt = P.do(lambda e, b=b, z=z, k=k, k0=k0: pe.transpose(pbank[b][:, k * 128:k * 128 + 128], z[:, k0 + k, :],
                                                                           ident[:, :]), t, free[b])
                n = min(g1.NCH - k0 * 128, kn * 128)
                dst = (g1.idx if w == 0 else g1.dl)[:, k0 * 128:k0 * 128 + n]
                free[b] = V.do(lambda e, b=b, dst=dst, n=n: v.tensor_copy(dst, pbank[b][:, 0:n]), pt)
        ready1 = free[6]
        true_peaks(g1, g1.pending[0])
        tab1 = finish_shift(g1)
        zero1 = V.do(lambda e: v.memset(big[:, :], 0.0), ready1)
        g1.tab_in = tab1

        def edge_pass(q, accf, Gt, lg, start, idx_in, dl_in, banks, fill, lo, hi, Q, tag):
            V, A, P, G, S = Q
            H, C, R, F = q.H, q.C, q.R, q.F
            bT, bD, bA = banks
            zt = [zb[:, s, :, 0:H] for s in range(NSL)]
            ar = [zc[:, s, :, 0:H] for s in range(NSL)]
            gat, sd, trp, stc, adg, z3, wex, msg, agg, add, sm = ({} for _ in range(11))
            regs = {}

            def alloc(e, nm):
                regs[nm] = [e.alloc_register(f"{nm}{tag}_{k}") for k in range(8 if nm == "dvr" else 4)]

            def rel(e, nm):
                for r in regs[nm]:
                    e.free_register(r)

            P.raw(lambda e: alloc(e, "per"))
            V.raw(lambda e: alloc(e, "dvr"))

            def g_gather(i):
                s = i % NSL
                for k in range(CH):
                    c = i * CH + k
                    gat[i] = G.dma(lambda e, k=k, s=s, c=c: e.indirect_dma_start(
                        out=Gt[s][:, k, :], out_offset=None, in_=q.table,
                        in_offset=bass.IndirectOffsetOnAxis(ap=q.idx[:, c:c + 1], axis=0)),
                        lg[s], agg.get(i - NSL), idx_in, *q.table_in)

            def v_onehot(i):
                s = i % NSL
                sd[i] = V.do(lambda e: v.tensor_tensor(Sb[:, s, :, :], iota[:, :].unsqueeze(1).broadcast_to([128, CH, 128]),
                                                       q.dl[:, i * CH:i * CH + CH].unsqueeze(2).broadcast_to([128, CH, 128]),
                                                       ALU.is_equal), agg.get(i - NSL), dl_in)

            def p_transpose(i):
                s = i % NSL
                for k in range(CH):
                    trp[i] = P.do(lambda e, k=k: pe.transpose(pbank[bT][:, k * 128:k * 128 + 128], Sb[:, s, k, :], ident[:, :]),
                                  sd[i], stc.get(i - 1, free[bT]))

            def a_stcopy(i):
                s = i % 2
                stc[i] = A.do(lambda e: a.copy(STb[:, s, :, :].rearrange("p c n -> p (c n)"), pbank[bT][:, :]), trp[i],
                              adg.get(i - 2))

            def p_adst(i):
                s = i % 2
                P.raw(lambda e: e.load(regs["per"], q.tm[0:1, q.K * 128 + i * CH:q.K * 128 + i * CH + CH]), *q.tm_in)
                for k in range(CH):
                    adg[i] = P.do(lambda e, k=k: pe.matmul(
                        pbank[bD][:, k * 16:k * 16 + 2 * H], STb[:, s, k, :],
                        q.tab[:, bass.ds(e.snap(regs["per"][k], min_val=0, max_val=T * 2 * H), 2 * H)], start=True, stop=True),
                        stc[i], q.tab_in, z3.get(i - 1, free[bD]))

            def v_score(i):
                s = i % NSL
                pv = pbank[bD][:, 0:64].rearrange("p (c w) -> p c w", w=16)
                t = V.do(lambda e: v.tensor_tensor(ar[s], Gt[s][:, :, F:R], pv[:, :, 0:H], ALU.add), adg[i], gat[i])
                t = V.do(lambda e: v.scalar_tensor_tensor(ar[s], ar[s], 0.2, ar[s], ALU.mult, ALU.max), t)
                z3[i] = V.do(lambda e: v.tensor_tensor(zt[s], ar[s], pv[:, :, H:2 * H], ALU.subtract), t, wex.get(i - NSL))

            def a_exp(i):
                s = i % NSL
                wex[i] = A.do(lambda e: a.activation(Gt[s][:, :, F:R], zt[s], ACT.Exp), z3[i])

            def v_message(c):
                i, k = divmod(c, CH)
                s = i % NSL
                hv = Gt[s][:, k, 0:F].rearrange("p (h c) -> p h c", c=C)
                msg[c] = V.do(lambda e: v.tensor_tensor(hv, hv, Gt[s][:, k, F:R].unsqueeze(2).broadcast_to([128, H, C]),
                                                        ALU.mult), wex[i])

            def p_sum(c):
                i, k = divmod(c, CH)
                s, b = i % NSL, bA[c % len(bA)]
                agg[i] = sm[c] = P.do(lambda e: pe.matmul(pbank[b][:, 0:R], Sb[:, s, k, :], Gt[s][:, k, :], start=True, stop=True),
                                      msg[c], add.get(c - len(bA), free[b]))

            def v_add(c):
                i, k = divmod(c, CH)
                b, rg = bA[c % len(bA)], 4 * (i % 2)
                if k == 0:
                    V.raw(lambda e: e.load(regs["dvr"][rg:rg + 4], q.tm[0:1, c:c + CH]), *q.tm_in)

                def f(e):
                    o = accf[:, bass.ds(e.snap(regs["dvr"][rg + k], min_val=0, max_val=T * R), R)]
                    return v.tensor_tensor(o, o, pbank[b][:, 0:R], ALU.add)
                add[c] = V.do(f, sm[c], add.get(c - 1, start))

            LAG = len(bA) - 1
            for i in range(lo, hi + 2):
                if i < hi:
                    g_gather(i)
                    v_onehot(i)
                    p_transpose(i)
                    a_stcopy(i)
                if lo + 1 <= i < hi + 1:
                    v_score(i - 1)
                    a_exp(i - 1)
                if i < hi:
                    p_adst(i)
                for k in range(CH):
                    c = (i - 2) * CH + k
                    if lo * CH <= c < hi * CH:
                        v_message(c)
                        p_sum(c)
                    if c - LAG >= lo * CH:
                        v_add(c - LAG)
                    if fill:
                        fill(i)
            for c in range(hi * CH - LAG, hi * CH):
                v_add(c)
            P.raw(lambda e: rel(e, "per"))
            V.raw(lambda e: rel(e, "dvr"))
            end = add[hi * CH - 1]
            free[bT], free[bD] = stc[hi - 1], z3[hi - 1]
            for b in bA:
                free[b] = end
            return end

        J2, NC2 = g2.J, g2.NCH
        XP = 512
        JP = J2 - XP
        x_free = last
        src2, dst2 = g2.idx[:, 0:1024].bitcast(i32), xtmp(1, i32)
        bI2, bF2, sc2, pos2, mask2 = xtmp(2, i32), xtmp(3, f32), xtmp(4, f32), xtmp(5, f32), xtmp(6, i32)
        Bv = [x_f[:, 7168 + 544 * n:7168 + 544 * n + 544].bitcast(f16)[:, 0:NC2] for n in range(3)]
        Av = [x_f[:, 9216 + 128 * n:9216 + 128 * n + 128].bitcast(f16).rearrange("p (w n) -> p w n", w=2) for n in range(3)]
        NB = 3
        hiF, loF, laneF, winF = bF2, sc2, pos2, xtmp(0, f32)
        addr2 = g2.dl[:, 0:1024].bitcast(i32)
        l_f2, l_s2, l_r2 = line("l_f2"), line("l_s2"), line("l_r2")
        S.dma(lambda e: e.dma_start(src2, ei_d[0, :].rearrange("(p j) -> p j", j=J2)), l_e2, x_free)
        S.dma(lambda e: e.dma_start(dst2, ei_d[1, :].rearrange("(p j) -> p j", j=J2)), l_e2)
        edges2 = l_e2.now()
        st = {}

        def sort2():
            zf = xtmp(10, i32, NC2)
            t = V.do(lambda e: v.memset(zf, 0), x_free)
            S.dma(lambda e: e.dma_start(slots2.rearrange("(p c) o -> p (c o)", p=128), zf), l_f2, t)
            gen = tiles_of(V, dst2, bI2, bF2, sc2, edges2)
            for n, t in enumerate(gen):
                if n % 2:
                    yield
            t = totals(V, P, t, (5, 6))
            t = padded_chunks(V, g2.cum[:, :], t)
            t = offsets(V, g2.cum[:, :], t)
            free[5] = free[6] = t
            yield
            t, tmi, _ = tile_map(g2, V, S, "2", t)
            g2.tm_in = [tmi]
            yield
            for n, gi in enumerate(SECT[:-1]):
                st["tails"] = t = V.do(lambda e, n=n, gi=gi: v.tensor_scalar(flags[0:1, 4 + n:5 + n], g2.cum[0:1, T - 1:T],
                                                                             float(CH * gi), None, ALU.is_gt), t)
            for t in ranks(V, g2, bF2, mask2, sc2, pos2, t):
                yield
            t = V.do(lambda e: v.tensor_scalar(dst2, dst2, 127, None, ALU.bitwise_and), t)
            t = V.do(lambda e: v.tensor_scalar(dst2, dst2, -1.0, 128.0, ALU.mult, ALU.add), t)
            t = V.do(lambda e: v.tensor_scalar(src2, src2, float(N - 1), None, ALU.min), t)
            yield
            t = V.do(lambda e: v.tensor_scalar(src2, src2, -1.0, float(N), ALU.mult, ALU.add), t)
            t = V.do(lambda e: v.scalar_tensor_tensor(src2, dst2, 8192.0, src2, ALU.mult, ALU.add), t)
            yield
            t = V.do(lambda e: v.tensor_copy(bI2, pos2), t)
            t = V.do(lambda e: v.tensor_scalar(mask2, bI2, 127, None, ALU.bitwise_and), t)
            t = V.do(lambda e: v.tensor_scalar(bI2, bI2, 7, None, ALU.logical_shift_right), t)
            yield
            st["addr"] = t = V.do(lambda e: v.scalar_tensor_tensor(addr2, mask2, float(NC2), bI2, ALU.mult, ALU.add), t)
            t = V.do(lambda e: v.tensor_copy(laneF, mask2), t)
            t = V.do(lambda e: v.tensor_copy(winF, bI2), t)
            yield
            t = V.do(lambda e: v.tensor_scalar(mask2, src2, 10, None, ALU.logical_shift_right), t)
            t = V.do(lambda e: v.tensor_copy(hiF, mask2), t)
            t = V.do(lambda e: v.tensor_scalar(mask2, src2, 1023, None, ALU.bitwise_and), t)
            st["loF"] = t = V.do(lambda e: v.tensor_scalar(loF, mask2, 1.0 / 1024, None, ALU.mult), t)
            yield
            used = {}
            segs = [(5, 0, 512), (6, 512, 1024), (7, 1024, NC2)]
            for j in range(JP):
                n = j % NB
                ta = V.do(lambda e, j=j, n=n: v.tensor_scalar(Bv[n], iota16[:, :], winF[:, j:j + 1], None, ALU.is_equal), t,
                          used.get(j - NB))
                V.do(lambda e, j=j, n=n: v.tensor_scalar(Av[n][:, 0, :], iota16[:, 0:128], laneF[:, j:j + 1], hiF[:, j:j + 1],
                                                         ALU.is_equal, ALU.mult))
                ta = V.do(lambda e, j=j, n=n: v.tensor_scalar(Av[n][:, 1, :], iota16[:, 0:128], laneF[:, j:j + 1],
                                                              loF[:, j:j + 1], ALU.is_equal, ALU.mult))
                for w in range(2):
                    for b, c0, c1 in segs:
                        used[j] = P.do(lambda e, w=w, b=b, c0=c0, c1=c1, n=n, j=j: pe.matmul(
                            pbank[b][:, 0:c1 - c0], Av[n][:, w, :], Bv[n][:, c0:c1], start=(j == 0 and w == 0),
                            stop=(j == JP - 1 and w == 1)), ta, free[b] if j == 0 else None)
                yield
            for b in (5, 6, 7):
                free[b] = used[JP - 1]
            st["sorted"] = used[JP - 1]

        SECT = list(range(204, g2.NCH // CH, 8)) + [g2.NCH // CH]

        scat = {"j": JP}

        def scatter2(n):
            for _ in range(n):
                j = scat["j"]
                if j >= J2:
                    return
                scat["j"] += 1
                G.dma(lambda e, j=j: e.indirect_dma_start(
                    out=slots2, out_offset=bass.IndirectOffsetOnAxis(ap=addr2.bitcast(u32)[:, j:j + 1], axis=0),
                    in_=src2[:, j:j + 1], in_offset=None, bounds_check=BLK * NC2 - 1, oob_is_err=False),
                    l_s2, st["addr"], l_f2.now())

        filler = sort2()
        state = {"done": False}
        NG1 = g1.NCH // CH

        def fill1(i):
            if not state["done"]:
                try:
                    next(filler)
                except StopIteration:
                    state["done"] = True
            if "addr" in st:
                st["n"] = st.get("n", 0) + 1
                if st["n"] > 24 and st["n"] % 4 == 0:
                    scatter2(1)

        lg1 = [line(f"l_g{i}") for i in range(NSL)]
        Gt1 = [Gb[:, s, :, :] for s in range(NSL)]
        done1 = edge_pass(g1, big, Gt1, lg1, zero1, ready1, ready1, (0, 1, (2, 3, 4)), fill1, 0, NG1, main, "a")
        for _ in filler:
            pass
        scatter2(J2)
        xin2 = {}
        t = V.do(lambda e: v.memset(x_sb[:, T - 1, :], 0.0), st["sorted"])
        l_x2s = [line(f"l_x2_{k}") for k in range(5)]
        for k in range(4):
            xin2[k] = S.dma(lambda e, k=k: e.dma_start(x_sb[:, 12 * k:12 * k + 12, :], xv[:, 12 * k:12 * k + 12, :]), l_x2s[k],
                            st["sorted"], st["loF"], l_f2.now())
        xin2[4] = S.dma(lambda e: e.dma_start(x_sb[0:N - 48 * 128, 48, :], x_d[48 * 128:N, :]), l_x2s[4], t)

        rec = sb("rec", [128, T, 8])
        t = V.do(lambda e: v.tensor_scalar(rec[:, :, :], acc1[:, 0:T, 256:264], 1e-16, None, ALU.add), done1)
        rect = V.do(lambda e: v.reciprocal(rec[:, :, :], rec[:, :, :]), t)
        ue, us, sta = {}, {}, {}

        def fin_a(i):
            s = i % 2
            u = acc1[:, i, 0:256]
            uh = u.rearrange("p (h c) -> p h c", c=32)
            xa = A.do(lambda e: a.activation(xn[:, s, :], x_sb[:, i, :], ACT.Identity, scale=rs1[:, i:i + 1], bias=nb1[:, i:i + 1]),
                      xin2[i // 12], ue.get(i - 2))
            t1 = V.do(lambda e: v.tensor_tensor(uh, uh, rec[:, i, :].unsqueeze(2).broadcast_to([128, 8, 32]), ALU.mult), rect)
            t1 = V.do(lambda e: v.tensor_tensor(u, u, biasB, ALU.add), t1)
            t1 = V.do(lambda e: v.tensor_tensor(u, u, xn[:, s, :], ALU.add), t1, xa)
            ue[i] = A.do(lambda e: a.activation(fold[:, s, :], u, ACT.Exp), t1, us.get(i - 2))

        def fin_b(i):
            s = i % 2
            u = acc1[:, i, 0:256]
            t0 = V.do(lambda e: v.tensor_scalar(fold[:, s, :], fold[:, s, :], 1.0, -1.0, ALU.min, ALU.add), ue[i])
            us[i] = V.do(lambda e: v.scalar_tensor_tensor(u, u, 0.0, fold[:, s, :], ALU.max, ALU.add), t0)
            sta[i] = stat(u, mv2, i, us[i])

        for i in range(T + 1):
            if i < T:
                fin_a(i)
            if i:
                fin_b(i - 1)
        lnr = rstd(mv2, rs2, None, 0, T, sta[T - 1])
        mv3 = mv1
        rs3, nb3 = rs1, nb1
        BT = 13
        r3 = {}
        for i in range(T + BT):
            if i < T:
                u = acc1[:, i, 0:256]
                t = V.do(lambda e, i=i, u=u: v.tensor_scalar(u, u, mv2[:, i, 0:1], rs2[:, i:i + 1], ALU.subtract, ALU.mult), lnr)
                t = V.do(lambda e, u=u: v.tensor_tensor(u, u, lnsB, ALU.mult), t)
                t = V.do(lambda e, u=u: v.tensor_tensor(u, u, lnbB, ALU.add), t)
                t = V.do(lambda e, i=i, u=u: v.tensor_tensor(x_sb[:, i, :], x_sb[:, i, :], u, ALU.add), t)
                if i == T - 1:
                    t = V.do(lambda e: v.tensor_scalar(x_sb[:, T - 1, :], x_sb[:, T - 1, :], rmask[:, :], None, ALU.mult), t)
                t = stat(x_sb[:, i, :], mv3, i, t)
                if i % BT == BT - 1 or i == T - 1:
                    lo = i // BT * BT
                    r3[i // BT] = rstd(mv3, rs3, nb3, lo, i + 1, t)
            if i >= BT:
                last2 = features(g2, Wx2, True, i - BT, rs3, nb3, r3[(i - BT) // BT], 100)
        featdone = [last2, (P.sem, P.count), (A.sem, A.count), l_h[0].now(), l_h[1].now()]
        xTdone = (V.sem, V.count)

        rawS = idx1f[:, 0:NC2].bitcast(i32)
        rawP = Gb[:, :, :, :].rearrange("p s c r -> p (s c r)")[:, 0:NC2].bitcast(i32)
        raw2_in = S.dma(lambda e: e.dma_start(rawS, slots2.rearrange("(p c) o -> p (c o)", p=128)), l_r2, l_s2.now(), l_f2.now(),
                        done1)
        for b, c0, c1 in ((5, 0, 512), (6, 512, 1024), (7, 1024, NC2)):
            t = V.do(lambda e, b=b, c0=c0, c1=c1: v.tensor_scalar(rawP[:, c0:c1], pbank[b][:, 0:c1 - c0], 1024.0, None, ALU.mult),
                     st["sorted"], done1)
            free[b] = t
        t = V.do(lambda e: v.tensor_tensor(rawP, rawP, rawS, ALU.add), t, raw2_in)
        t2 = V.do(lambda e: v.tensor_scalar(rawS, rawP, 8191, None, ALU.bitwise_and), t)
        t = V.do(lambda e: v.tensor_scalar(rawP, rawP, 13, None, ALU.logical_shift_right), t)
        t2 = V.do(lambda e: v.tensor_scalar(g2.idx[:, :], rawS, -1.0, float(N), ALU.mult, ALU.add), t2)
        ready2 = V.do(lambda e: v.tensor_scalar(g2.dl[:, :], rawP, -1.0, 128.0, ALU.mult, ALU.add), t)

        t = V.do(lambda e: v.tensor_copy(asall[:, :, 0:4], acc2[:, 0:T, 16:20]), last2)
        shift_table(g2, t, True)
        true_peaks(g2, g2.pending[0])
        g2.tab_in = finish_shift(g2)
        g2.table_in = [*g2.table_in, g2.tab_in]
        tab2 = g2.tab[:, 0:T * 8].rearrange("p (t w) -> p t w", t=T)
        zo = small4[:, :].rearrange("p (t h) -> p t h", h=4)
        t = V.do(lambda e: v.tensor_tensor(zo, acc2[:, 0:T, 16:20], tab2[:, :, 0:4], ALU.add), g2.tab_in)
        t = V.do(lambda e: v.scalar_tensor_tensor(zo, zo, 0.2, zo, ALU.mult, ALU.max), t)
        t = V.do(lambda e: v.tensor_tensor(zo, zo, tab2[:, :, 4:8], ALU.subtract), t)
        t = A.do(lambda e: a.activation(acc2[:, 0:T, 16:20], zo, ACT.Exp), t)
        for h in range(4):
            tt = V.do(lambda e, h=h: v.tensor_tensor(acc2[:, 0:T, 4 * h:4 * h + 4], acc2[:, 0:T, 4 * h:4 * h + 4],
                                                     acc2[:, 0:T, 16 + h:17 + h].broadcast_to([128, T, 4]), ALU.mult), t)
        start2 = V.do(lambda e: v.memset(acc2[:, T, :], 0.0), tt)

        W1s = early[:, 0:2048].rearrange("p (w k f) -> p w k f", w=2, k=2)
        W2s = early[:, 2048:4096].rearrange("p (w f d) -> p w f d", w=2, f=4)
        Gt2 = [early[:, 4096 + 80 * s:4096 + 80 * s + 80].rearrange("p (c r) -> p c r", r=20) for s in range(NSL)]
        hh = Gb[:, :, :, :].rearrange("p s c r -> p (s c r)")[:, 0:4096].rearrange("p (s f n) -> p s f n", s=2, f=4)
        Yb = idx1f[:, 0:1536].rearrange("p (s t d) -> p s t d", s=3, t=2)
        l_w1 = [line(f"l_w1{i}") for i in range(2)]
        l_y = [line(f"l_y{i}") for i in range(3)]
        groups = [(4 * i, 4) for i in range(12)] + [(48, 1)]
        blk = [(ei, gi) for ei in range(4) for gi in range(13)]
        use1, use2, wl, gel, mm2 = {}, {}, {}, {}, {}
        ffn = {"n1": 0, "n2": 0, "ny": 0}

        def wload(ei):
            s = ei % 2
            S.dma(lambda e: e.dma_start(W1s[:, s, :, :], W1_d[ei].rearrange("(k p) f -> p k f", p=128)), l_w1[s],
                  use1.get(ei - 2), g2.tab_in, *featdone)
            wl[ei] = S.dma(lambda e: e.dma_start(W2s[:, s, :, :], W2_d[ei].rearrange("(f p) d -> p f d", p=128)), l_w1[s],
                           use2.get(ei - 2))

        def up(bi):
            ei, gi = blk[bi]
            t0, nt = groups[gi]
            s, w = bi % 2, ei % 2
            for f in range(4):
                b = 5 + ffn["n1"] % 2
                ffn["n1"] += 1
                for k in range(2):
                    p = P.do(lambda e, k=k, f=f, b=b: pe.matmul(
                        pbank[b][:, 0:nt * 128], W1s[:, w, k, f * 128:f * 128 + 128],
                        xT[:, t0:t0 + nt, k * 128:k * 128 + 128], start=k == 0, stop=k == 1), wl[ei], free[b], xTdone)
                    if nt == 4 and k == 0:
                        yield
                gel[(bi, f)] = free[b] = A.do(lambda e, f=f, b=b: a.activation(hh[:, s, f, 0:nt * 128], pbank[b][:, 0:nt * 128],
                                                                               ACT.Gelu, bias=b1c[:, ei, f:f + 1]),
                                              p, mm2.get(bi - 2), start2)
                use1[ei] = p
                yield

        yslot = {}

        def down(bi):
            ei, gi = blk[bi]
            t0, nt = groups[gi]
            s, w = bi % 2, ei % 2
            for j in range(nt):
                ti = t0 + j
                b = (4, 7)[ffn["n2"] % 2]
                ffn["n2"] += 1
                for f in range(4):
                    p = P.do(lambda e, f=f, b=b, j=j: pe.matmul(pbank[b][:, 0:D], hh[:, s, f, j * 128:j * 128 + 128],
                                                                W2s[:, w, f, :], start=f == 0, stop=f == 3),
                             gel[(bi, f)], free[b])
                mm2[bi] = use2[ei] = p
                sl = ffn["ny"] % 3
                free[b] = V.do(lambda e, b=b, sl=sl, j=j: v.tensor_tensor(Yb[:, sl, j % 2, :], pbank[b][:, 0:D], b2B[:, ei, :],
                                                                          ALU.add), p, yslot.get(sl))
                if j % 2 or nt == 1:
                    n = 1 if nt == 1 else 2
                    yslot[sl] = S.dma(lambda e, sl=sl, ti=ti, n=n: e.dma_start(
                        Y_d[(ti - n + 1) * 128:(ti + 1) * 128, ei, :].rearrange("(t p) d -> p t d", p=128), Yb[:, sl, 0:n, :]),
                        l_y[sl], free[b])
                    ffn["ny"] += 1
                yield

        def experts():
            wload(0)
            wload(1)
            yield from up(0)
            for bi in range(len(blk)):
                gens = [up(bi + 1)] if bi + 1 < len(blk) else []
                gens.append(down(bi))
                while gens:
                    for gn in list(gens):
                        try:
                            next(gn)
                            yield
                        except StopIteration:
                            gens.remove(gn)
                if blk[bi][1] == 12 and blk[bi][0] + 2 < 4:
                    wload(blk[bi][0] + 2)

        fgen = experts()
        fst2 = {"n": 0, "done": False}

        def fill2(i):
            fst2["n"] += 1
            if not fst2["done"]:
                try:
                    next(fgen)
                except StopIteration:
                    fst2["done"] = True

        for _ in range(PRE2):
            fill2(0)
        lg2 = [line(f"l_gg{i}") for i in range(NSL)]
        done2 = edge_pass(g2, acc2f, Gt2, lg2, start2, ready2, ready2, (0, 1, (2, 3)), fill2, 0, SECT[0], main, "b")
        for _ in fgen:
            pass
        Z = queues("z")
        lgz = [line(f"l_gz{i}") for i in range(NSL)]
        for n in range(len(SECT) - 1):
            kept = list(free)
            edge_pass(g2, acc2f, Gt2, lgz, done2, ready2, ready2, (0, 1, (2, 3)), None, SECT[n], SECT[n + 1], Z, f"z{n}")
            free[:] = kept
            when(4 + n, st["tails"], Z, lgz)
        done2 = (V.sem, V.count)

        late = STb[:, :, :, :].rearrange("p s c n -> p (s c n)")
        late2 = Sb[:, :, :, :].rearrange("p s c n -> p (s c n)")
        hk = late[:, 0:784].rearrange("p (t c) -> p t c", t=T)
        sq = late2[:, 0:784].rearrange("p (t c) -> p t c", t=T)
        sc4 = late2[:, 784:980].rearrange("p (t c) -> p t c", t=T)
        r1 = late2[:, 980:1176].rearrange("p (t c) -> p t c", t=T)
        gate = late2[:, 1176:1372].rearrange("p (t c) -> p t c", t=T)
        m1, ct = late2[:, 1372:1421], late2[:, 1421:1470]
        t = V.do(lambda e: v.tensor_scalar(r1, acc2[:, 0:T, 16:20], 1e-16, None, ALU.add), done2, (P.sem, P.count))
        t = V.do(lambda e: v.reciprocal(r1, r1), t)
        for h in range(4):
            tt = V.do(lambda e, h=h: v.tensor_tensor(hk[:, :, 4 * h:4 * h + 4], acc2[:, 0:T, 4 * h:4 * h + 4],
                                                     r1[:, :, h:h + 1].broadcast_to([128, T, 4]), ALU.mult), t)

        def bc16(ap):
            return ap.unsqueeze(1).broadcast_to([128, T, 16])

        def col(ap, n):
            return ap.unsqueeze(2).broadcast_to([128, T, n])

        t = V.do(lambda e: v.tensor_tensor(hk, hk, bc16(gB[:, 0, :]), ALU.add), tt)
        t = V.do(lambda e: v.tensor_reduce(m1, hk, X, ALU.add), t)
        t = V.do(lambda e: v.tensor_scalar(m1, m1, 1.0 / 16, None, ALU.mult), t)
        t = V.do(lambda e: v.tensor_tensor(hk, hk, col(m1, 16), ALU.subtract), t)
        t = V.do(lambda e: v.tensor_tensor(sq, hk, hk, ALU.mult), t)
        t = V.do(lambda e: v.tensor_reduce(ct, sq, X, ALU.add), t)
        t = A.do(lambda e: a.activation(ct, ct, ACT.Sqrt, scale=1.0 / 16, bias=epsc[:, :]), t)
        t = V.do(lambda e: v.reciprocal(ct, ct), t)
        t = V.do(lambda e: v.tensor_tensor(hk, hk, col(ct, 16), ALU.mult), t)
        t = V.do(lambda e: v.tensor_tensor(hk, hk, bc16(gB[:, 1, :]), ALU.mult), t)
        t = V.do(lambda e: v.tensor_tensor(hk, hk, bc16(gB[:, 2, :]), ALU.add), t)
        t = V.do(lambda e: v.tensor_tensor(sc4, hk[:, :, 0:4], hk[:, :, 4:8], ALU.add), t)
        t = V.do(lambda e: v.tensor_tensor(sc4, sc4, hk[:, :, 8:12], ALU.add), t)
        t = V.do(lambda e: v.tensor_tensor(sc4, sc4, hk[:, :, 12:16], ALU.add), t)
        t = V.do(lambda e: v.tensor_scalar(sc4, sc4, 0.25, None, ALU.mult), t)
        t = V.do(lambda e: v.tensor_reduce(m1, sc4, X, ALU.max), t)
        rank = sq[:, :, 0:4]
        t = V.do(lambda e: v.memset(rank, 0.0), t)
        for i in range(4):
            for j in range(4):
                if i == j:
                    continue
                op = ALU.is_ge if j < i else ALU.is_gt
                t = V.do(lambda e, i=i, j=j, op=op: v.tensor_tensor(ct, sc4[:, :, j], sc4[:, :, i], op), t)
                t = V.do(lambda e, i=i: v.tensor_tensor(sq[:, :, i], sq[:, :, i], ct, ALU.add), t)
        t = V.do(lambda e: v.tensor_scalar(rank, rank, 2.0, None, ALU.is_lt), t)
        t = V.do(lambda e: v.tensor_tensor(r1, sc4, col(m1, 4), ALU.subtract), t)
        t = A.do(lambda e: a.activation(r1, r1, ACT.Exp), t)
        t = V.do(lambda e: v.tensor_tensor(r1, r1, rank, ALU.mult), t)
        t = V.do(lambda e: v.tensor_reduce(ct, r1, X, ALU.add), t)
        t = V.do(lambda e: v.reciprocal(ct, ct), t)
        gated = V.do(lambda e: v.tensor_tensor(gate, r1, col(ct, 4), ALU.mult), t)

        NY = 6
        Yr = big[:, 0:NY * 2048].rearrange("p (s t e d) -> p s t e d", s=NY, t=2, e=4)
        l_yr = [line(f"l_yr{i}") for i in range(NY)]
        l_o = line("l_o")
        ffn_end = (P.sem, P.count)
        ydone = [z.now() for z in l_y]
        con = {}

        def yload(n):
            s = n % NY
            k = 1 if n == 24 else 2
            con[("in", n)] = S.dma(lambda e: e.dma_start(Yr[:, s, 0:k, :, :].rearrange("p t e d -> p t (e d)"),
                                                         Y_d[256 * n:256 * n + 128 * k, :, :].rearrange("(t p) e d -> p t (e d)", p=128)),
                                   l_yr[s], con.get(("out", n - NY)), ffn_end, *ydone)

        for n in range(NY):
            yload(n)
        for n in range(25):
            s = n % NY
            for j in range(1 if n == 24 else 2):
                ti = 2 * n + j
                t = None
                for ei in range(4):
                    t = V.do(lambda e, ti=ti, ei=ei, s=s, j=j: v.scalar_tensor_tensor(
                        x_sb[:, ti, :], Yr[:, s, j, ei, :], gate[:, ti, ei:ei + 1], x_sb[:, ti, :], ALU.mult, ALU.add),
                        con[("in", n)], gated, t)
            con[("out", n)] = t
            if n < 24:
                S.dma(lambda e, n=n: e.dma_start(out_d[n * 256:n * 256 + 256, :].rearrange("(t p) d -> p t d", p=128),
                                                 x_sb[:, 2 * n:2 * n + 2, :]), l_o, t)
            else:
                S.dma(lambda e: e.dma_start(out_d[48 * 128:N, :], x_sb[0:N - 48 * 128, 48, :]), l_o, t)
            if n + NY < 25:
                yload(n + NY)
        S.wait(l_o.now())

        block = ctx.enter_context(nc.Block())

        @block.sync
        def _(e):
            S.emit(e)

        @block.scalar
        def _(e):
            A.emit(e)

        @block.vector
        def _(e):
            V.emit(e)

        @block.tensor
        def _(e):
            P.emit(e)

        @block.gpsimd
        def _(e):
            G.emit(e)


_INS = ['x', 'src', 'dst', 'L0_gnn_W', 'L0_gnn_att_src', 'L0_gnn_att_dst', 'L0_gnn_bias', 'L0_gnn_ln_scale',
        'L0_gnn_ln_bias', 'L0_ffn_W_gat', 'L0_ffn_att_src', 'L0_ffn_att_dst', 'L0_ffn_b_gat', 'L0_ffn_ln_gamma',
        'L0_ffn_ln_beta', 'L0_ffn_W1', 'L0_ffn_b1', 'L0_ffn_W2', 'L0_ffn_b2', 'L0_ffn_edge_index']


def kernel(**inputs):
    import numpy as _np
    import concourse.bacc as _bacc
    from concourse import mybir as _mybir
    from concourse.bass_utils import run_bass_kernel_spmd as _run

    nc = _bacc.Bacc("TRN2", target_bir_lowering=False, num_devices=1)
    arrays, args = {}, []
    for name in _INS:
        a = _np.ascontiguousarray(inputs[name])
        arrays[f"in_{name}_dram"] = a
        args.append(nc.dram_tensor(f"in_{name}_dram", a.shape, _mybir.dt.from_np(a.dtype), kind="ExternalInput").ap())
    args.append(nc.dram_tensor("out_0_dram", (N, D), _mybir.dt.float32, kind="ExternalOutput").ap())
    build(nc, *args)
    r = _run(nc, [arrays], core_ids=[0])
    return r.results[0]["out_0_dram"]
```

```python
import concourse.bass as bass
from concourse import mybir
from contextlib import ExitStack

N = 6250
T = 49
NP = T * 128
D = 256
BLK = 128
CH = 4
NSL = 4
SPREAD = 16.0


class Queue:

    def __init__(self, name, sem):
        self.name, self.sem, self.count, self.items, self.seen = name, sem, 0, [], {}

    def wait(self, *tokens):
        for tok in tokens:
            if tok is None:
                continue
            sem, value = tok
            if self.seen.get(id(sem), 0) >= value:
                continue
            self.seen[id(sem)] = value
            self.items.append(lambda eng, sem=sem, value=value: eng.wait_ge(sem, value))

    def do(self, fn, *waits):
        self.wait(*waits)
        self.count += 1
        self.items.append(lambda eng, fn=fn: fn(eng).then_inc(self.sem, 1))
        return (self.sem, self.count)

    def raw(self, fn, *waits):
        self.wait(*waits)
        self.items.append(lambda eng, fn=fn: fn(eng))

    def dma(self, fn, line, *waits):
        self.wait(*waits)
        line.count += 16
        self.items.append(lambda eng, fn=fn, sem=line.sem: fn(eng).then_inc(sem, 16))
        return (line.sem, line.count)

    def emit(self, eng):
        for item in self.items:
            item(eng)


class Line:
    def __init__(self, sem):
        self.sem, self.count = sem, 0

    def now(self):
        return (self.sem, self.count)


def build(nc, x_d, src_d, dst_d, W_d, as_d, ad_d, bias_d, lns_d, lnb_d, Wg_d, gas_d, gad_d, bg_d, gam_d, bet_d,
          W1_d, b1_d, W2_d, b2_d, ei_d, out_d):
    f32, i32, u32, i16, f16, b16 = (mybir.dt.float32, mybir.dt.int32, mybir.dt.uint32, mybir.dt.int16, mybir.dt.float16,
                                     mybir.dt.bfloat16)
    ALU = mybir.AluOpType
    ACT = mybir.ActivationFunctionType
    X = mybir.AxisListType.X

    ctx = ExitStack()
    with ctx:
        def sb(name, shape, dt=f32):
            return ctx.enter_context(nc.sbuf_tensor(name, shape, dt))

        def pb(name, shape, dt=f32):
            return ctx.enter_context(nc.psum_tensor(name, shape, dt))

        def sem(name):
            return ctx.enter_context(nc.semaphore(name))

        lines, conditional = [], []

        def line(name):
            lines.append(Line(sem(name)))
            return lines[-1]

        def queues(tag):
            return tuple(Queue(n, sem(f"q_{n}{tag}")) for n in ("dve", "act", "pe", "pool", "sp"))

        V, A, P, G, S = main = queues("")
        v, a, g, pe = nc.vector, nc.scalar, nc.gpsimd, nc.tensor
        flags = sb("flags", [1, 16], i32)

        def when(index, ready, subs, ends):
            conditional.extend(ends)
            starts = [(q.sem, q.count) for q in main if q.count] + [ln.now() for ln in lines if ln.count and ln not in conditional]
            finals = [(q.sem, q.count) for q in subs if q.count] + [ln.now() for ln in ends if ln.count]
            for mq, sq in zip(main, subs):
                taken, sq.items = sq.items, []

                def item(eng, taken=taken, name=sq.name):
                    reg = eng.alloc_register(f"flag{index}_{name}")
                    eng.wait_ge(*ready)
                    eng.load([reg], flags[0:1, index:index + 1])
                    with eng.If_ne(reg, 0):
                        for st in starts:
                            eng.wait_ge(*st)
                        for it in taken:
                            it(eng)
                        for fi in finals:
                            eng.wait_ge(*fi)
                    eng.free_register(reg)
                mq.items.append(item)

        class Graph:
            pass

        g1, g2 = Graph(), Graph()
        g1.n, g1.E, g1.J, g1.H, g1.C = 1, 100000, 782, 8, 32
        g2.n, g2.E, g2.J, g2.H, g2.C = 2, 131072, 1024, 4, 4
        for q in (g1, g2):
            q.F = q.H * q.C
            q.R = q.F + q.H
            q.AR = q.R if q.n == 1 else 6 * q.H
            q.W = CH if q.n == 1 else 16
            q.NCH = -(-(-(-q.E // BLK) + T) // q.W) * q.W
            q.K = -(-q.NCH // BLK)
            q.table = nc.dram_tensor(f"table{q.n}", (NP, q.R), f32).ap()
            q.asrc = nc.dram_tensor(f"asrc{q.n}", (NP, q.H), f32).ap()
            q.tm_d = nc.dram_tensor(f"tm{q.n}", (2 * q.K * 128,), i16).ap()
            q.dl = sb(f"dl{q.n}", [128, q.NCH])
            q.dl16 = sb(f"dlh{q.n}", [128, q.NCH], f16)
            q.tab = sb(f"tab{q.n}", [128, (T + 1) * 2 * q.H])
            q.tm = sb(f"tmr{q.n}", [1, 2 * q.K * 128], i16)
            q.cum = sb(f"cum{q.n}", [128, T])
            q.flagrow = sb(f"fr{q.n}", [1, 8])
        idx1f = sb("idx1", [128, 1664])
        g1.idx = idx1f[:, 0:g1.NCH].bitcast(u32)
        g2.idx = sb("idx2", [128, g2.NCH], u32)
        slots1 = nc.dram_tensor("slots1", (g1.NCH * BLK, 2), i32).ap()
        slots2 = nc.dram_tensor("slots2", (g2.NCH * BLK, 1), i32).ap()
        rowS_d = nc.dram_tensor("rowS", (g1.J, BLK), i32).ap()
        rowD_d = nc.dram_tensor("rowD", (g1.J, BLK), i32).ap()
        Y_d = nc.dram_tensor("Y", (NP, 4, D), f32).ap()

        big = sb("big", [128, (T + 1) * g1.R])
        x_f = sb("x_sb", [128, T * D])
        x_sb = x_f[:, :].rearrange("p (t d) -> p t d", d=D)
        acc1 = big[:, :].rearrange("p (t r) -> p t r", r=g1.R)
        acc2f = sb("acc2", [128, (T + 1) * g2.AR])
        acc2 = acc2f[:, :].rearrange("p (t r) -> p t r", r=g2.AR)
        xT = acc1

        early = sb("early", [128, 4608])

        def part(lo, n, dt=f32):
            ap = early[:, lo:lo + n]
            return ap if dt == f32 else ap.bitcast(dt)

        Wt = part(0, 512).rearrange("p (k d) -> p k d", k=2)
        attB = part(512, 512).rearrange("p (k d) -> p k d", k=2)
        fold = part(1024, 512).rearrange("p (k d) -> p k d", k=2)
        xn = part(1536, 512).rearrange("p (k d) -> p k d", k=2)
        xTb = part(2048, 512).rearrange("p (s k n) -> p s k n", s=2, k=2)
        hrow = part(2560, 528).rearrange("p (s r) -> p s r", s=2)
        Wx1 = part(3088, 544).rearrange("p (k d) -> p k d", k=2)
        biasB, lnsB, lnbB = part(3632, 256), part(3888, 256), part(4144, 256)

        Wx2 = sb("Wx2", [128, 2, 24])
        gatB = sb("gatB", [128, 2, 16])
        gB = sb("gB", [128, 3, 16])
        b2B = sb("b2B", [128, 4, D])
        b1c = sb("b1c", [128, 4, 4])
        iota = sb("iota", [128, 128])
        ident = sb("ident", [128, 128])
        ident16 = sb("ident16", [128, 128], b16)
        tri = sb("tri", [128, 128])
        ones = sb("ones", [128, 128])
        pidx = sb("pidx", [128, 9])
        rmask = sb("rmask", [128, 1])
        epsc = sb("epsc", [128, 1])
        iota16 = sb("iota16", [128, g2.NCH], f16)
        cnt, tot, pre, nch, dd, off, junk = (sb(n, [128, T]) for n in ("cnt", "tot", "pre", "nch", "dd", "off", "junk"))
        nchi = sb("nchi", [128, T], i32)
        tcn = sb("tcn", [128, 9])
        t128 = sb("t128", [128, 9])
        tci = sb("tci", [128, 2, 9], i16)
        pair = sb("pair", [128, 9])
        pairu = sb("pairu", [128, 9], u32)
        small = sb("small", [128, 32])
        small4 = sb("small4", [128, 4 * T])
        PRE2 = 24
        PACE = 645

        pbank = [pb(f"pb{i}", [128, 512]) for i in range(8)]
        free = [None] * 8

        l_x, l_w, l_e1, l_e2 = (line(n) for n in ("l_x", "l_w", "l_e1", "l_e2"))

        def tmp(i, dt, n=1024):
            ap = big[:, i * 1024:i * 1024 + n]
            return ap.bitcast(dt) if dt != f32 else ap

        def xtmp(i, dt, n=1024):
            ap = x_f[:, i * 1024:i * 1024 + n]
            return ap.bitcast(dt) if dt != f32 else ap

        src1, dst1, nxt1 = tmp(0, i32, 782), tmp(1, i32, 782), tmp(2, i32, 782)
        V.do(lambda e: v.memset(tmp(0, i32), 0))
        V.do(lambda e: v.memset(tmp(1, i32), 8191))
        t = V.do(lambda e: v.memset(tmp(2, i32), 8191))
        J1 = g1.J
        for buf, ap, o in ((src1, src_d, 0), (dst1, dst_d, 0), (nxt1, dst_d, 1)):
            S.dma(lambda e, buf=buf, ap=ap, o=o: e.dma_start(
                buf[0:127, :], ap[o:o + 127 * J1].rearrange("(p j) -> p j", j=J1)), l_e1, t)
            n = g1.E - 127 * J1 - o
            S.dma(lambda e, buf=buf, ap=ap, o=o, n=n: e.dma_start(
                buf[127:128, 0:n], ap[o + 127 * J1:g1.E].rearrange("(p j) -> p j", p=1)), l_e1)
        edges1 = l_e1.now()
        t = V.do(lambda e: v.memset(x_sb[:, T - 1, :], 0.0))
        xv = x_d[0:48 * 128, :].rearrange("(t p) d -> p t d", p=128)
        for k in range(4):
            S.dma(lambda e, k=k: e.dma_start(x_sb[:, 12 * k:12 * k + 12, :], xv[:, 12 * k:12 * k + 12, :]), l_x)
        x_in = S.dma(lambda e: e.dma_start(x_sb[0:N - 48 * 128, 48, :], x_d[48 * 128:N, :]), l_x, t)

        def load(dst, srcap, *waits):
            return S.dma(lambda e: e.dma_start(dst, srcap, allow_slow_non_contiguous=True), l_w, *waits)

        load(Wt, W_d.rearrange("(k p) n -> p k n", p=128))
        load(Wx1[:, :, 0:D], W_d.rearrange("(k p) n -> p k n", p=128))
        load(Wx2[:, :, 0:16], Wg_d.rearrange("(k p) n -> p k n", p=128))
        load(attB[:, 0, :], as_d.rearrange("h c -> (h c)").partition_broadcast(128))
        load(attB[:, 1, :], ad_d.rearrange("h c -> (h c)").partition_broadcast(128))
        load(gatB[:, 0, :], gas_d.rearrange("h c -> (h c)").partition_broadcast(128))
        load(gatB[:, 1, :], gad_d.rearrange("h c -> (h c)").partition_broadcast(128))
        load(biasB, bias_d.partition_broadcast(128))
        load(lnsB, lns_d.partition_broadcast(128))
        load(lnbB, lnb_d.partition_broadcast(128))
        load(gB[:, 0, :], bg_d.partition_broadcast(128))
        load(gB[:, 1, :], gam_d.partition_broadcast(128))
        load(gB[:, 2, :], bet_d.partition_broadcast(128))
        load(b2B[:, :, :].rearrange("p e d -> p (e d)"), b2_d.rearrange("e d -> (e d)").partition_broadcast(128))
        weights_in = load(b1c[:, :, :], b1_d.rearrange("e (f p) -> p e f", p=128))

        imp = dict(allow_small_or_imprecise_dtypes=True)
        t = G.do(lambda e: g.iota(iota[:, :], [[1, 128]], base=0, channel_multiplier=0, **imp))
        G.do(lambda e: g.iota(pidx[:, :], [[128, 9]], base=0, channel_multiplier=1, **imp))
        G.do(lambda e: g.iota(iota16[:, :], [[1, g2.NCH]], base=0, channel_multiplier=0, **imp))
        t = G.do(lambda e: g.memset(ones[:, :], 1.0))
        G.do(lambda e: g.memset(epsc[:, :], 1e-5))
        G.do(lambda e: g.affine_select(out=ident[:, :], in_=ones[:, :], compare_op=ALU.is_equal, fill=0.0, base=0,
                                       pattern=[[1, 128]], channel_multiplier=-1), t)
        G.do(lambda e: g.affine_select(out=tri[:, :], in_=ones[:, :], compare_op=ALU.is_gt, fill=0.0, base=0,
                                       pattern=[[1, 128]], channel_multiplier=-1))
        G.do(lambda e: g.affine_select(out=ident16[:, :], in_=ones[:, :], compare_op=ALU.is_equal, fill=0.0, base=0,
                                       pattern=[[1, 128]], channel_multiplier=-1))
        consts = G.do(lambda e: g.affine_select(out=rmask[:, :], in_=ones[:, 0:1], compare_op=ALU.is_gt, fill=0.0,
                                                base=N - 48 * 128, pattern=[[0, 1]], channel_multiplier=-1))

        def tiles_of(Vq, dstI, bI, bF, sc, ready, step=None):
            t = Vq.do(lambda e: v.tensor_scalar(bI, dstI, 7, None, ALU.logical_shift_right), ready)
            t = Vq.do(lambda e: v.tensor_copy(bF, bI), t)
            for b in range(T):
                t = Vq.do(lambda e, b=b: v.tensor_scalar(sc, bF, float(b), 0.0, ALU.is_equal, ALU.add,
                                                         accum_out=cnt[:, b:b + 1]), t)
                yield t

        def totals(Vq, Pq, ready, banks):
            t = Pq.do(lambda e: pe.matmul(pbank[banks[0]][:, 0:T], ones[:, :], cnt[:, :], start=True, stop=True), ready, consts,
                      free[banks[0]])
            t = Pq.do(lambda e: pe.matmul(pbank[banks[1]][:, 0:T], tri[:, :], cnt[:, :], start=True, stop=True), free[banks[1]])
            t = Vq.do(lambda e: v.tensor_copy(tot[:, :], pbank[banks[0]][:, 0:T]), t)
            return Vq.do(lambda e: v.tensor_copy(pre[:, :], pbank[banks[1]][:, 0:T]), t)

        def prefix(Vq, cum, n, ready):
            return Vq.do(lambda e: v.tensor_tensor_scan(cum, ones[:, 0:T], n, 0.0, ALU.mult, ALU.add), ready, consts)

        def shift7(Vq, out, in_, add, ready):
            t = Vq.do(lambda e: v.tensor_scalar(nchi[:, :], in_, float(add), None, ALU.add), ready)
            t = Vq.do(lambda e: v.tensor_scalar(nchi[:, :], nchi[:, :], 7, None, ALU.arith_shift_right), t)
            return Vq.do(lambda e: v.tensor_copy(out, nchi[:, :]), t)

        def padded_chunks(Vq, cum, ready):
            t = shift7(Vq, nch[:, :], tot[:, :], 127, ready)
            return prefix(Vq, cum, nch[:, :], t)

        def offsets(Vq, cum, ready):
            t = Vq.do(lambda e: v.tensor_tensor(off[:, :], cum, nch[:, :], ALU.subtract), ready)
            t = Vq.do(lambda e: v.tensor_scalar(off[:, :], off[:, :], 128.0, -1.0, ALU.mult, ALU.add), t)
            return Vq.do(lambda e: v.tensor_tensor(off[:, :], off[:, :], pre[:, :], ALU.add), t)

        def tile_map(q, Vq, Sq, tag, ready):
            lt, ll = line(f"l_tm{tag}"), line(f"l_tml{tag}")
            t = ready
            for k in range(q.K):
                t = Vq.do(lambda e, k=k: v.tensor_scalar(junk[:, :], q.cum[:, :], pidx[:, k:k + 1], 0.0, ALU.is_le, ALU.add,
                                                         accum_out=tcn[:, k:k + 1]), t)
            K = q.K
            Vq.do(lambda e: v.tensor_scalar(tci[:, 0, 0:K], tcn[:, 0:K], float(q.AR), None, ALU.mult), t)
            t = Vq.do(lambda e: v.tensor_scalar(tci[:, 1, 0:K], tcn[:, 0:K], float(2 * q.H), None, ALU.mult))
            for w in range(2):
                for k in range(K):
                    Sq.dma(lambda e, w=w, k=k: e.dma_start(
                        q.tm_d[(w * K + k) * 128:(w * K + k + 1) * 128].rearrange("(p o) -> p o", o=1), tci[:, w, k:k + 1]), lt, t)
            Sq.dma(lambda e: e.dma_start(q.tm[:, :], q.tm_d.rearrange("(a n) -> a n", a=1)), ll, lt.now())
            return t, ll.now(), [lt, ll]

        def ranks(Vq, q, bF, mask, sc, pos, ready, Aq=None, far=None):
            J = q.J
            onesJ = ones[:, 0:1].broadcast_to([128, J])
            t = Vq.do(lambda e: v.memset(pos, float(2 ** 26)), ready)
            made, used = {}, {}

            def masks(b):
                if Aq is None:
                    made[b] = Vq.do(lambda e: v.tensor_scalar(mask, bF, float(b), None, ALU.is_equal), t)
                    return
                ta = Aq.do(lambda e: a.activation(far, bF, ACT.Abs, scale=-1.0, bias=iota[:, b:b + 1]), ready, made.get(b - 1))
                made[b] = Aq.do(lambda e: a.activation(mask[b % 2], far, ACT.Relu, scale=-1.0, bias=ones[:, 0:1]), ta,
                                used.get(b - 2))

            if Aq is not None:
                masks(0)
            for b in range(T):
                if Aq is None:
                    masks(b)
                elif b + 1 < T:
                    masks(b + 1)
                mk = mask if Aq is None else mask[b % 2]
                if Aq is None:
                    t = made[b]
                yield t
                t = Vq.do(lambda e, b=b, mk=mk: v.tensor_tensor_scan(sc, onesJ, mk, off[:, b:b + 1], ALU.mult, ALU.add), t, made[b])
                yield t
                used[b] = t = Vq.do(lambda e, mk=mk: v.copy_predicated(pos, mk, sc), t)
                if Aq is None:
                    yield t

        def run(gen):
            t = None
            for t in gen:
                pass
            return t

        bI1, bF1, sc1 = tmp(3, i32, J1), tmp(4, f32, J1), tmp(5, f32, J1)
        l_row = line("l_row")
        S.dma(lambda e: e.dma_start(rowS_d.rearrange("a b -> (a b)").rearrange("(p j) -> p j", p=128), src1), l_row, edges1)
        S.dma(lambda e: e.dma_start(rowD_d.rearrange("a b -> (a b)").rearrange("(p j) -> p j", p=128), dst1), l_row)
        rows_out = l_row.now()
        t = run(tiles_of(V, dst1, bI1, bF1, sc1, edges1))
        t = V.do(lambda e: v.scalar_tensor_tensor(sc1, dst1, 1.0, nxt1, ALU.mult, ALU.is_gt, accum_out=small[:, 0:1]), t)
        t = totals(V, P, t, (0, 1))
        t = V.do(lambda e: v.tensor_tensor_scan(off[:, :], ones[:, 0:T], tot[:, :], 0.0, ALU.mult, ALU.add), t)
        t = V.do(lambda e: v.tensor_tensor(dd[:, :], off[:, :], tot[:, :], ALU.subtract), t)
        t = shift7(V, dd[:, :], dd[:, :], 0, t)
        t = shift7(V, nch[:, :], off[:, :], -1, t)
        t = V.do(lambda e: v.tensor_tensor(nch[:, :], nch[:, :], dd[:, :], ALU.subtract), t)
        t = V.do(lambda e: v.tensor_scalar(nch[:, :], nch[:, :], 1.0, None, ALU.add), t)
        t = V.do(lambda e: v.tensor_scalar(off[:, :], tot[:, :], 0.0, None, ALU.is_gt), t)
        t = V.do(lambda e: v.tensor_tensor(nch[:, :], nch[:, :], off[:, :], ALU.mult), t)
        t = prefix(V, g1.cum[:, :], nch[:, :], t)
        t = V.do(lambda e: v.tensor_tensor(dd[:, :], dd[:, :], g1.cum[:, :], ALU.subtract), t)
        t = V.do(lambda e: v.tensor_tensor(dd[:, :], dd[:, :], nch[:, :], ALU.add), t)
        t = V.do(lambda e: v.tensor_tensor(off[:, 0:T - 1], dd[:, 1:T], dd[:, 0:T - 1], ALU.subtract), t)
        t = V.do(lambda e: v.memset(off[:, T - 1:T], 0.0), t)
        for k in range(g1.K):
            t = V.do(lambda e, k=k: v.scalar_tensor_tensor(junk[:, :], g1.cum[:, :], pidx[:, k:k + 1], off[:, :], ALU.is_le,
                                                           ALU.mult, accum_out=pair[:, k:k + 1]), t)
        t = V.do(lambda e: v.tensor_tensor(pair[:, 0:g1.K], pair[:, 0:g1.K], pidx[:, 0:g1.K], ALU.add), t)
        t = V.do(lambda e: v.tensor_scalar(pairu[:, 0:g1.K], pair[:, 0:g1.K], float(J1 - 1), 0.0, ALU.min, ALU.max), t)
        t, tm1_in, _ = tile_map(g1, V, S, "1", t)
        g1.tm_in = [tm1_in]
        R1S, R1D = tmp(6, i32, 896).rearrange("p (k n) -> p k n", n=128), tmp(7, i32, 896).rearrange("p (k n) -> p k n", n=128)
        l_blk = line("l_blk")
        for k in range(g1.K):
            for rb, rd in ((R1S, rowS_d), (R1D, rowD_d)):
                G.dma(lambda e, k=k, rb=rb, rd=rd: e.indirect_dma_start(
                    out=rb[:, k, :], out_offset=None, in_=rd,
                    in_offset=bass.IndirectOffsetOnAxis(ap=pairu[:, k:k + 1], axis=0)), l_blk, rows_out, t)
        blocks_in = l_blk.now()
        t = P.do(lambda e: pe.matmul(pbank[0][:, 64:65], ones[:, :], small[:, 0:1], start=True, stop=True), t)
        flag1 = V.do(lambda e: v.tensor_copy(flags[0:1, 0:1], pbank[0][0:1, 64:65]), t)
        free[0] = free[1] = flag1

        U = VU, _, _, GU, SU = queues("u")
        l_fu, l_su, l_ru = line("l_fu"), line("l_su"), line("l_ru")
        fillu = tmp(8, i32, 2 * 896).rearrange("p (n w) -> p n w", w=2)
        VU.do(lambda e: v.memset(fillu[:, :, 0], N))
        t = VU.do(lambda e: v.memset(fillu[:, :, 1], 8191))
        SU.dma(lambda e: e.dma_start(slots1.rearrange("(p c) w -> p (c w)", p=128), fillu[:, 0:832, :].rearrange("p n w -> p (n w)")), l_fu, t)
        t = padded_chunks(VU, g1.cum[:, :], None)
        t = offsets(VU, g1.cum[:, :], t)
        masku, posu = tmp(10, i32, J1), tmp(11, f32, J1)
        t = run(ranks(VU, g1, bF1, masku, sc1, posu, t))
        t = VU.do(lambda e: v.tensor_copy(bI1, posu), t)
        payu = tmp(8, i32, 2 * 832).rearrange("p (n w) -> p n w", w=2)
        t = VU.do(lambda e: v.tensor_copy(payu[:, 0:J1, 0], src1), l_fu.now(), t)
        t = VU.do(lambda e: v.tensor_copy(payu[:, 0:J1, 1], dst1), t)
        for j in range(J1):
            GU.dma(lambda e, j=j: e.indirect_dma_start(
                out=slots1, out_offset=bass.IndirectOffsetOnAxis(ap=bI1.bitcast(u32)[:, j:j + 1], axis=0),
                in_=payu[:, j, :], in_offset=None, bounds_check=BLK * g1.NCH - 1, oob_is_err=False), l_su, t, l_fu.now())
        t, _, endu = tile_map(g1, VU, SU, "u", t)
        rawu = tmp(8, i32, 7 * 256).rearrange("p (k n w) -> p k n w", k=7, w=2)
        full = g1.NCH // 128
        SU.dma(lambda e: e.dma_start(rawu[:, 0:full, :, :].rearrange("p k n w -> p k (n w)"),
                                     slots1[0:full * 128 * 128, :].rearrange("(k p n) w -> p k (n w)", p=128, n=128)), l_ru,
               l_su.now())
        SU.dma(lambda e: e.dma_start(rawu[0:g1.NCH - full * 128, full, :, :].rearrange("p n w -> p (n w)"),
                                     slots1[full * 128 * 128:g1.NCH * 128, :].rearrange("(p n) w -> p (n w)", n=128)), l_ru,
               l_su.now())
        t = VU.do(lambda e: v.tensor_copy(R1S, rawu[:, :, :, 0]), l_ru.now(), t)
        VU.do(lambda e: v.tensor_copy(R1D, rawu[:, :, :, 1]), t)

        t = None
        for w in range(2):
            t = V.do(lambda e, w=w: v.tensor_tensor(fold, Wt, attB[:, w, :].unsqueeze(1).broadcast_to([128, 2, D]),
                                                    ALU.mult), weights_in, t)
            t = V.do(lambda e, w=w: v.tensor_reduce(Wx1[:, :, D + 8 * w:D + 8 * w + 8],
                                                    fold.rearrange("p k (h c) -> p k h c", c=32), X, ALU.add), t)
        for w in range(2):
            t = V.do(lambda e, w=w: v.tensor_tensor(fold[:, :, 0:16], Wx2[:, :, 0:16],
                                                    gatB[:, w, :].unsqueeze(1).broadcast_to([128, 2, 16]), ALU.mult), t)
            t = V.do(lambda e, w=w: v.tensor_reduce(Wx2[:, :, 16 + 4 * w:20 + 4 * w],
                                                    fold[:, :, 0:16].rearrange("p k (h c) -> p k h c", c=4), X, ALU.add), t)
        folded = t

        mv1 = sb("mv1", [128, T, 2])
        rs1 = sb("rs1", [128, T])
        mv2 = sb("mv2", [128, T, 2])
        rs2 = sb("rs2", [128, T])
        nb1 = sb("nb1", [128, T])
        nb2 = sb("nb2", [128, T])
        asall = sb("asall", [128, T, 8])
        l_h = [line(f"l_h{i}") for i in range(2)]

        def stat(get, mv, i, ready):
            t = V.do(lambda e: v.bn_stats(bst[:, i, :], get), ready)
            return V.do(lambda e: v.bn_aggr(mv[:, i, :], bst[:, i, :]), t)

        def rstd(mv, rs, nb, lo, hi, ready):
            r = A.do(lambda e: a.activation(rs[:, lo:hi], mv[:, lo:hi, 1], ACT.Sqrt, bias=epsc[:, :]), ready, consts)
            t = V.do(lambda e: v.reciprocal(rs[:, lo:hi], rs[:, lo:hi]), r)
            if nb is None:
                return t
            return V.do(lambda e: v.scalar_tensor_tensor(nb[:, lo:hi], mv[:, lo:hi, 0], -1.0, rs[:, lo:hi], ALU.mult, ALU.mult), t)

        fst = {"tT": {}, "tw": {}, "cp": {}, "hc": {}, "mm": {}}

        def features(q, Wx, keep_T, i, last, rs, nb, ready, n0):
            M = q.F + 2 * q.H
            tT, tw, cp, hcp, mm = (fst[k] for k in ("tT", "tw", "cp", "hc", "mm"))

            def columns(i):
                return xT[:, i, 0:256].rearrange("p (k n) -> p k n", k=2) if keep_T else xTb[:, i % 2, :, :]

            if i < last:
                s, n = i % 2, n0 + i
                va = A.do(lambda e: a.activation(xn[:, s, :], x_sb[:, i, :], ACT.Identity, scale=rs[:, i:i + 1],
                                                 bias=nb[:, i:i + 1]), ready, tT.get(n - 2))
                for k in range(2):
                    tT[n] = P.do(lambda e, k=k: pe.transpose(pbank[s][:, k * 128:k * 128 + 128],
                                                             xn[:, s, k * 128:k * 128 + 128], ident[:, :]),
                                 va, cp.get(n - 2, free[s]))
            if 0 <= i - 1 < last:
                i1, s1, n1 = i - 1, (i - 1) % 2, n0 + i - 1
                Cq, copy = (A, a.copy) if keep_T else (V, v.tensor_copy)
                cp[n1] = Cq.do(lambda e: copy(columns(i1), pbank[s1][:, 0:256].rearrange("p (k n) -> p k n", k=2)),
                               tT[n1], mm.get(n1 - 2))
                for k in range(2):
                    mm[n1] = P.do(lambda e, k=k: pe.matmul(pbank[2 + s1][:, 0:M], columns(i1)[:, k, :], Wx[:, k, :],
                                                           start=k == 0, stop=k == 1),
                                  cp[n1], folded, tw.get(n1 - 2, free[2 + s1]))
            if 0 <= i - 2 < last:
                i2, s2, n2 = i - 2, (i - 2) % 2, n0 + i - 2
                hc = A.do(lambda e: a.copy(hrow[:, s2, 0:q.R], pbank[2 + s2][:, 0:q.R]), mm[n2], hcp.get(n2 - 2))
                if keep_T:
                    V.do(lambda e: v.tensor_copy(acc2[:, i2, 0:q.R], pbank[2 + s2][:, 0:q.R]), hc)
                else:
                    V.do(lambda e: v.tensor_copy(asall[:, i2, 0:q.H], pbank[2 + s2][:, q.F:q.R]), hc)
                tw[n2] = V.do(lambda e: v.tensor_copy(q.tab[:, 2 * q.H * i2:2 * q.H * i2 + q.H],
                                                      pbank[2 + s2][:, q.R:q.R + q.H]))
                hcp[n2] = S.dma(lambda e: e.dma_start(q.table[128 * i2:128 * i2 + 128, :], hrow[:, s2, 0:q.R]), l_h[s2], hc)
                q.table_in = [hcp[n2], hcp.get(n2 - 1)]
                return tw[n2]

        def peaks(q, last, index):
            H = q.H
            b = 4
            t = V.do(lambda e: v.tensor_reduce(small[:, 0:H], asall[:, :, 0:H].rearrange("p t h -> p h t"), X, ALU.max), last)
            t = V.do(lambda e: v.tensor_reduce(small[:, H:2 * H], asall[:, :, 0:H].rearrange("p t h -> p h t"), X, ALU.min), t)
            t = V.do(lambda e: v.tensor_scalar(small[:, H:2 * H], small[:, H:2 * H], -1.0, None, ALU.mult), t)
            t = P.do(lambda e: pe.transpose(pbank[b][0:2 * H, 0:128], small[:, 0:2 * H], ident[:, :]), t, free[b])
            t = V.do(lambda e: v.tensor_reduce(small[0:2 * H, 16:17], pbank[b][0:2 * H, 0:128], X, ALU.max), t)
            t = V.do(lambda e: v.tensor_scalar(small[0:2 * H, 0:2 * H], ident[0:2 * H, 0:2 * H], small[0:2 * H, 16:17], None,
                                               ALU.mult), t)
            t = P.do(lambda e: pe.matmul(pbank[b][:, 128:128 + 2 * H], ones[0:2 * H, :], small[0:2 * H, 0:2 * H], start=True,
                                         stop=True), t)
            peak = t = V.do(lambda e: v.tensor_copy(q.peak[:, :], pbank[b][:, 128:128 + 2 * H]), t)
            t = V.do(lambda e: v.tensor_tensor(q.flagrow[:, 0:H], q.peak[0:1, 0:H], q.peak[0:1, H:2 * H], ALU.add), t)
            t = V.do(lambda e: v.tensor_reduce(small[0:1, 20:21], q.flagrow[:, 0:H], X, ALU.max), t)
            t = V.do(lambda e: v.tensor_scalar(flags[0:1, index:index + 1], small[0:1, 20:21], SPREAD, None, ALU.is_gt), t)
            free[b] = t
            return peak, t

        def shift_table(q, ready, own):
            H = q.H
            tabv = q.tab[:, 0:T * 2 * H].rearrange("p (t w) -> p t w", t=T)
            peak, flag = peaks(q, ready, q.n)
            t = V.do(lambda e: v.tensor_copy(tabv[:, :, H:2 * H], q.peak[:, 0:H].unsqueeze(1).broadcast_to([128, T, H])), flag)
            t = V.do(lambda e: v.memset(q.tab[:, T * 2 * H:(T + 1) * 2 * H], 0.0), t)
            q.pending = (flag, own)
            return t

        def finish_shift(q):
            H = q.H
            tabv = q.tab[:, 0:T * 2 * H].rearrange("p (t w) -> p t w", t=T)
            t = V.do(lambda e: v.tensor_tensor(tabv[:, :, H:2 * H], tabv[:, :, H:2 * H], tabv[:, :, 0:H], ALU.add),
                     (V.sem, V.count))
            t = V.do(lambda e: v.scalar_tensor_tensor(tabv[:, :, H:2 * H], tabv[:, :, H:2 * H], 0.2,
                                                      tabv[:, :, H:2 * H], ALU.mult, ALU.max), t)
            if q.n == 2:
                t = thirds([tab3[:, :, w, :] for w in range(3)], q.tab[:, :].rearrange("p (t h) -> p t h", h=2 * H),
                           rest3, t)
            return t

        def thirds(parts, whole, rest, ready, V=V):
            t = V.do(lambda e: v.tensor_copy(parts[0], whole), ready)
            t = V.do(lambda e: v.tensor_tensor(rest, whole, parts[0], ALU.subtract), t)
            t = V.do(lambda e: v.tensor_copy(parts[1], rest), t)
            t = V.do(lambda e: v.tensor_tensor(rest, rest, parts[1], ALU.subtract), t)
            return V.do(lambda e: v.tensor_copy(parts[2], rest), t)

        xs = {n: sem("x_" + n) for n in ("v", "p", "z", "m", "go_p", "end_p")}

        def true_peaks(q, ready):
            H, R = q.H, q.R
            flag, own = q.pending
            xd, xr = Sb[:, 0, 1, 0:1], Sb[:, 0, 1, 8:8 + H]
            rows = (big if q.n == 1 else early)[:, 0:q.NCH * H].rearrange("p (c h) -> p c h", h=H)
            Z = Sb[:, 1, 0, :]
            ZH = Sb[:, 2:4, :, :].rearrange("p s c n -> p (s c n)")[:, 0:H * 128].rearrange("p (h n) -> p h n", n=128)
            red = small[:, 0:H]
            tabv = q.tab[:, 0:T * 2 * H].rearrange("p (t w) -> p t w", t=T)
            W = queues(f"w{q.n}")
            l_ta, l_tg = line(f"l_ta{q.n}"), line(f"l_tg{q.n}")
            W[4].dma(lambda e: e.dma_start(q.asrc.rearrange("(t p) h -> p t h", p=128), asall[:, :, 0:H]), l_ta)
            for c in range(q.NCH):
                W[3].dma(lambda e, c=c: e.indirect_dma_start(
                    out=rows[:, c, :], out_offset=None, in_=q.asrc,
                    in_offset=bass.IndirectOffsetOnAxis(ap=q.idx[:, c:c + 1], axis=0)), l_tg, l_ta.now())
            when(q.n, ready, W, [l_ta, l_tg])

            def enter(eng):
                reg = eng.alloc_register(f"xf{q.n}")
                eng.load([reg], flags[0:1, q.n:q.n + 1])
                return reg

            def on_v(eng):
                reg = enter(eng)
                rt = eng.alloc_register(f"xt{q.n}")
                with eng.If_ne(reg, 0):
                    if own:
                        v.tensor_copy(tabv[:, :, H:2 * H], asall[:, :, 0:H]).then_inc(xs["m"], 1)
                    else:
                        v.memset(q.tab[:, :].rearrange("p (t w) -> p t w", w=2 * H)[:, :, H:2 * H], -1e30).then_inc(xs["m"], 1)
                    eng.wait_ge(xs["m"], 1)
                    eng.sem_clear(xs["m"])
                    with eng.Fori(0, q.NCH) as i:
                        iv = eng.snap(i, min_val=0, max_val=q.NCH - 1)
                        v.tensor_copy(xr, rows[:, bass.ds(iv, 1), :].rearrange("p c h -> p (c h)")).then_inc(xs["v"], 1)
                        v.tensor_copy(xd, q.dl[:, bass.ds(iv, 1)]).then_inc(xs["v"], 1)
                        eng.wait_ge(xs["v"], 2)
                        v.tensor_scalar(Z, iota[:, :], xd, None, ALU.is_equal).then_inc(xs["v"], 1)
                        eng.wait_ge(xs["v"], 3)
                        v.tensor_scalar(Z, Z, -1.0, 1e30, ALU.add, ALU.mult).then_inc(xs["v"], 1)
                        eng.wait_ge(xs["v"], 4)
                        v.tensor_tensor(ZH, Z.unsqueeze(1).broadcast_to([128, H, 128]),
                                        xr.unsqueeze(2).broadcast_to([128, H, 128]), ALU.add).then_inc(xs["v"], 1)
                        eng.wait_ge(xs["p"], H)
                        for w in range(H // 4):
                            v.tensor_reduce(red[:, 4 * w:4 * w + 4], pbank[w][:, :].rearrange("p (h n) -> p h n", n=128), X,
                                            ALU.max).then_inc(xs["z"], 1)
                        eng.wait_ge(xs["z"], H // 4)
                        eng.load([rt], q.tm[0:1, bass.ds(iv + q.K * 128, 1)])
                        o = q.tab[:, bass.ds(eng.snap(rt, min_val=0, max_val=T * 2 * H) + H, H)]
                        v.tensor_tensor(o, o, red, ALU.max).then_inc(xs["m"], 1)
                        eng.wait_ge(xs["m"], 1)
                        eng.wait_ge(xs["end_p"], 1)
                        for n in ("v", "p", "z", "m", "end_p"):
                            eng.sem_clear(xs[n])
                        eng.sem_inc(xs["go_p"], 1)
                eng.free_register(rt)
                eng.free_register(reg)

            def on_p(eng):
                reg = enter(eng)
                with eng.If_ne(reg, 0):
                    with eng.Fori(0, q.NCH) as i:
                        eng.wait_ge(xs["v"], 5)
                        for h in range(H):
                            pe.transpose(pbank[h // 4][:, 128 * (h % 4):128 * (h % 4) + 128], ZH[:, h, :],
                                         ident[:, :]).then_inc(xs["p"], 1)
                        eng.wait_ge(xs["p"], H)
                        eng.sem_inc(xs["end_p"], 1)
                        eng.wait_ge(xs["go_p"], 1)
                        eng.sem_clear(xs["go_p"])
                eng.free_register(reg)

            V.items.append(on_v)
            P.items.append(on_p)

        for q in (g1, g2):
            q.peak = sb(f"peak{q.n}", [128, 2 * q.H])

        Gb = sb("Gb", [128, NSL, CH, g1.R])
        Sall = sb("Sall", [128, 3072])
        Sb = Sall[:, 0:2048].rearrange("p (s c n) -> p s c n", s=NSL, c=CH)
        S16 = Sall[:, 2048:3072].bitcast(b16).rearrange("p (s c n) -> p s c n", s=NSL, c=CH)
        STb = sb("STb", [128, 2, CH, 128])
        bst = Sall[:, 392:392 + 6 * T].rearrange("p (t w) -> p t w", w=6)
        tab3 = g2.dl[:, 0:600].bitcast(b16).rearrange("p (t w h) -> p t w h", w=3, h=8)
        rest3 = Sall[:, 0:400].rearrange("p (t h) -> p t h", h=8)
        ad2 = big[:, T * g1.R:T * g1.R + 128].rearrange("p (c h) -> p c h", h=8)
        sums2 = [asall[:, :, :].rearrange("p t h -> p (t h)")[:, 160 * n:160 * n + 160].rearrange("p (c r) -> p c r", r=20)
                 for n in range(2)]
        zb = sb("zb", [128, NSL, CH, 8])[:, :, :, :]
        zc = sb("zc", [128, NSL, CH, 8])[:, :, :, :]

        t = x_in
        for i in range(T):
            t = stat(x_sb[:, i, :], mv1, i, x_in)
        st1 = rstd(mv1, rs1, nb1, 0, T, t)
        for i in range(T + 2):
            last = features(g1, Wx1, False, i, T, rs1, nb1, st1, 0)
        when(0, flag1, U, [l_fu, l_su, l_ru] + endu)
        tab1 = shift_table(g1, last, False)

        K1 = g1.K
        t = V.do(lambda e: v.tensor_scalar(t128[:, 0:K1], tcn[:, 0:K1], -128.0, None, ALU.mult), blocks_in)
        dF, sF, ok = tmp(3, f32, 896), tmp(4, f32, 896), tmp(5, f32, 896)
        dF3, sF3 = (z.rearrange("p (k n) -> p k n", n=128) for z in (dF, sF))
        for k in range(K1):
            t = V.do(lambda e, k=k: v.tensor_scalar(dF3[:, k, :], R1D[:, k, :], t128[:, k:k + 1], None, ALU.add), t)
        t = V.do(lambda e: v.tensor_scalar(ok, dF, 0.0, None, ALU.is_ge), t)
        t = V.do(lambda e: v.scalar_tensor_tensor(ok, dF, 128.0, ok, ALU.is_lt, ALU.mult), t)
        t = V.do(lambda e: v.tensor_scalar(sF, tmp(6, i32, 896), float(N - 1), None, ALU.min), t)
        t = V.do(lambda e: v.scalar_tensor_tensor(sF, sF, float(-N), ok, ALU.add, ALU.mult), t)
        t = V.do(lambda e: v.tensor_scalar(sF, sF, float(N), None, ALU.add), t)
        for b, w, z in ((5, 0, sF3), (6, 1, dF3)):
            for k0 in (0, 4):
                kn = min(4, K1 - k0)
                for k in range(kn):
                    pt = P.do(lambda e, b=b, z=z, k=k, k0=k0: pe.transpose(pbank[b][:, k * 128:k * 128 + 128], z[:, k0 + k, :],
                                                                           ident[:, :]), t, free[b])
                n = min(g1.NCH - k0 * 128, kn * 128)
                dst = (g1.idx if w == 0 else g1.dl)[:, k0 * 128:k0 * 128 + n]
                free[b] = V.do(lambda e, b=b, dst=dst, n=n: v.tensor_copy(dst, pbank[b][:, 0:n]), pt)
        ready1 = V.do(lambda e: v.tensor_copy(g1.dl16[:, :], g1.dl[:, :]), free[6])
        true_peaks(g1, g1.pending[0])
        tab1 = finish_shift(g1)
        zero1 = V.do(lambda e: v.memset(big[:, :], 0.0), ready1)
        g1.tab_in = tab1

        def edge_pass(q, accf, Gt, lg, start, idx_in, dl_in, banks, fill, lo, hi, Q, tag):
            V, A, P, G, S = Q
            H, C, R, F = q.H, q.C, q.R, q.F
            bT, bD, bA = banks
            zt = [zb[:, s, :, 0:H] for s in range(NSL)]
            ar = [zc[:, s, :, 0:H] for s in range(NSL)]
            gat, sd, trp, stc, adg, z3, wex, msg, agg, add, sm, s32 = ({} for _ in range(12))
            regs = {}

            def alloc(e, nm):
                regs[nm] = [e.alloc_register(f"{nm}{tag}_{k}") for k in range(8 if nm == "dvr" else 4)]

            def rel(e, nm):
                for r in regs[nm]:
                    e.free_register(r)

            P.raw(lambda e: alloc(e, "per"))
            V.raw(lambda e: alloc(e, "dvr"))

            def g_gather(i):
                s = i % NSL
                for k in range(CH):
                    c = i * CH + k
                    gat[i] = G.dma(lambda e, k=k, s=s, c=c: e.indirect_dma_start(
                        out=Gt[s][:, k, :], out_offset=None, in_=q.table,
                        in_offset=bass.IndirectOffsetOnAxis(ap=q.idx[:, c:c + 1], axis=0)),
                        lg[s], agg.get(i - NSL), idx_in, *q.table_in)

            def v_onehot(i):
                s = i % NSL
                sd[i] = V.do(lambda e: v.tensor_tensor(S16[:, s, :, :], iota16[:, 0:128].unsqueeze(1).broadcast_to([128, CH, 128]),
                                                       q.dl16[:, i * CH:i * CH + CH].unsqueeze(2).broadcast_to([128, CH, 128]),
                                                       ALU.is_equal), trp.get(i - NSL), s32.get(i - NSL), dl_in)

            def p_transpose(i):
                s = i % NSL
                for k in range(CH):
                    trp[i] = P.do(lambda e, k=k: pe.transpose(pbank[bT][:, :].bitcast(b16)[:, k * 128:k * 128 + 128],
                                                              S16[:, s, k, :], ident16[:, :]),
                                  sd[i], stc.get(i - 1, free[bT]))

            def a_widen(i):
                s = i % NSL
                s32[i] = A.do(lambda e: a.copy(Sb[:, s, :, :].rearrange("p c n -> p (c n)"),
                                               S16[:, s, :, :].rearrange("p c n -> p (c n)")), sd[i], agg.get(i - NSL))

            def a_stcopy(i):
                s = i % 2
                stc[i] = A.do(lambda e: a.copy(STb[:, s, :, :].rearrange("p c n -> p (c n)"),
                                               pbank[bT][:, :].bitcast(b16)[:, 0:CH * 128]), trp[i],
                              adg.get(i - 2))

            def p_adst(i):
                s = i % 2
                P.raw(lambda e: e.load(regs["per"], q.tm[0:1, q.K * 128 + i * CH:q.K * 128 + i * CH + CH]), *q.tm_in)
                for k in range(CH):
                    adg[i] = P.do(lambda e, k=k: pe.matmul(
                        pbank[bD][:, k * 16:k * 16 + 2 * H], STb[:, s, k, :],
                        q.tab[:, bass.ds(e.snap(regs["per"][k], min_val=0, max_val=T * 2 * H), 2 * H)], start=True, stop=True),
                        stc[i], q.tab_in, z3.get(i - 1, free[bD]))

            def v_score(i):
                s = i % NSL
                pv = pbank[bD][:, 0:64].rearrange("p (c w) -> p c w", w=16)
                t = V.do(lambda e: v.tensor_tensor(ar[s], Gt[s][:, :, F:R], pv[:, :, 0:H], ALU.add), adg[i], gat[i])
                t = V.do(lambda e: v.scalar_tensor_tensor(ar[s], ar[s], 0.2, ar[s], ALU.mult, ALU.max), t)
                z3[i] = V.do(lambda e: v.tensor_tensor(zt[s], ar[s], pv[:, :, H:2 * H], ALU.subtract), t, wex.get(i - NSL))

            def a_exp(i):
                s = i % NSL
                wex[i] = A.do(lambda e: a.activation(Gt[s][:, :, F:R], zt[s], ACT.Exp), z3[i])

            def v_message(c):
                i, k = divmod(c, CH)
                s = i % NSL
                hv = Gt[s][:, k, 0:F].rearrange("p (h c) -> p h c", c=C)
                msg[c] = V.do(lambda e: v.tensor_tensor(hv, hv, Gt[s][:, k, F:R].unsqueeze(2).broadcast_to([128, H, C]),
                                                        ALU.mult), wex[i])

            def p_sum(c):
                i, k = divmod(c, CH)
                s, b = i % NSL, bA[c % len(bA)]
                agg[i] = sm[c] = P.do(lambda e: pe.matmul(pbank[b][:, 0:R], Sb[:, s, k, :], Gt[s][:, k, :], start=True, stop=True),
                                      msg[c], s32[i], add.get(c - len(bA), free[b]))

            def v_add(c):
                i, k = divmod(c, CH)
                b, rg = bA[c % len(bA)], 4 * (i % 2)
                if k == 0:
                    V.raw(lambda e: e.load(regs["dvr"][rg:rg + 4], q.tm[0:1, c:c + CH]), *q.tm_in)

                def f(e):
                    o = accf[:, bass.ds(e.snap(regs["dvr"][rg + k], min_val=0, max_val=T * R), R)]
                    return v.tensor_tensor(o, o, pbank[b][:, 0:R], ALU.add)
                add[c] = V.do(f, sm[c], add.get(c - 1, start))

            LAG = len(bA) - 1
            for i in range(lo, hi + 3):
                if i < hi:
                    g_gather(i)
                    v_onehot(i)
                    p_transpose(i)
                    a_stcopy(i)
                if lo + 2 <= i < hi + 2:
                    v_score(i - 2)
                    a_exp(i - 2)
                if lo + 1 <= i < hi + 1:
                    a_widen(i - 1)
                    p_adst(i - 1)
                for k in range(CH):
                    c = (i - 3) * CH + k
                    if lo * CH <= c < hi * CH:
                        v_message(c)
                        p_sum(c)
                    if c - LAG >= lo * CH:
                        v_add(c - LAG)
                    if fill:
                        fill(i)
            for c in range(hi * CH - LAG, hi * CH):
                v_add(c)
            P.raw(lambda e: rel(e, "per"))
            V.raw(lambda e: rel(e, "dvr"))
            q.adds, end = add, add[hi * CH - 1]
            free[bT], free[bD] = stc[hi - 1], z3[hi - 1]
            for b in bA:
                free[b] = end
            return end

        J2, NC2, W2 = g2.J, g2.NCH, g2.W
        XP = 448
        JP = J2 - XP
        x_free = last
        src2, dst2 = g2.idx[:, 0:1024].bitcast(i32), xtmp(1, i32)
        bI2, bF2, sc2, pos2, mask2 = xtmp(2, i32), xtmp(3, f32), xtmp(4, f32), xtmp(5, f32), xtmp(6, i32)
        Bv = [x_f[:, 7168 + 544 * n:7168 + 544 * n + 544].bitcast(f16)[:, 0:NC2] for n in range(4)]
        Av = [x_f[:, 9344 + 192 * n:9344 + 192 * n + 192].bitcast(f16).rearrange("p (w n) -> p w n", w=3) for n in range(4)]
        NB = 4
        nhiF, nloF = xtmp(1, f32), xtmp(2, f32)
        hiF, loF, laneF, winF = bF2, sc2, pos2, xtmp(0, f32)
        addr2 = g2.dl[:, 0:1024].bitcast(i32)
        l_f2, l_s2, l_r2 = line("l_f2"), line("l_s2"), line("l_r2")
        S.dma(lambda e: e.dma_start(src2, ei_d[0, :].rearrange("(p j) -> p j", j=J2)), l_e2, x_free)
        S.dma(lambda e: e.dma_start(dst2, ei_d[1, :].rearrange("(p j) -> p j", j=J2)), l_e2)
        edges2 = l_e2.now()
        st = {}

        def sort2():
            zf = xtmp(10, i32, NC2)
            t = V.do(lambda e: v.memset(zf, 0), x_free)
            S.dma(lambda e: e.dma_start(slots2.rearrange("(p c) o -> p (c o)", p=128), zf), l_f2, t)
            gen = tiles_of(V, dst2, bI2, bF2, sc2, edges2)
            for n, t in enumerate(gen):
                if n % 2:
                    yield
            t = totals(V, P, t, (5, 6))
            t = padded_chunks(V, g2.cum[:, :], t)
            t = offsets(V, g2.cum[:, :], t)
            free[5] = free[6] = t
            yield
            t, tmi, _ = tile_map(g2, V, S, "2", t)
            g2.tm_in = [tmi]
            yield
            for n, gi in enumerate(SECT[:-1]):
                st["tails"] = t = V.do(lambda e, n=n, gi=gi: v.tensor_scalar(flags[0:1, 4 + n:5 + n], g2.cum[0:1, T - 1:T],
                                                                             float(W2 * gi), None, ALU.is_gt), t)
            for t in ranks(V, g2, bF2, (mask2, xtmp(7, i32)), sc2, pos2, t, A, xtmp(8, f32)):
                yield
            t = V.do(lambda e: v.tensor_scalar(dst2, dst2, 127, None, ALU.bitwise_and), t)
            t = V.do(lambda e: v.tensor_scalar(dst2, dst2, -1.0, 128.0, ALU.mult, ALU.add), t)
            t = V.do(lambda e: v.tensor_scalar(src2, src2, float(N - 1), None, ALU.min), t)
            yield
            t = V.do(lambda e: v.tensor_scalar(src2, src2, -1.0, float(N), ALU.mult, ALU.add), t)
            t = V.do(lambda e: v.scalar_tensor_tensor(src2, dst2, 8192.0, src2, ALU.mult, ALU.add), t)
            yield
            t = V.do(lambda e: v.tensor_copy(bI2, pos2), t)
            t = V.do(lambda e: v.tensor_scalar(mask2, bI2, 127, None, ALU.bitwise_and), t)
            t = V.do(lambda e: v.tensor_scalar(bI2, bI2, 7, None, ALU.logical_shift_right), t)
            yield
            st["addr"] = t = V.do(lambda e: v.scalar_tensor_tensor(addr2, mask2, float(NC2), bI2, ALU.mult, ALU.add), t)
            t = V.do(lambda e: v.tensor_copy(laneF, mask2), t)
            t = V.do(lambda e: v.tensor_copy(winF, bI2), t)
            yield
            t = V.do(lambda e: v.tensor_scalar(mask2, src2, 10, None, ALU.logical_shift_right), t)
            t = V.do(lambda e: v.tensor_copy(hiF, mask2), t)
            t = V.do(lambda e: v.tensor_scalar(mask2, src2, 1023, None, ALU.bitwise_and), t)
            st["loF"] = t = V.do(lambda e: v.tensor_scalar(loF, mask2, 1.0 / 1024, None, ALU.mult), t)
            yield
            V.do(lambda e: v.tensor_scalar(nhiF, hiF, -1.0, None, ALU.mult), t)
            t = V.do(lambda e: v.tensor_scalar(nloF, loF, -1.0, None, ALU.mult))
            used = {}
            segs = [(5, 0, 512), (6, 512, 1024), (7, 1024, NC2)]
            made = {}

            def onehots(j, t):
                n = j % NB
                ta = V.do(lambda e: v.tensor_scalar(Bv[n], iota16[:, :], winF[:, j:j + 1], None, ALU.is_equal), t,
                          used.get(j - NB))
                tl = A.do(lambda e: a.activation(Av[n][:, 2, :], iota16[:, 0:128], ACT.Abs, scale=-1.0, bias=laneF[:, j:j + 1]),
                          t, used.get(j - NB))
                A.do(lambda e: a.activation(Av[n][:, 0, :], Av[n][:, 2, :], ACT.Relu, scale=nhiF[:, j:j + 1],
                                            bias=hiF[:, j:j + 1]), tl)
                tl = A.do(lambda e: a.activation(Av[n][:, 1, :], Av[n][:, 2, :], ACT.Relu, scale=nloF[:, j:j + 1],
                                                 bias=loF[:, j:j + 1]))
                made[j] = (ta, tl)

            def place(j):
                n = j % NB
                for w in range(2):
                    for b, c0, c1 in segs:
                        used[j] = P.do(lambda e, w=w, b=b, c0=c0, c1=c1: pe.matmul(
                            pbank[b][:, 0:c1 - c0], Av[n][:, w, :], Bv[n][:, c0:c1], start=(j == 0 and w == 0),
                            stop=(j == JP - 1 and w == 1)), *made[j], free[b] if j == 0 else None)

            for j in range(JP + 2):
                if j >= 2:
                    place(j - 2)
                if j < JP:
                    onehots(j, t)
                yield
            for b in (5, 6, 7):
                free[b] = used[JP - 1]
            st["sorted"] = used[JP - 1]

        SECT = list(range(51, g2.NCH // W2, 2)) + [g2.NCH // W2]

        scat = {"j": JP}

        def scatter2(n):
            for _ in range(n):
                j = scat["j"]
                if j >= J2:
                    return
                scat["j"] += 1
                G.dma(lambda e, j=j: e.indirect_dma_start(
                    out=slots2, out_offset=bass.IndirectOffsetOnAxis(ap=addr2.bitcast(u32)[:, j:j + 1], axis=0),
                    in_=src2[:, j:j + 1], in_offset=None, bounds_check=BLK * NC2 - 1, oob_is_err=False),
                    l_s2, st["addr"], l_f2.now())

        filler = sort2()
        state = {"done": False}
        NG1 = g1.NCH // CH

        def fill1(i):
            if not state["done"]:
                try:
                    next(filler)
                except StopIteration:
                    state["done"] = True
            if "addr" in st:
                st["n"] = st.get("n", 0) + 1
                if st["n"] > 24 and st["n"] % (16 if state["done"] else 2) == 0:
                    scatter2(1)

        lg1 = [line(f"l_g{i}") for i in range(NSL)]
        Gt1 = [Gb[:, s, :, :] for s in range(NSL)]
        done1 = edge_pass(g1, big, Gt1, lg1, zero1, ready1, ready1, (0, 1, (2, 3, 4)), fill1, 0, NG1, main, "a")
        for _ in filler:
            pass
        scatter2(J2)
        xin2 = {}
        t = V.do(lambda e: v.memset(x_sb[:, T - 1, :], 0.0), st["sorted"])
        l_x2s = [line(f"l_x2_{k}") for k in range(5)]
        for k in range(4):
            xin2[k] = S.dma(lambda e, k=k: e.dma_start(x_sb[:, 12 * k:12 * k + 12, :], xv[:, 12 * k:12 * k + 12, :]), l_x2s[k],
                            st["sorted"], st["loF"], l_f2.now(), g1.adds[CH * (NG1 - 24 + 5 * k)])
        xin2[4] = S.dma(lambda e: e.dma_start(x_sb[0:N - 48 * 128, 48, :], x_d[48 * 128:N, :]), l_x2s[4], t)

        rec = Sall[:, 0:392].rearrange("p (t h) -> p t h", h=8)
        t = V.do(lambda e: v.tensor_scalar(rec[:, :, :], acc1[:, 0:T, 256:264], 1e-16, None, ALU.add), done1)
        rect = V.do(lambda e: v.reciprocal(rec[:, :, :], rec[:, :, :]), t)
        ue, us, sta = {}, {}, {}

        def fin_a(i):
            s = i % 2
            u = acc1[:, i, 0:256]
            uh = u.rearrange("p (h c) -> p h c", c=32)
            xa = A.do(lambda e: a.activation(xn[:, s, :], x_sb[:, i, :], ACT.Identity, scale=rs1[:, i:i + 1], bias=nb1[:, i:i + 1]),
                      xin2[i // 12], ue.get(i - 2))
            t1 = V.do(lambda e: v.tensor_tensor(uh, uh, rec[:, i, :].unsqueeze(2).broadcast_to([128, 8, 32]), ALU.mult), rect)
            yield
            t1 = V.do(lambda e: v.tensor_tensor(u, u, biasB, ALU.add), t1)
            yield
            t1 = V.do(lambda e: v.tensor_tensor(u, u, xn[:, s, :], ALU.add), t1, xa)
            ue[i] = A.do(lambda e: a.activation(fold[:, s, :], u, ACT.Exp), t1, us.get(i - 2))

        def fin_b(i):
            s = i % 2
            u = acc1[:, i, 0:256]
            t0 = V.do(lambda e: v.tensor_scalar(fold[:, s, :], fold[:, s, :], 1.0, -1.0, ALU.min, ALU.add), ue[i])
            yield
            us[i] = V.do(lambda e: v.scalar_tensor_tensor(u, u, 0.0, fold[:, s, :], ALU.max, ALU.add), t0)

        def fin_c(i):
            t = V.do(lambda e: v.bn_stats(bst[:, i, :], acc1[:, i, 0:256]), us[i])
            yield
            yield
            sta[i] = V.do(lambda e: v.bn_aggr(mv2[:, i, :], bst[:, i, :]), t)

        def turns(*gens):
            left = list(gens)
            while left:
                left = [gn for gn in left if next(gn, left) is not left]

        for i in range(T + 2):
            turns(*(fn(n) for fn, n in ((fin_a, i), (fin_b, i - 1), (fin_c, i - 2)) if 0 <= n < T))
        lnr = rstd(mv2, rs2, nb2, 0, T, sta[T - 1])
        mv3 = mv1
        rs3, nb3 = rs1, nb1
        BT = 7
        r3 = {}
        lnd = {}

        def ln_a(i):
            u = acc1[:, i, 0:256]
            t = A.do(lambda e: a.activation(u, u, ACT.Identity, scale=rs2[:, i:i + 1], bias=nb2[:, i:i + 1]), lnr)
            lnd[i] = t

        def ln_b(i):
            u = acc1[:, i, 0:256]
            t = V.do(lambda e: v.tensor_tensor(u, u, lnsB, ALU.mult), lnd[i])
            yield
            t = V.do(lambda e: v.tensor_tensor(u, u, lnbB, ALU.add), t)
            yield
            lnd[i] = V.do(lambda e: v.tensor_tensor(x_sb[:, i, :], x_sb[:, i, :], u, ALU.add), t)

        def ln_c(i):
            t = lnd[i]
            if i == T - 1:
                t = V.do(lambda e: v.tensor_scalar(x_sb[:, T - 1, :], x_sb[:, T - 1, :], rmask[:, :], None, ALU.mult), t)
            t = V.do(lambda e: v.bn_stats(bst[:, i, :], x_sb[:, i, :]), t)
            yield
            t = V.do(lambda e: v.bn_aggr(mv3[:, i, :], bst[:, i, :]), t)
            yield
            if i % BT == BT - 1 or i == T - 1:
                lo = i // BT * BT
                r3[i // BT] = rstd(mv3, rs3, nb3, lo, i + 1, t)

        for i in range(T + BT + 3):
            if i < T:
                ln_a(i)
            turns(*(fn(n) for fn, n in ((ln_b, i), (ln_c, i - 1)) if 0 <= n < T))
            if i > BT:
                last2 = features(g2, Wx2, True, i - BT - 1, T, rs3, nb3, r3.get((i - BT - 1) // BT), 100)
        featdone = [last2, (P.sem, P.count), (A.sem, A.count), l_h[0].now(), l_h[1].now()]
        xTdone = (A.sem, A.count)

        rawS = idx1f[:, 0:NC2].bitcast(i32)
        rawP = Gb[:, :, :, :].rearrange("p s c r -> p (s c r)")[:, 0:NC2].bitcast(i32)
        raw2_in = S.dma(lambda e: e.dma_start(rawS, slots2.rearrange("(p c) o -> p (c o)", p=128)), l_r2, l_s2.now(), l_f2.now(),
                        done1)
        for b, c0, c1 in ((5, 0, 512), (6, 512, 1024), (7, 1024, NC2)):
            t = V.do(lambda e, b=b, c0=c0, c1=c1: v.tensor_scalar(rawP[:, c0:c1], pbank[b][:, 0:c1 - c0], 1024.0, None, ALU.mult),
                     st["sorted"], done1)
            free[b] = t
        t = V.do(lambda e: v.tensor_tensor(rawP, rawP, rawS, ALU.add), t, raw2_in)
        t2 = V.do(lambda e: v.tensor_scalar(rawS, rawP, 8191, None, ALU.bitwise_and), t)
        t = V.do(lambda e: v.tensor_scalar(rawP, rawP, 13, None, ALU.logical_shift_right), t)
        t2 = V.do(lambda e: v.tensor_scalar(g2.idx[:, :], rawS, -1.0, float(N), ALU.mult, ALU.add), t2)
        t = V.do(lambda e: v.tensor_scalar(g2.dl[:, :], rawP, -1.0, 128.0, ALU.mult, ALU.add), t)
        ready2 = V.do(lambda e: v.tensor_copy(g2.dl16[:, :], g2.dl[:, :]), t)

        t = V.do(lambda e: v.tensor_copy(asall[:, :, 0:4], acc2[:, 0:T, 16:20]), last2)
        shift_table(g2, t, True)
        true_peaks(g2, g2.pending[0])
        g2.tab_in = finish_shift(g2)
        g2.table_in = [*g2.table_in, g2.tab_in]
        tab2 = g2.tab[:, 0:T * 8].rearrange("p (t w) -> p t w", t=T)
        zo = small4[:, :].rearrange("p (t h) -> p t h", h=4)
        t = V.do(lambda e: v.tensor_tensor(zo, acc2[:, 0:T, 16:20], tab2[:, :, 0:4], ALU.add), g2.tab_in)
        t = V.do(lambda e: v.scalar_tensor_tensor(zo, zo, 0.2, zo, ALU.mult, ALU.max), t)
        t = V.do(lambda e: v.tensor_tensor(zo, zo, tab2[:, :, 4:8], ALU.subtract), t)
        t = A.do(lambda e: a.activation(acc2[:, 0:T, 16:20], zo, ACT.Exp), t)
        for h in range(4):
            tt = V.do(lambda e, h=h: v.tensor_tensor(acc2[:, 0:T, 4 * h:4 * h + 4], acc2[:, 0:T, 4 * h:4 * h + 4],
                                                     acc2[:, 0:T, 16 + h:17 + h].broadcast_to([128, T, 4]), ALU.mult), t)
        start2 = V.do(lambda e: v.memset(acc2[:, T, :], 0.0), tt)

        W1s = early[:, 0:2048].rearrange("p (w k f) -> p w k f", w=2, k=2)
        W2s = early[:, 2048:4096].rearrange("p (w f d) -> p w f d", w=2, f=4)
        Gt2 = [z.rearrange("p (c r) -> p c r", r=20) for z in (g1.dl[:, 0:320], g1.dl[:, 320:640], g1.tab[:, 0:320])]
        Mb = [z.bitcast(b16).rearrange("p (c w r) -> p c w r", w=3, c=W2) for z in (g1.tab[:, 320:800], early[:, 4096:4576])]
        S2 = Sall[:, :].bitcast(b16).rearrange("p (s c n) -> p s c n", s=3, c=W2)
        ST2 = STb[:, :, :, :].rearrange("p s c n -> p (s c n)")[:, 0:512].bitcast(b16).rearrange("p (s c n) -> p s c n", s=2, c=CH)
        tab3f = g2.dl[:, 0:600].bitcast(b16)
        z2 = [z.rearrange("p s c h -> p (s c h)")[:, 0:64].rearrange("p (c h) -> p c h", h=4) for z in (zb, zc)]
        hh = Gb[:, :, :, :].rearrange("p s c r -> p (s c r)")[:, 0:4096].rearrange("p (s f n) -> p s f n", s=2, f=4)
        Yb = idx1f[:, 0:1536].rearrange("p (s t d) -> p s t d", s=3, t=2)
        l_w1 = [line(f"l_w1{i}") for i in range(2)]
        l_y = [line(f"l_y{i}") for i in range(3)]
        groups = [(4 * i, 4) for i in range(12)] + [(48, 1)]
        blk = [(ei, gi) for ei in range(4) for gi in range(13)]
        use1, use2, wl, gel, mm2 = {}, {}, {}, {}, {}
        ffn = {"n1": 0, "n2": 0, "ny": 0}

        def wload(ei):
            s = ei % 2
            S.dma(lambda e: e.dma_start(W1s[:, s, :, :], W1_d[ei].rearrange("(k p) f -> p k f", p=128)), l_w1[s],
                  use1.get(ei - 2), g2.tab_in, *featdone)
            wl[ei] = S.dma(lambda e: e.dma_start(W2s[:, s, :, :], W2_d[ei].rearrange("(f p) d -> p f d", p=128)), l_w1[s],
                           use2.get(ei - 2))

        def up(bi):
            ei, gi = blk[bi]
            t0, nt = groups[gi]
            s, w = bi % 2, ei % 2
            for f in range(4):
                b = 5 + ffn["n1"] % 2
                ffn["n1"] += 1
                for k in range(2):
                    p = P.do(lambda e, k=k, f=f, b=b: pe.matmul(
                        pbank[b][:, 0:nt * 128], W1s[:, w, k, f * 128:f * 128 + 128],
                        xT[:, t0:t0 + nt, k * 128:k * 128 + 128], start=k == 0, stop=k == 1), wl[ei], free[b], xTdone)
                    if nt == 4 and k == 0:
                        yield
                gel[(bi, f)] = free[b] = A.do(lambda e, f=f, b=b: a.activation(hh[:, s, f, 0:nt * 128], pbank[b][:, 0:nt * 128],
                                                                               ACT.Gelu, bias=b1c[:, ei, f:f + 1]),
                                              p, mm2.get(bi - 2), start2)
                use1[ei] = p
                yield

        yslot = {}

        def down(bi):
            ei, gi = blk[bi]
            t0, nt = groups[gi]
            s, w = bi % 2, ei % 2
            for j in range(nt):
                ti = t0 + j
                b = (4, 7)[ffn["n2"] % 2]
                ffn["n2"] += 1
                for f in range(4):
                    p = P.do(lambda e, f=f, b=b, j=j: pe.matmul(pbank[b][:, 0:D], hh[:, s, f, j * 128:j * 128 + 128],
                                                                W2s[:, w, f, :], start=f == 0, stop=f == 3),
                             gel[(bi, f)], free[b])
                mm2[bi] = use2[ei] = p
                sl = ffn["ny"] % 3
                free[b] = V.do(lambda e, b=b, sl=sl, j=j: v.tensor_tensor(Yb[:, sl, j % 2, :], pbank[b][:, 0:D], b2B[:, ei, :],
                                                                          ALU.add), p, yslot.get(sl))
                if j % 2 or nt == 1:
                    n = 1 if nt == 1 else 2
                    yslot[sl] = S.dma(lambda e, sl=sl, ti=ti, n=n: e.dma_start(
                        Y_d[(ti - n + 1) * 128:(ti + 1) * 128, ei, :].rearrange("(t p) d -> p t d", p=128), Yb[:, sl, 0:n, :]),
                        l_y[sl], free[b])
                    ffn["ny"] += 1
                yield

        def experts():
            wload(0)
            wload(1)
            yield from up(0)
            for bi in range(len(blk)):
                gens = [up(bi + 1)] if bi + 1 < len(blk) else []
                gens.append(down(bi))
                while gens:
                    for gn in list(gens):
                        try:
                            next(gn)
                            yield
                        except StopIteration:
                            gens.remove(gn)
                if blk[bi][1] == 12 and blk[bi][0] + 2 < 4:
                    wload(blk[bi][0] + 2)

        fgen = experts()
        fst2 = {"n": 0, "done": False}

        def fill2(i):
            fst2["n"] += 1
            if not fst2["done"] and fst2["n"] * PACE // 1000 > (fst2["n"] - 1) * PACE // 1000:
                try:
                    next(fgen)
                except StopIteration:
                    fst2["done"] = True

        def edge_pass2(start, fill, lo, hi, lg, Q, tag):
            q, H, C, R, F = g2, 4, 4, 20, 16
            bT, bD, bA = 0, 1, (2, 3)
            V, A, P, G, S = Q
            gat, sd, trp, stc, adg, z3, wex, msg, whole, add, sm = ({} for _ in range(11))
            regs = {}

            def alloc(e, nm):
                regs[nm] = [e.alloc_register(f"{nm}{tag}_{k}") for k in range(8 if nm == "dvr" else 4)]

            def rel(e, nm):
                for r in regs[nm]:
                    e.free_register(r)

            P.raw(lambda e: alloc(e, "per"))
            V.raw(lambda e: alloc(e, "dvr"))

            def g_gather(i):
                s = i % 3
                for k in range(W2):
                    c = i * W2 + k
                    gat[i] = G.dma(lambda e, k=k, c=c: e.indirect_dma_start(
                        out=Gt2[s][:, k, :], out_offset=None, in_=q.table,
                        in_offset=bass.IndirectOffsetOnAxis(ap=q.idx[:, c:c + 1], axis=0)),
                        lg[s], msg.get(i - 3), ready2, *q.table_in)

            def v_onehot(n):
                i, u = divmod(n, 4)
                sd[n] = V.do(lambda e: v.tensor_tensor(S2[:, i % 3, u * CH:u * CH + CH, :],
                                                       iota16[:, 0:128].unsqueeze(1).broadcast_to([128, CH, 128]),
                                                       q.dl16[:, n * CH:n * CH + CH].unsqueeze(2).broadcast_to([128, CH, 128]),
                                                       ALU.is_equal), sm.get((n - 12) * CH + CH - 1), ready2)

            def p_transpose(i, u):
                n, s = 4 * i + u, i % 3
                for k in range(CH):
                    trp[n] = P.do(lambda e, k=k: pe.transpose(pbank[bT][:, :].bitcast(b16)[:, k * 128:k * 128 + 128],
                                                              S2[:, s, u * CH + k, :], ident16[:, :]),
                                  sd[n], stc.get(n - 1, free[bT]))
                stc[n] = A.do(lambda e: a.copy(ST2[:, n % 2, :, :].rearrange("p c n -> p (c n)"),
                                               pbank[bT][:, :].bitcast(b16)[:, 0:CH * 128]), trp[n], adg.get(n - 2))

            def p_adst(n):
                i, u = divmod(n, 4)
                P.raw(lambda e: e.load(regs["per"], q.tm[0:1, n * CH:n * CH + CH]), *q.tm_in)
                for k in range(CH):
                    o = (u * CH + k) * 6 * H
                    adg[n] = P.do(lambda e, k=k, o=o: pe.matmul(
                        pbank[bD][:, o:o + 6 * H], ST2[:, n % 2, k, :],
                        tab3f[:, bass.ds(e.snap(regs["per"][k], min_val=0, max_val=T * 6 * H), 6 * H)], start=True, stop=True),
                        stc[n], q.tab_in, z3.get(i - 1, free[bD]))

            def v_score(i):
                s = i % 3
                z, pv = z2[i % 2], ad2
                z3[i] = t = V.do(lambda e: v.tensor_reduce(
                    ad2, pbank[bD][:, 0:W2 * 6 * H].rearrange("p (c w h) -> p c h w", w=3, h=2 * H), X, ALU.add), adg[4 * i + 3])
                t = V.do(lambda e: v.tensor_tensor(z, Gt2[s][:, :, F:R], pv[:, :, 0:H], ALU.add), t, gat[i], wex.get(i - 2))
                t = V.do(lambda e: v.scalar_tensor_tensor(z, z, 0.2, z, ALU.mult, ALU.max), t)
                t = V.do(lambda e: v.tensor_tensor(z, z, pv[:, :, H:2 * H], ALU.subtract), t)
                wex[i] = A.do(lambda e: a.activation(Gt2[s][:, :, F:R], z, ACT.Exp), t)

            def v_messages(i):
                s = i % 3
                hv = Gt2[s][:, :, 0:F].rearrange("p c (h k) -> p c h k", k=C)
                t = V.do(lambda e: v.tensor_tensor(hv, hv, Gt2[s][:, :, F:R].unsqueeze(3).broadcast_to([128, W2, H, C]),
                                                   ALU.mult), wex[i])
                msg[i] = thirds([Mb[i % 2][:, :, w, :] for w in range(3)], Gt2[s], Gt2[s], t, V)

            def p_sum(c):
                i, k = divmod(c, W2)
                b = bA[c // 8 % 2]
                sm[c] = P.do(lambda e: pe.matmul(pbank[b][:, c % 8 * 60:c % 8 * 60 + 60], S2[:, i % 3, k, :], Mb[i % 2][:, k, :, :],
                                                 start=True, stop=True), msg[i], whole.get(c // 8 - 2, free[b]))

            def v_whole(n):
                whole[n] = V.do(lambda e: v.tensor_reduce(
                    sums2[n % 2], pbank[bA[n % 2]][:, 0:480].rearrange("p (c w r) -> p c r w", w=3, r=R), X, ALU.add),
                    sm[8 * n + 7])

            def v_add(c):
                rg = 4 * (c // CH % 2)
                if c % CH == 0:
                    V.raw(lambda e: e.load(regs["dvr"][rg:rg + 4], q.tm[0:1, c:c + CH]), *q.tm_in)

                def f(e):
                    o = acc2f[:, bass.ds(e.snap(regs["dvr"][rg + c % CH], min_val=0, max_val=T * q.AR), R)]
                    return v.tensor_tensor(o, o, sums2[c // 8 % 2][:, c % 8, :], ALU.add)
                add[c] = V.do(f, whole[c // 8], add.get(c - 1, start))

            for i in range(lo, hi + 2):
                if i < hi:
                    g_gather(i)
                    if i == lo:
                        v_onehot(4 * i)
                if lo <= i - 2:
                    v_messages(i - 2)
                for u in range(4):
                    if i < hi:
                        if 4 * i + u + 1 < 4 * hi:
                            v_onehot(4 * i + u + 1)
                        p_transpose(i, u)
                    if u == 0 and lo <= i - 1 < hi:
                        p_adst(4 * i - 1)
                        v_score(i - 1)
                    if u and i < hi:
                        p_adst(4 * i + u - 1)
                    for k in range(CH):
                        c = (i - 2) * W2 + u * CH + k
                        if c >= lo * W2:
                            p_sum(c)
                            if c - 8 >= lo * W2:
                                if c % 8 == 0:
                                    v_whole(c // 8 - 1)
                                v_add(c - 8)
                        if fill:
                            fill(i)
            v_whole(hi * 2 - 1)
            for c in range(hi * W2 - 8, hi * W2):
                v_add(c)
            P.raw(lambda e: rel(e, "per"))
            V.raw(lambda e: rel(e, "dvr"))
            free[bT], free[bD] = stc[4 * hi - 1], z3[hi - 1]
            for b in bA:
                free[b] = add[hi * W2 - 1]
            return add[hi * W2 - 1]

        for _ in range(PRE2):
            next(fgen)
        lg2 = [line(f"l_gg{i}") for i in range(3)]
        done2 = edge_pass2(start2, fill2, 0, SECT[0], lg2, main, "b")
        Z = queues("z")
        lgz = [line(f"l_gz{i}") for i in range(3)]
        for n in range(len(SECT) - 1):
            kept = list(free)
            edge_pass2(done2, None, SECT[n], SECT[n + 1], lgz, Z, f"z{n}")
            free[:] = kept
            when(4 + n, st["tails"], Z, lgz)
        done2 = (V.sem, V.count)

        late2 = Sall
        hk = late2[:, 1472:2256].rearrange("p (t c) -> p t c", t=T)
        sq = late2[:, 0:784].rearrange("p (t c) -> p t c", t=T)
        sc4 = late2[:, 784:980].rearrange("p (t c) -> p t c", t=T)
        r1 = late2[:, 980:1176].rearrange("p (t c) -> p t c", t=T)
        gate = late2[:, 1176:1372].rearrange("p (t c) -> p t c", t=T)
        m1, ct = late2[:, 1372:1421], late2[:, 1421:1470]

        def more(t):
            for _ in range(2):
                next(fgen, None)
            return t

        t = more(V.do(lambda e: v.tensor_scalar(r1, acc2[:, 0:T, 16:20], 1e-16, None, ALU.add), done2))
        t = more(V.do(lambda e: v.reciprocal(r1, r1), t))
        for h in range(4):
            tt = more(V.do(lambda e, h=h: v.tensor_tensor(hk[:, :, 4 * h:4 * h + 4], acc2[:, 0:T, 4 * h:4 * h + 4],
                                                     r1[:, :, h:h + 1].broadcast_to([128, T, 4]), ALU.mult), t))

        def bc16(ap):
            return ap.unsqueeze(1).broadcast_to([128, T, 16])

        def col(ap, n):
            return ap.unsqueeze(2).broadcast_to([128, T, n])

        t = more(V.do(lambda e: v.tensor_tensor(hk, hk, bc16(gB[:, 0, :]), ALU.add), tt))
        t = more(V.do(lambda e: v.tensor_reduce(m1, hk, X, ALU.add), t))
        t = more(V.do(lambda e: v.tensor_scalar(m1, m1, 1.0 / 16, None, ALU.mult), t))
        t = more(V.do(lambda e: v.tensor_tensor(hk, hk, col(m1, 16), ALU.subtract), t))
        t = more(V.do(lambda e: v.tensor_tensor(sq, hk, hk, ALU.mult), t))
        t = more(V.do(lambda e: v.tensor_reduce(ct, sq, X, ALU.add), t))
        t = more(A.do(lambda e: a.activation(ct, ct, ACT.Sqrt, scale=1.0 / 16, bias=epsc[:, :]), t))
        t = more(V.do(lambda e: v.reciprocal(ct, ct), t))
        t = more(V.do(lambda e: v.tensor_tensor(hk, hk, col(ct, 16), ALU.mult), t))
        t = more(V.do(lambda e: v.tensor_tensor(hk, hk, bc16(gB[:, 1, :]), ALU.mult), t))
        t = more(V.do(lambda e: v.tensor_tensor(hk, hk, bc16(gB[:, 2, :]), ALU.add), t))
        t = more(V.do(lambda e: v.tensor_tensor(sc4, hk[:, :, 0:4], hk[:, :, 4:8], ALU.add), t))
        t = more(V.do(lambda e: v.tensor_tensor(sc4, sc4, hk[:, :, 8:12], ALU.add), t))
        t = more(V.do(lambda e: v.tensor_tensor(sc4, sc4, hk[:, :, 12:16], ALU.add), t))
        t = more(V.do(lambda e: v.tensor_scalar(sc4, sc4, 0.25, None, ALU.mult), t))
        t = more(V.do(lambda e: v.tensor_reduce(m1, sc4, X, ALU.max), t))
        rank = sq[:, :, 0:4]
        t = more(V.do(lambda e: v.memset(rank, 0.0), t))
        for i in range(4):
            for j in range(4):
                if i == j:
                    continue
                op = ALU.is_ge if j < i else ALU.is_gt
                t = more(V.do(lambda e, i=i, j=j, op=op: v.tensor_tensor(ct, sc4[:, :, j], sc4[:, :, i], op), t))
                t = more(V.do(lambda e, i=i: v.tensor_tensor(sq[:, :, i], sq[:, :, i], ct, ALU.add), t))
        t = more(V.do(lambda e: v.tensor_scalar(rank, rank, 2.0, None, ALU.is_lt), t))
        t = more(V.do(lambda e: v.tensor_tensor(r1, sc4, col(m1, 4), ALU.subtract), t))
        t = more(A.do(lambda e: a.activation(r1, r1, ACT.Exp), t))
        t = more(V.do(lambda e: v.tensor_tensor(r1, r1, rank, ALU.mult), t))
        t = more(V.do(lambda e: v.tensor_reduce(ct, r1, X, ALU.add), t))
        t = more(V.do(lambda e: v.reciprocal(ct, ct), t))
        gated = more(V.do(lambda e: v.tensor_tensor(gate, r1, col(ct, 4), ALU.mult), t))

        for _ in fgen:
            pass

        NY = 6
        Yr = big[:, 0:NY * 2048].rearrange("p (s t e d) -> p s t e d", s=NY, t=2, e=4)
        l_yr = [line(f"l_yr{i}") for i in range(NY)]
        l_o = line("l_o")
        ffn_end = (P.sem, P.count)
        ydone = [z.now() for z in l_y]
        con = {}

        def yload(n):
            s = n % NY
            k = 1 if n == 24 else 2
            con[("in", n)] = S.dma(lambda e: e.dma_start(Yr[:, s, 0:k, :, :].rearrange("p t e d -> p t (e d)"),
                                                         Y_d[256 * n:256 * n + 128 * k, :, :].rearrange("(t p) e d -> p t (e d)", p=128)),
                                   l_yr[s], con.get(("out", n - NY)), ffn_end, *ydone)

        for n in range(NY):
            yload(n)
        for n in range(25):
            s = n % NY
            for j in range(1 if n == 24 else 2):
                ti = 2 * n + j
                t = None
                for ei in range(4):
                    t = V.do(lambda e, ti=ti, ei=ei, s=s, j=j: v.scalar_tensor_tensor(
                        x_sb[:, ti, :], Yr[:, s, j, ei, :], gate[:, ti, ei:ei + 1], x_sb[:, ti, :], ALU.mult, ALU.add),
                        con[("in", n)], gated, t)
            con[("out", n)] = t
            if n < 24:
                S.dma(lambda e, n=n: e.dma_start(out_d[n * 256:n * 256 + 256, :].rearrange("(t p) d -> p t d", p=128),
                                                 x_sb[:, 2 * n:2 * n + 2, :]), l_o, t)
            else:
                S.dma(lambda e: e.dma_start(out_d[48 * 128:N, :], x_sb[0:N - 48 * 128, 48, :]), l_o, t)
            if n + NY < 25:
                yload(n + NY)
        S.wait(l_o.now())

        block = ctx.enter_context(nc.Block())

        @block.sync
        def _(e):
            S.emit(e)

        @block.scalar
        def _(e):
            A.emit(e)

        @block.vector
        def _(e):
            V.emit(e)

        @block.tensor
        def _(e):
            P.emit(e)

        @block.gpsimd
        def _(e):
            G.emit(e)


_INS = ['x', 'src', 'dst', 'L0_gnn_W', 'L0_gnn_att_src', 'L0_gnn_att_dst', 'L0_gnn_bias', 'L0_gnn_ln_scale',
        'L0_gnn_ln_bias', 'L0_ffn_W_gat', 'L0_ffn_att_src', 'L0_ffn_att_dst', 'L0_ffn_b_gat', 'L0_ffn_ln_gamma',
        'L0_ffn_ln_beta', 'L0_ffn_W1', 'L0_ffn_b1', 'L0_ffn_W2', 'L0_ffn_b2', 'L0_ffn_edge_index']


def kernel(**inputs):
    import numpy as _np
    import concourse.bacc as _bacc
    from concourse import mybir as _mybir
    from concourse.bass_utils import run_bass_kernel_spmd as _run

    nc = _bacc.Bacc("TRN2", target_bir_lowering=False, num_devices=1)
    arrays, args = {}, []
    for name in _INS:
        a = _np.ascontiguousarray(inputs[name])
        arrays[f"in_{name}_dram"] = a
        args.append(nc.dram_tensor(f"in_{name}_dram", a.shape, _mybir.dt.from_np(a.dtype), kind="ExternalInput").ap())
    args.append(nc.dram_tensor("out_0_dram", (N, D), _mybir.dt.float32, kind="ExternalOutput").ap())
    build(nc, *args)
    r = _run(nc, [arrays], core_ids=[0])
    return r.results[0]["out_0_dram"]
```
